# Optimizing a Trainium2 kernel written in Bass

```python
import numpy as np
import jax
import jax.numpy as jnp

def _softmax(x, axis=-1):
    return jax.nn.softmax(x, axis=axis)

def _gelu(x):
    return jax.nn.gelu(x, approximate=True)

def _silu(x):
    return jax.nn.silu(x)

def _sigmoid(x):
    return jax.nn.sigmoid(x)

def _layernorm(x, axis=-1, eps=1e-05):
    m = jnp.mean(x, axis=axis, keepdims=True)
    v = jnp.var(x, axis=axis, keepdims=True)
    return (x - m) / jnp.sqrt(v + eps)

def _scatter_add(tgt, idx, src, axis=0):
    return tgt.at[idx].add(src)

def _segment_sum(src, seg, n):
    return jax.ops.segment_sum(src, seg, n)
kernel_name = 'mk_macaron_d2_jaxref_r8_bfefe1'

def setup_inputs(seed: int=0):
    np.random.seed(seed)
    _w = jnp.asarray

    def _L0_attn_setup():
        import jax, jax.numpy as jnp
        import numpy as np
        HIDDEN = 512
        NUM_HEADS = 32
        HEAD_DIM = HIDDEN // NUM_HEADS
        B, S = (2, 128)

        def _alibi_slopes(n):
            start = 2.0 ** (-2.0 ** (-(np.log2(n) - 3)))
            return np.array([start ** (i + 1) for i in range(n)], dtype=np.float32)
        key = jax.random.key(seed)
        k1, k2, k3, k4 = jax.random.split(key, 4)
        hidden_states = jax.random.normal(k1, (B, S, HIDDEN), jnp.float32)
        Wq = jax.random.normal(k2, (HIDDEN, HIDDEN), jnp.float32) * 0.02
        Wkv = jax.random.normal(k3, (HIDDEN, 2 * HEAD_DIM), jnp.float32) * 0.02
        Wo = jax.random.normal(k4, (HIDDEN, HIDDEN), jnp.float32) * 0.02
        return {'hidden_states': hidden_states, 'Wq': Wq, 'Wkv': Wkv, 'Wo': Wo}
    _L0_attn_in = _L0_attn_setup()

    def _L0_ffn_setup():
        import jax, jax.numpy as jnp
        import numpy as np
        R = 16
        LORA_ALPHA = 16
        SCALING = LORA_ALPHA / R
        key = jax.random.key(seed)
        kx, kr, ka = jax.random.split(key, 3)
        B, S, D, DO, E = (4, 256, 512, 512, 8)
        x = jax.random.normal(kx, (B, S, D), dtype=jnp.float32)
        bound_r = 1.0 / np.sqrt(D)
        route_w = jax.random.uniform(kr, (E, D), jnp.float32, -bound_r, bound_r)
        bound_a = 1.0 / np.sqrt(D)
        A = jax.random.uniform(ka, (E, R, D), jnp.float32, -bound_a, bound_a)
        kb = jax.random.fold_in(key, 7)
        Bw = jax.random.normal(kb, (E, DO, R), dtype=jnp.float32) * 0.02
        return {'x': x, 'route_w': route_w, 'A': A, 'Bw': Bw}
    _L0_ffn_in = _L0_ffn_setup()

    def _L1_attn_setup():
        import math
        import jax, jax.numpy as jnp
        import numpy as np
        N_HEADS = 32
        ALIBI_BIAS_MAX = 8

        def _alibi_slopes(n_heads, alibi_bias_max=8):
            _n = 2 ** math.ceil(math.log2(n_heads))
            m = jnp.arange(1, _n + 1, dtype=jnp.float32) * (alibi_bias_max / _n)
            slopes = 1.0 / jnp.power(2.0, m)
            if _n != n_heads:
                slopes = jnp.concatenate([slopes[1::2], slopes[::2]])[:n_heads]
            return slopes
        key = jax.random.key(seed)
        k1, k2, k3 = jax.random.split(key, 3)
        B, S, D = (1, 256, 512)
        x = jax.random.normal(k1, (B, S, D), dtype=jnp.float32)
        w_qkv = jax.random.normal(k2, (3 * D, D), dtype=jnp.float32) * 0.02
        b_qkv = jnp.zeros((3 * D,), dtype=jnp.float32)
        w_out = jax.random.normal(k3, (D, D), dtype=jnp.float32) * 0.02
        b_out = jnp.zeros((D,), dtype=jnp.float32)
        return {'x': x, 'w_qkv': w_qkv, 'b_qkv': b_qkv, 'w_out': w_out, 'b_out': b_out}
    _L1_attn_in = _L1_attn_setup()

    def _L1_ffn_setup():
        import jax, jax.numpy as jnp
        import numpy as np
        SCALING = 16.0 / 8.0
        GAMMA = 1.0
        EPS = 1e-12
        key = jax.random.key(seed)
        ks = jax.random.split(key, 8)
        B, T, H, O = (4, 256, 512, 512)
        E_tot, E_act, r = (16, 4, 8)
        return {'x': jax.random.normal(ks[0], (B, T, H), jnp.float32), 'W_base': jax.random.normal(ks[1], (O, H), jnp.float32) * 0.02, 'b_base': jax.random.normal(ks[2], (O,), jnp.float32) * 0.02, 'lora_A': jax.random.normal(ks[3], (E_tot, r, H), jnp.float32) * 0.02, 'lora_B': jax.random.normal(ks[4], (E_tot, O, r), jnp.float32) * 0.02, 'router_W': jax.random.normal(ks[5], (E_tot, H), jnp.float32) * 0.02, 'router_b': jax.random.normal(ks[6], (E_tot,), jnp.float32) * 0.02, 'domain_prior': jax.random.uniform(ks[7], (E_tot,), jnp.float32), 'active': jnp.arange(E_act, dtype=jnp.int32)}
    _L1_ffn_in = _L1_ffn_setup()
    _d = {'L0_attn_hidden_states': _L0_attn_in['hidden_states'], 'L0_attn_Wq': _L0_attn_in['Wq'], 'L0_attn_Wkv': _L0_attn_in['Wkv'], 'L0_attn_Wo': _L0_attn_in['Wo'], 'L0_ffn_route_w': _L0_ffn_in['route_w'], 'L0_ffn_A': _L0_ffn_in['A'], 'L0_ffn_Bw': _L0_ffn_in['Bw'], 'L1_attn_w_qkv': _L1_attn_in['w_qkv'], 'L1_attn_b_qkv': _L1_attn_in['b_qkv'], 'L1_attn_w_out': _L1_attn_in['w_out'], 'L1_attn_b_out': _L1_attn_in['b_out'], 'L1_ffn_W_base': _L1_ffn_in['W_base'], 'L1_ffn_b_base': _L1_ffn_in['b_base'], 'L1_ffn_lora_A': _L1_ffn_in['lora_A'], 'L1_ffn_lora_B': _L1_ffn_in['lora_B'], 'L1_ffn_router_W': _L1_ffn_in['router_W'], 'L1_ffn_router_b': _L1_ffn_in['router_b'], 'L1_ffn_domain_prior': _L1_ffn_in['domain_prior'], 'L1_ffn_active': _L1_ffn_in['active']}
    _x0 = _d['L0_attn_hidden_states']
    _d['L0_attn_hidden_states'] = jax.random.normal(jax.random.fold_in(jax.random.key(seed), 1), (4, 512, 512), dtype=_x0.dtype)
    del _x0
    return _d

def reference(L0_attn_hidden_states, L0_attn_Wq, L0_attn_Wkv, L0_attn_Wo, L0_ffn_route_w, L0_ffn_A, L0_ffn_Bw, L1_attn_w_qkv, L1_attn_b_qkv, L1_attn_w_out, L1_attn_b_out, L1_ffn_W_base, L1_ffn_b_base, L1_ffn_lora_A, L1_ffn_lora_B, L1_ffn_router_W, L1_ffn_router_b, L1_ffn_domain_prior, L1_ffn_active):

    def _L0_attn_ref(hidden_states, Wq, Wkv, Wo):
        import jax, jax.numpy as jnp
        import numpy as np
        HIDDEN = 512
        NUM_HEADS = 32
        HEAD_DIM = HIDDEN // NUM_HEADS
        B, S = (2, 128)

        def _alibi_slopes(n):
            start = 2.0 ** (-2.0 ** (-(np.log2(n) - 3)))
            return np.array([start ** (i + 1) for i in range(n)], dtype=np.float32)
        b, s, h = hidden_states.shape
        scale = HEAD_DIM ** (-0.5)
        q = (hidden_states @ Wq).reshape(b, s, NUM_HEADS, HEAD_DIM)
        kv = hidden_states @ Wkv
        k, v = (kv[..., :HEAD_DIM], kv[..., HEAD_DIM:])
        scores = jnp.einsum('bqhd,bkd->bhqk', q, k) * scale
        pos = jnp.arange(s)
        slopes = jnp.asarray(_alibi_slopes(NUM_HEADS))
        bias = slopes[:, None, None] * (pos[None, None, :] - pos[None, :, None]).astype(jnp.float32)
        causal = pos[None, :] <= pos[:, None]
        scores = jnp.where(causal[None, None], scores + bias[None], -jnp.inf)
        attn = jax.nn.softmax(scores, axis=-1)
        out = jnp.einsum('bhqk,bkd->bqhd', attn, v).reshape(b, s, h)
        return out @ Wo

    def _L0_ffn_ref(x, route_w, A, Bw):
        import jax, jax.numpy as jnp
        import numpy as np
        R = 16
        LORA_ALPHA = 16
        SCALING = LORA_ALPHA / R
        logits = jnp.einsum('bsd,ed->bse', x, route_w)
        topk_v, topk_idx = jax.lax.top_k(logits, 1)
        E = logits.shape[-1]
        route_weight = jax.nn.one_hot(topk_idx[..., 0], E, dtype=logits.dtype) * topk_v
        h = jnp.einsum('bsd,erd->bser', x, A)
        wh = route_weight[..., None] * h
        out = jnp.einsum('bser,eor->bso', wh, Bw) * SCALING
        return out

    def _L1_attn_ref(x, w_qkv, b_qkv, w_out, b_out):
        import math
        import jax, jax.numpy as jnp
        import numpy as np
        N_HEADS = 32
        ALIBI_BIAS_MAX = 8

        def _alibi_slopes(n_heads, alibi_bias_max=8):
            _n = 2 ** math.ceil(math.log2(n_heads))
            m = jnp.arange(1, _n + 1, dtype=jnp.float32) * (alibi_bias_max / _n)
            slopes = 1.0 / jnp.power(2.0, m)
            if _n != n_heads:
                slopes = jnp.concatenate([slopes[1::2], slopes[::2]])[:n_heads]
            return slopes
        B, S, D = x.shape
        H = N_HEADS
        hd = D // H
        qkv = jnp.einsum('bsd,od->bso', x, w_qkv) + b_qkv
        q, k, v = jnp.split(qkv, 3, axis=-1)
        q = q.reshape(B, S, H, hd)
        k = k.reshape(B, S, H, hd)
        v = v.reshape(B, S, H, hd)
        scale = 1.0 / math.sqrt(hd)
        scores = jnp.einsum('bqhd,bkhd->bhqk', q, k) * scale
        slopes = _alibi_slopes(H, ALIBI_BIAS_MAX)
        positions = jnp.arange(1 - S, 1, dtype=jnp.float32)
        alibi = slopes[:, None] * positions[None, :]
        scores = scores + alibi[None, :, None, :]
        causal = jnp.arange(S)[:, None] >= jnp.arange(S)[None, :]
        scores = jnp.where(causal[None, None, :, :], scores, jnp.float32(-1000000000.0))
        attn = jax.nn.softmax(scores, axis=-1)
        out = jnp.einsum('bhqk,bkhd->bqhd', attn, v).reshape(B, S, D)
        return jnp.einsum('bsd,od->bso', out, w_out) + b_out

    def _L1_ffn_ref(x, W_base, b_base, lora_A, lora_B, router_W, router_b, domain_prior, active):
        import jax, jax.numpy as jnp
        import numpy as np
        SCALING = 16.0 / 8.0
        GAMMA = 1.0
        EPS = 1e-12
        y = jnp.einsum('bth,oh->bto', x, W_base) + b_base
        A = lora_A[active]
        Bm = lora_B[active]
        z = jnp.einsum('bth,erh->bter', x, A)
        contribs = jnp.einsum('bter,eor->bteo', z, Bm) * SCALING
        logits = jnp.einsum('bth,eh->bte', x, router_W) + router_b
        logits = logits[..., active]
        prior = domain_prior[active]
        alpha = jax.nn.softmax(jnp.log(prior + EPS) + logits / GAMMA, axis=-1)
        return y + jnp.einsum('bteo,bte->bto', contribs, alpha)
    x = L0_attn_hidden_states
    x = x + 0.5 * _L0_ffn_ref(_layernorm(x, axis=-1), L0_ffn_route_w, L0_ffn_A, L0_ffn_Bw)
    x = x + _L0_attn_ref(_layernorm(x, axis=-1), L0_attn_Wq, L0_attn_Wkv, L0_attn_Wo)
    x = x + 0.5 * _L0_ffn_ref(_layernorm(x, axis=-1), L0_ffn_route_w, L0_ffn_A, L0_ffn_Bw)
    x = x + 0.5 * _L1_ffn_ref(_layernorm(x, axis=-1), L1_ffn_W_base, L1_ffn_b_base, L1_ffn_lora_A, L1_ffn_lora_B, L1_ffn_router_W, L1_ffn_router_b, L1_ffn_domain_prior, L1_ffn_active)
    x = x + _L1_attn_ref(_layernorm(x, axis=-1), L1_attn_w_qkv, L1_attn_b_qkv, L1_attn_w_out, L1_attn_b_out)
    x = x + 0.5 * _L1_ffn_ref(_layernorm(x, axis=-1), L1_ffn_W_base, L1_ffn_b_base, L1_ffn_lora_A, L1_ffn_lora_B, L1_ffn_router_W, L1_ffn_router_b, L1_ffn_domain_prior, L1_ffn_active)
    return x

_drawn_inputs = setup_inputs


def setup_inputs(seed=0):
    import zlib

    import numpy as np

    out = dict(_drawn_inputs(seed))
    spreads = {'L1_attn_b_qkv': (0.0, 0.1), 'L1_attn_b_out': (0.0, 0.1)}
    factors = {'L0_attn_Wq': 5.64,
     'L1_ffn_b_base': 3.164,
     'L1_ffn_router_W': 6.69,
     'L1_ffn_router_b': 200.0,
     'L1_ffn_domain_prior': 200.0}
    for name, (base, spread) in spreads.items():
        noise = np.random.default_rng([zlib.crc32(name.encode()), seed]).standard_normal(out[name].shape)
        drawn = base * np.exp(spread * noise) if base else spread * noise
        out[name] = jnp.asarray(drawn.astype(out[name].dtype))
    for name, factor in factors.items():
        out[name] = (out[name] * factor).astype(out[name].dtype)
    return out
```

```python
from contextlib import ExitStack

import numpy as np

import concourse.bass as bass
from concourse import mybir

F32 = mybir.dt.float32
F32R = mybir.dt.float32r
BF16 = mybir.dt.bfloat16
I32 = mybir.dt.int32
U32 = mybir.dt.uint32
ALU = mybir.AluOpType
ACT = mybir.ActivationFunctionType
AX = mybir.AxisListType

P = 128
BATCH, SEQ, D = 4, 512, 512
TOKENS = BATCH * SEQ
KC = D // P
QT = SEQ // P
HEADS, HD = 32, 16
E0, R0 = 8, 16
E1, A1, R1 = 16, 4, 8
Z1 = A1 * R1
EPS = 1e-5
MASKED = -1e30
SCORE_SCALE = HD ** -0.5
RSQRT_MAGIC = 1597463007.0

UH = 4
UNITS = HEADS // UH
CHUNKS = HEADS * HD // P
STACKS = 3
PART0 = 2
MAX0 = P - 2


ONE, DMA_ONE = 1, 16


def twice(b, t):
    return b * QT + max(t - 1, 0)


def layer_norm(dve, x, xhat, small, nb, sem, base, xhat_free, ready):
    stats, mean, ve, y, a = small
    n = QT
    for t in range(QT):
        dve.bn_stats(stats[:, t, :], x[:, nb * QT + t, :]).then_inc(sem, 1)
    dve.wait_ge(sem, base + n)
    dve.tensor_tensor(mean[:], stats[:, :, 1], stats[:, :, 4], ALU.add).then_inc(sem, 1)
    dve.tensor_tensor(a[:], stats[:, :, 1], stats[:, :, 4], ALU.subtract).then_inc(sem, 1)
    dve.tensor_tensor(ve[:], stats[:, :, 2], stats[:, :, 5], ALU.add).then_inc(sem, 1)
    dve.wait_ge(sem, base + n + 3)
    dve.tensor_scalar(mean[:], mean[:], 0.5, None, ALU.mult).then_inc(sem, 1)
    dve.tensor_tensor(a[:], a[:], a[:], ALU.mult).then_inc(sem, 1)
    dve.tensor_scalar(ve[:], ve[:], 1.0 / D, EPS, ALU.mult, ALU.add).then_inc(sem, 1)
    dve.wait_ge(sem, base + n + 6)
    dve.scalar_tensor_tensor(ve[:], a[:], 0.25, ve[:], ALU.mult, ALU.add).then_inc(sem, 1)
    n += 7
    dve.wait_ge(sem, base + n)
    dve.tensor_scalar(y[:].bitcast(I32), ve[:].bitcast(I32), -0.5, RSQRT_MAGIC, ALU.mult, ALU.add).then_inc(sem, 1)
    n += 1
    for _ in range(3):
        dve.wait_ge(sem, base + n)
        dve.tensor_tensor(a[:], y[:], y[:], ALU.mult).then_inc(sem, 1)
        dve.wait_ge(sem, base + n + 1)
        dve.scalar_tensor_tensor(a[:], a[:], -0.5, ve[:], ALU.mult, ALU.mult).then_inc(sem, 1)
        dve.wait_ge(sem, base + n + 2)
        dve.scalar_tensor_tensor(y[:], a[:], 1.5, y[:], ALU.add, ALU.mult).then_inc(sem, 1)
        n += 3
    dve.wait_ge(sem, base + n)
    xhat_free()
    for t in range(QT):
        dve.tensor_scalar(xhat[:, t, :], x[:, nb * QT + t, :], mean[:, t:t + 1], y[:, t:t + 1],
                          ALU.subtract, ALU.mult).then_inc(ready, 1)


LN_STEPS = QT + 7 + 1 + 9


def macaron(nc, x_in, w, out, stages=6):
    ctx = ExitStack()
    nsem = [0]

    def sb(name, shape, dt=F32, c=ctx):
        return c.enter_context(nc.sbuf_tensor(name, shape, dt))

    def ps(name, shape, dt=F32, c=ctx):
        return c.enter_context(nc.psum_tensor(name, shape, dt))

    def sem(name):
        nsem[0] += 1
        return ctx.enter_context(nc.semaphore(name))

    with ctx:
        x = sb("x", [P, TOKENS // P, D])
        xhat = sb("xhat", [P, QT, D])
        xT = sb("xT", [P, KC, SEQ])
        ident = sb("ident", [P, P])
        identb = sb("identb", [P, P], BF16)
        causal = sb("causal", [P, P], BF16)
        ln_small = (sb("ln_stats", [P, QT, 6]), sb("ln_mean", [P, QT]), sb("ln_ve", [P, QT]),
                    sb("ln_y", [P, QT]), sb("ln_a", [P, QT]))
        w_base = sb("w_base", [P, KC, D])
        w_z1 = sb("w_z1", [P, KC, Z1 + A1])
        w_b1 = sb("w_b1", [Z1, D])
        half_b = sb("half_b", [P, D])
        gate_b = sb("gate_b", [P, A1])
        causal_t = sb("causal_t", [P, P], BF16)
        Qs = [sb(f"Qs{i}", [P, UH, SEQ], F32R) for i in range(STACKS)]
        Ks = [sb(f"Ks{i}", [P, UH, SEQ], F32R) for i in range(STACKS)]
        slopes = sb("slopes", [2, HEADS])
        got_consts, zeroed, rounded, keys_in, passed = (
            sem(n) for n in ("got_consts", "zeroed_stacks", "rounded", "keys_in", "passed"))

        got_x0, got_x, got_ffn0, got_att0, got_raw1, got_base1, got_att1 = (
            sem(n) for n in ("got_x0", "got_x", "got_ffn0", "got_att0", "got_raw1", "got_base1", "got_att1"))
        stored = sem("stored")
        x_rows = x_in.rearrange("b (t p) d -> p (b t) d", p=P)

        layer0 = ExitStack()
        w_ar0 = sb("w_ar0", [P, KC, E0 * R0 + E0], F32, layer0)
        w_b0 = sb("w_b0", [P, D], F32, layer0)
        number8 = sb("number8", [P, E0], F32, layer0)
        layer0a = ExitStack()
        w_q0 = sb("w_q0", [P, KC, D], F32, layer0a)
        w_k0 = sb("w_k0", [P, KC, 3 * HD], F32, layer0a)
        w_v0 = sb("w_v0", [P, KC, HD], F32, layer0a)
        w_o0 = sb("w_o0", [P, KC, D], F32, layer0a)

        with ExitStack() as c:
            act_i = sb("act_i", [P, A1], I32, c)
            act_f = sb("act_f", [P, A1], F32, c)
            act_n = sb("act_n", [P, A1], F32, c)
            row_i = sb("row_i", [P, R1 + 2], I32, c)
            row_f = sb("row_f", [P, R1 + 2], F32, c)
            row_e = sb("row_e", [P, 1], I32, c)
            row_r = sb("row_r", [P, 1], I32, c)
            rank_i = sb("rank_i", [P, R1], I32, c)
            rank_f = sb("rank_f", [P, R1], F32, c)
            iota_i = sb("iota_i", [P, E0], I32, c)
            part_i = sb("part_i", [P, 1], I32, c)
            part_f = sb("part_f", [P, 1], F32, c)
            sel_e = sb("sel_e", [P, A1], F32, c)
            sel_r = sb("sel_r", [P, R1], F32, c)
            sel_er = sb("sel_er", [P, A1, R1], F32, c)
            sel_e16 = sb("sel_e16", [E1, A1], F32, c)
            lora_a = sb("lora_a", [P, D], F32, c)
            lora_b = sb("lora_b", [P, D], F32, c)
            rout = sb("rout", [E1, D], F32, c)
            rb = sb("rb", [E1, 1], F32, c)
            prior = sb("prior", [E1, 1], F32, c)
            lprior = sb("lprior", [E1, 1], F32, c)
            bias_bc = sb("bias_bc", [E1, P], F32, c)
            ones16 = sb("ones16", [E1, P], F32, c)
            pg = ps("pg", [P, KC, 512], F32, c)
            pb = ps("pb", [P, 512], F32, c)
            pl = ps("pl", [P, 512], F32, c)
            consts, iotas, zeroed_masks = sem("consts"), sem("iotas"), sem("zeroed_masks")
            s_dve, s_ln, s_act = sem("s_dve"), sem("s_ln"), sem("s_act")
            picked, xhat_ready = sem("picked"), sem("xhat_ready0")

            with nc.Block() as block:
                @block.sync
                def _(sp):
                    for t in range(QT):
                        sp.dma_start(x[:, t, :], x_rows[:, t, :]).then_inc(got_x0, 16)
                    sp.dma_start(w_ar0[:], w["ar0"].rearrange("(c p) m -> p c m", p=P)).then_inc(got_ffn0, 16)
                    sp.dma_start(w_b0[:], w["b0"]).then_inc(got_ffn0, 16)
                    sp.dma_start(act_i[:], w["active"].partition_broadcast(P)).then_inc(got_raw1, 16)
                    sp.dma_start(lora_a[:], w["lora_a"]).then_inc(got_raw1, 16)
                    sp.dma_start(lora_b[:], w["lora_b"]).then_inc(got_raw1, 16)
                    sp.dma_start(rout[:], w["router_w"]).then_inc(got_raw1, 16)
                    sp.dma_start(rb[:], w["router_b"].rearrange("(e a) -> e a", a=1)).then_inc(got_raw1, 16)
                    sp.dma_start(prior[:], w["prior"].rearrange("(e a) -> e a", a=1)).then_inc(got_raw1, 16)
                    sp.dma_start(half_b[:], w["b_base"].partition_broadcast(P)).then_inc(got_raw1, 16)
                    for b in range(1, BATCH):
                        sp.dma_start(x[:, b * QT:(b + 1) * QT, :], x_rows[:, b * QT:(b + 1) * QT, :]).then_inc(got_x, 16)
                    for dst, src in ((w_q0, "wq0"), (w_k0, "wk0"), (w_v0, "wv0"), (w_o0, "wo0")):
                        sp.dma_start(dst[:], w[src].rearrange("(c p) m -> p c m", p=P)).then_inc(got_att0, 16)
                    sp.dma_start(w_base[:], w["base"].rearrange("(c p) m -> p c m", p=P)).then_inc(got_base1, 16)

                @block.gpsimd
                def _(pool):
                    pool.memset(ident[:], 0.0).then_inc(zeroed_masks, 1)
                    pool.memset(identb[:], 0.0).then_inc(zeroed_masks, 1)
                    pool.memset(causal[:], 0.0).then_inc(zeroed_masks, 1)
                    pool.memset(causal_t[:], 0.0).then_inc(zeroed_masks, 1)
                    pool.iota(part_i[:], [[0, 1]], base=0, channel_multiplier=1).then_inc(iotas, 1)
                    pool.iota(rank_i[:], [[1, R1]], base=0, channel_multiplier=0).then_inc(iotas, 1)
                    pool.iota(iota_i[:], [[1, E0]], base=0, channel_multiplier=0).then_inc(iotas, 1)
                    pool.wait_ge(zeroed_masks, 4)
                    for m in (ident, identb):
                        pool.affine_select(out=m[:], in_=m[:], compare_op=ALU.not_equal, fill=1.0, base=0,
                                           pattern=[[-1, P]], channel_multiplier=1).then_inc(consts, 1)
                    pool.affine_select(out=causal[:], in_=causal[:], compare_op=ALU.is_ge, fill=MASKED, base=0,
                                       pattern=[[-1, P]], channel_multiplier=1).then_inc(consts, 1)
                    pool.affine_select(out=causal_t[:], in_=causal_t[:], compare_op=ALU.is_ge, fill=MASKED, base=0,
                                       pattern=[[1, P]], channel_multiplier=-1).then_inc(consts, 1)
                    pool.memset(ones16[:], 1.0).then_inc(consts, 1)

                @block.scalar
                def _(act):
                    act.wait_ge(s_dve, 1)
                    act.activation(lprior[:], prior[:], ACT.Ln).then_inc(s_act, 1)
                    act.wait_ge(picked, 1)
                    act.copy(w_z1[:], pg[:, :, 0:Z1 + A1]).then_inc(s_act, 1)
                    act.wait_ge(picked, 2)
                    act.copy(w_b1[:], pb[0:Z1, :]).then_inc(s_act, 1)
                    act.wait_ge(picked, 3)
                    act.copy(gate_b[:], pl[:, 0:A1]).then_inc(s_act, 1)

                @block.vector
                def _(dve):
                    k = 0

                    def step(ins):
                        nonlocal k
                        ins.then_inc(s_dve, 1)
                        k += 1
                        dve.wait_ge(s_dve, k)

                    dve.wait_ge(got_raw1, 7 * 16)
                    step(dve.tensor_scalar(prior[:], prior[:], 1e-12, None, ALU.add))
                    step(dve.tensor_copy(act_f[:], act_i[:]))
                    step(dve.tensor_scalar(act_n[:], act_f[:], 0.0, float(E1), ALU.is_lt, ALU.mult))
                    step(dve.tensor_tensor(act_f[:], act_f[:], act_n[:], ALU.add))
                    dve.wait_ge(iotas, 3)
                    step(dve.tensor_scalar(row_e[:], part_i[:], 3, None, ALU.logical_shift_right))
                    step(dve.tensor_scalar(row_r[:], part_i[:], R1 - 1, None, ALU.bitwise_and))
                    step(dve.tensor_copy(row_f[:, 0:1], row_e[:]))
                    step(dve.tensor_copy(row_f[:, 1:2], row_r[:]))
                    step(dve.tensor_copy(part_f[:], part_i[:]))
                    step(dve.tensor_copy(rank_f[:], rank_i[:]))
                    step(dve.tensor_scalar(number8[:], iota_i[:], float(-E0), None, ALU.add))
                    step(dve.tensor_scalar(sel_e[:], act_f[:], row_f[:, 0:1], None, ALU.is_equal))
                    step(dve.tensor_scalar(sel_r[:], rank_f[:], row_f[:, 1:2], None, ALU.is_equal))
                    step(dve.tensor_tensor(sel_er[:], sel_e[:].unsqueeze(2).broadcast_to([P, A1, R1]),
                                           sel_r[:].unsqueeze(1).broadcast_to([P, A1, R1]), ALU.mult))
                    step(dve.tensor_scalar(sel_e16[:], act_f[0:E1, :], part_f[0:E1, :], None, ALU.is_equal))
                    dve.wait_ge(s_act, 1)
                    step(dve.tensor_tensor(rb[:], rb[:], lprior[:], ALU.add))
                    dve.wait_ge(consts, 5)
                    step(dve.tensor_scalar(bias_bc[:], ones16[:], rb[:, 0:1], None, ALU.mult))
                    step(dve.tensor_scalar(half_b[:], half_b[:], 0.5, None, ALU.mult))
                    dve.wait_ge(got_x0, QT * 16)
                    layer_norm(dve, x, xhat, ln_small, 0, s_ln, 0, lambda: None, xhat_ready)

                @block.tensor
                def _(pe):
                    pe.wait_ge(s_dve, 17)
                    for k in range(KC):
                        last = pe.matmul(pg[:, k, 0:Z1], lora_a[:, k * P:(k + 1) * P], sel_er[:].rearrange("p a r -> p (a r)"),
                                         start=True, stop=True)
                        last = pe.matmul(pg[:, k, Z1:Z1 + A1], rout[:, k * P:(k + 1) * P], sel_e16[:],
                                         start=True, stop=True)
                    last.then_inc(picked, 1)
                    pe.matmul(pb[0:Z1, :], sel_er[:].rearrange("p a r -> p (a r)"), lora_b[:],
                              start=True, stop=True).then_inc(picked, 1)
                    pe.matmul(pl[:, 0:A1], bias_bc[:], sel_e16[:], start=True, stop=True).then_inc(picked, 1)

        def transposes(pe, b, pT, ready, done):
            for t in range(QT):
                if t == 0:
                    pe.wait_ge(done, ONE + b * QT)
                elif t > 1:
                    pe.wait_ge(done, ONE + b * QT + t - 1)
                for k in range(KC):
                    last = pe.transpose(pT[t % 2][:, k * P:(k + 1) * P], xhat[:, t, k * P:(k + 1) * P], ident[:])
                last.then_inc(ready, 1)

        def ffn0(tag, first):
            with ExitStack() as c:
                mx = sb(tag + "mx", [P, 2], F32, c)
                hit = sb(tag + "hit", [P, 2, E0], F32, c)
                pick = sb(tag + "pick", [P, 2], F32, c)
                gate = sb(tag + "gate", [P, 2, E0], F32, c)
                if first:
                    key_rows = sb("key_rows", [4, SEQ], F32, c)
                    key_rows_r = sb("key_rows_r", [4, SEQ], F32R, c)
                wh = sb(tag + "wh", [P, 2, E0 * R0], F32, c)
                whT = sb(tag + "whT", [P, 2, P], F32, c)
                pT = [ps(f"{tag}pT{i}", [P, 512], F32, c) for i in range(2)]
                pH = [ps(f"{tag}pH{i}", [P, 512], F32, c) for i in range(2)]
                pW = [ps(f"{tag}pW{i}", [P, 512], F32, c) for i in range(2)]
                pY = [ps(f"{tag}pY{i}", [P, 512], F32, c) for i in range(2)]
                xt_ready, xt_done, h_ready, wh_done, wt_ready, wt_done, y_ready, x_done = (
                    sem(tag + n) for n in ("xt_ready", "xt_done", "h_ready", "wh_done", "wt_ready", "wt_done",
                                           "y_ready", "x_done"))
                xhat_ready, s_ln, s_gate = sem(tag + "xhat"), sem(tag + "s_ln"), sem(tag + "s_gate")

                with nc.Block() as block:
                    if first:
                        @block.gpsimd
                        def _(pool):
                            for m in Ks + Qs:
                                pool.memset(m[:].bitcast(F32), 0.0).then_inc(zeroed, 1)
                            pool.wait_ge(got_consts, 32)
                            pool.wait_ge(zeroed, 2 * STACKS)
                            pool.tensor_copy(key_rows_r[:], key_rows[:]).then_inc(rounded, 1)

                        @block.sync
                        def _(sp):
                            sp.dma_start(key_rows[:], w["key_rows"]).then_inc(got_consts, 16)
                            sp.dma_start(slopes[:], w["slopes"]).then_inc(got_consts, 16)
                            sp.wait_ge(zeroed, 2 * STACKS)
                            sp.wait_ge(rounded, 1)
                            for m in Ks:
                                for row, at in ((0, 0), (2, MAX0)):
                                    for j in range(UH):
                                        sp.dma_start(m[at:at + 2, j, :].bitcast(F32),
                                                     key_rows_r[row:row + 2, :].bitcast(F32)).then_inc(keys_in, 16)
                            sp.wait_ge(keys_in, 2 * UH * STACKS * 16)

                    @block.tensor
                    def _(pe):
                        if first:
                            pe.wait_ge(got_ffn0, 2 * 16)
                        for s in (h_ready, wt_ready, y_ready,):
                            pe.sem_inc(s, ONE)
                        with pe.Fori(0, BATCH) as b:
                            pe.wait_ge(xhat_ready, ONE + b * QT)
                            transposes(pe, b, pT, xt_ready, xt_done)

                            def up(t):
                                pe.wait_ge(xt_done, ONE + b * QT + t + 1)
                                pe.wait_ge(wh_done, ONE + twice(b, t))
                                for k in range(KC):
                                    last = pe.matmul(pH[t % 2][:, 0:E0 * R0 + E0], xT[:, k, t * P:(t + 1) * P],
                                                     w_ar0[:, k, :], start=(k == 0), stop=(k == KC - 1))
                                last.then_inc(h_ready, 1)

                            def down(t):
                                pe.wait_ge(wh_done, ONE + b * QT + t + 1)
                                pe.wait_ge(wt_done, ONE + twice(b, t))
                                pe.transpose(pW[t % 2][:, 0:P], wh[:, t % 2, :], ident[:]).then_inc(wt_ready, 1)
                                pe.wait_ge(wt_done, ONE + b * QT + t + 1)
                                pe.wait_ge(x_done, ONE + twice(b, t))
                                pe.matmul(pY[t % 2][:], whT[:, t % 2, :], w_b0[:], start=True, stop=True).then_inc(y_ready, 1)

                            up(0)
                            for t in range(1, QT):
                                up(t)
                                down(t - 1)
                            down(QT - 1)

                    @block.scalar
                    def _(act):
                        for s in (xt_done, wt_done,):
                            act.sem_inc(s, ONE)
                        with act.Fori(0, BATCH) as b:
                            for t in range(QT):
                                act.wait_ge(xt_ready, b * QT + t + 1)
                                if t == 0:
                                    act.wait_ge(h_ready, ONE + b * QT)
                                act.copy(xT[:, :, t * P:(t + 1) * P],
                                         pT[t % 2][:].rearrange("p (k q) -> p k q", k=KC)).then_inc(xt_done, 1)
                            for t in range(QT):
                                act.wait_ge(wt_ready, ONE + b * QT + t + 1)
                                act.wait_ge(y_ready, ONE + twice(b, t))
                                act.copy(whT[:, t % 2, :], pW[t % 2][:, 0:P]).then_inc(wt_done, 1)

                    @block.vector
                    def _(dve):
                        if first:
                            dve.wait_ge(got_x, (BATCH - 1) * 16)
                        for s in (xhat_ready, wh_done, x_done,):
                            dve.sem_inc(s, ONE)
                        with dve.Fori(0, BATCH) as b:
                            def xhat_free():
                                dve.wait_ge(xt_ready, (b + 1) * QT)

                            dve.wait_ge(x_done, ONE + b * QT)
                            layer_norm(dve, x, xhat, ln_small, (b + 1) % BATCH, s_ln, b * LN_STEPS, xhat_free, xhat_ready)

                            def route(t):
                                i, n = t % 2, b * QT * 4 + t * 4
                                dve.wait_ge(h_ready, ONE + b * QT + t + 1)
                                logits = pH[i][:, E0 * R0:E0 * R0 + E0]
                                dve.tensor_reduce(mx[:, i:i + 1], logits, AX.X, ALU.max).then_inc(s_gate, 1)
                                dve.wait_ge(s_gate, n + 1)
                                dve.scalar_tensor_tensor(hit[:, i, :], logits, mx[:, i:i + 1], number8[:],
                                                         ALU.is_ge, ALU.mult).then_inc(s_gate, 1)
                                dve.wait_ge(s_gate, n + 2)
                                dve.tensor_reduce(pick[:, i:i + 1], hit[:, i, :], AX.X, ALU.min).then_inc(s_gate, 1)
                                dve.wait_ge(s_gate, n + 3)
                                dve.tensor_scalar(gate[:, i, :], number8[:], pick[:, i:i + 1], mx[:, i:i + 1],
                                                  ALU.is_equal, ALU.mult).then_inc(s_gate, 1)
                                dve.wait_ge(s_gate, n + 4)
                                dve.wait_ge(wt_ready, ONE + twice(b, t))
                                dve.tensor_tensor(wh[:, i, :].rearrange("p (e r) -> p e r", e=E0),
                                                  pH[i][:, 0:E0 * R0].rearrange("p (e r) -> p e r", e=E0),
                                                  gate[:, i, :].unsqueeze(2).broadcast_to([P, E0, R0]),
                                                  ALU.mult).then_inc(wh_done, 1)

                            def residual(t):
                                dve.wait_ge(y_ready, ONE + b * QT + t + 1)
                                xt = x[:, b * QT + t, :]
                                dve.scalar_tensor_tensor(xt, pY[t % 2][:], 0.5, xt, ALU.mult, ALU.add).then_inc(x_done, 1)

                            route(0)
                            for t in range(1, QT):
                                route(t)
                                residual(t - 1)
                            residual(QT - 1)

        def ffn1(tag, first, last_stage, prefetch):
            with ExitStack() as c:
                lg = sb(tag + "lg", [P, 2, A1], F32, c)
                nm = sb(tag + "nm", [P, 2], F32, c)
                ex = sb(tag + "ex", [P, 2, A1], F32, c)
                sm = sb(tag + "sm", [P, 2], F32, c)
                rs = sb(tag + "rs", [P, 2], F32, c)
                al = sb(tag + "al", [P, 2, A1], F32, c)
                wz = sb(tag + "wz", [P, 2, Z1], F32, c)
                wzT = sb(tag + "wzT", [Z1, 2, P], F32, c)
                pT = [ps(f"{tag}pT{i}", [P, 512], F32, c) for i in range(2)]
                pZ = [ps(f"{tag}pZ{i}", [P, 512], F32, c) for i in range(2)]
                pW = [ps(f"{tag}pW{i}", [P, 512], F32, c) for i in range(2)]
                pY = [ps(f"{tag}pY{i}", [P, 512], F32, c) for i in range(2)]
                xt_ready, xt_done, z_ready, lg_done, ex_done, wz_done, wt_ready, wt_done, y_ready, x_done = (
                    sem(tag + n) for n in ("xt_ready", "xt_done", "z_ready", "lg_done", "ex_done", "wz_done",
                                           "wt_ready", "wt_done", "y_ready", "x_done"))
                xhat_ready, s_ln, s_gate, s_res = sem(tag + "xhat"), sem(tag + "s_ln"), sem(tag + "s_gate"), sem(tag + "s_res")

                with nc.Block() as block:
                    @block.tensor
                    def _(pe):
                        if first:
                            pe.wait_ge(got_base1, 16)
                        for s in (wt_ready, y_ready,):
                            pe.sem_inc(s, ONE)
                        with pe.Fori(0, BATCH) as b:
                            pe.wait_ge(xhat_ready, ONE + b * QT)
                            transposes(pe, b, pT, xt_ready, xt_done)

                            def low_rank(t):
                                pe.wait_ge(xt_done, ONE + b * QT + t + 1)
                                pe.wait_ge(wz_done, ONE + twice(b, t))
                                for k in range(KC):
                                    last = pe.matmul(pZ[t % 2][:, 0:Z1 + A1], xT[:, k, t * P:(t + 1) * P],
                                                     w_z1[:, k, :], start=(k == 0), stop=(k == KC - 1))
                                last.then_inc(z_ready, 1)

                            def base(t):
                                pe.wait_ge(x_done, ONE + twice(b, t))
                                for k in range(KC):
                                    pe.matmul(pY[t % 2][:], xT[:, k, t * P:(t + 1) * P], w_base[:, k, :],
                                              start=(k == 0), stop=False)

                            def experts(t):
                                pe.wait_ge(wz_done, ONE + b * QT + t + 1)
                                pe.wait_ge(wt_done, ONE + twice(b, t))
                                pe.transpose(pW[t % 2][0:Z1, 0:P], wz[:, t % 2, :], ident[:]).then_inc(wt_ready, 1)
                                pe.wait_ge(wt_done, ONE + b * QT + t + 1)
                                pe.matmul(pY[t % 2][:], wzT[:, t % 2, :], w_b1[:], start=False, stop=True).then_inc(y_ready, 1)

                            low_rank(0)
                            for t in range(QT):
                                base(t)
                                if t + 1 < QT:
                                    low_rank(t + 1)
                                experts(t)

                    @block.scalar
                    def _(act):
                        for s in (xt_done, wt_done,):
                            act.sem_inc(s, ONE)
                        with act.Fori(0, BATCH) as b:
                            for t in range(QT):
                                act.wait_ge(xt_ready, b * QT + t + 1)
                                if t == 0:
                                    act.wait_ge(y_ready, ONE + b * QT)
                                act.copy(xT[:, :, t * P:(t + 1) * P],
                                         pT[t % 2][:].rearrange("p (k q) -> p k q", k=KC)).then_inc(xt_done, 1)
                            for t in range(QT):
                                i = t % 2
                                act.wait_ge(lg_done, b * QT + t + 1)
                                act.activation(ex[:, i, :], lg[:, i, :], ACT.Exp, bias=nm[:, i:i + 1],
                                               accum_out=sm[:, i:i + 1]).then_inc(ex_done, 1)
                                act.wait_ge(wt_ready, ONE + b * QT + t + 1)
                                act.wait_ge(y_ready, ONE + twice(b, t))
                                act.copy(wzT[:, i, :], pW[i][0:Z1, 0:P]).then_inc(wt_done, 1)

                    @block.vector
                    def _(dve):
                        for s in (xhat_ready, wz_done, x_done,):
                            dve.sem_inc(s, ONE)
                        with dve.Fori(0, BATCH) as b:
                            def xhat_free():
                                dve.wait_ge(xt_ready, (b + 1) * QT)

                            dve.wait_ge(x_done, ONE + b * QT)
                            layer_norm(dve, x, xhat, ln_small, (b + 1) % BATCH, s_ln, b * LN_STEPS, xhat_free, xhat_ready)

                            def gate(t):
                                i, n = t % 2, b * QT * 3 + t * 3
                                dve.wait_ge(z_ready, b * QT + t + 1)
                                dve.tensor_tensor(lg[:, i, :], pZ[i][:, Z1:Z1 + A1], gate_b[:], ALU.add).then_inc(s_gate, 1)
                                dve.wait_ge(s_gate, n + 1)
                                dve.tensor_reduce(nm[:, i:i + 1], lg[:, i, :], AX.X, ALU.max, negate=True).then_inc(lg_done, 1)
                                dve.wait_ge(ex_done, b * QT + t + 1)
                                dve.reciprocal(rs[:, i:i + 1], sm[:, i:i + 1]).then_inc(s_gate, 1)
                                dve.wait_ge(s_gate, n + 2)
                                dve.tensor_scalar(al[:, i, :], ex[:, i, :], rs[:, i:i + 1], 2.0, ALU.mult, ALU.mult).then_inc(s_gate, 1)
                                dve.wait_ge(s_gate, n + 3)
                                dve.wait_ge(wt_ready, ONE + twice(b, t))
                                dve.tensor_tensor(wz[:, i, :].rearrange("p (a r) -> p a r", a=A1),
                                                  pZ[i][:, 0:Z1].rearrange("p (a r) -> p a r", a=A1),
                                                  al[:, i, :].unsqueeze(2).broadcast_to([P, A1, R1]),
                                                  ALU.mult).then_inc(wz_done, 1)

                            def residual(t):
                                dve.wait_ge(y_ready, ONE + b * QT + t + 1)
                                xt = x[:, b * QT + t, :]
                                dve.scalar_tensor_tensor(xt, pY[t % 2][:], 0.5, xt, ALU.mult, ALU.add).then_inc(s_res, 1)
                                dve.wait_ge(s_res, b * QT + t + 1)
                                dve.tensor_tensor(xt, xt, half_b[:], ALU.add).then_inc(x_done, 1)

                            gate(0)
                            for t in range(1, QT):
                                gate(t)
                                residual(t - 1)
                            residual(QT - 1)

                    @block.sync
                    def _(sp):
                        if prefetch is not None:
                            prefetch(sp)
                        if last_stage:
                            out_rows = out.rearrange("b (t p) d -> p (b t) d", p=P)
                            with sp.Fori(0, TOKENS // P) as i:
                                sp.wait_ge(x_done, ONE + i + 1)
                                sp.dma_start(out_rows[:, bass.ds(i, 1), :], x[:, bass.ds(i, 1), :]).then_inc(stored, 16)
                            sp.wait_ge(stored, TOKENS // P * 16)

        def attention(tag, w_q, w_k, w_v, w_o, own_k, got_weights, n_weights, b_qk, b_v, b_o):
            GROUPS = [(0, (0, 1, 2, 3)), (1, (0, 1)), (1, (2, 3))] + [(qt, (j,)) for qt in (2, 3) for j in range(UH)]
            HALF = 5

            def groups(n, lo, hi):
                return [("A", n, g) for g in range(lo, hi)] if n < UNITS else []

            def projected(c):
                return [("Q", c)] + ([("K", c)] if own_k else [])

            items = [("T", t) for t in range(QT)]
            if not own_k:
                items += [("K", 0)]
            items += projected(0) + [("V", t) for t in (range(QT) if own_k else (0,))] + projected(1)
            items += groups(0, 0, len(GROUPS)) + [("M", 0)] + groups(1, 0, HALF)
            for n in range(UNITS):
                if n % 2 == 0 and n // 2 + 2 < CHUNKS:
                    items += projected(n // 2 + 2)
                if n + 1 < UNITS:
                    items += groups(n + 1, HALF, len(GROUPS)) + [("M", n + 1)] + groups(n + 2, 0, HALF)
            items += [("W", t) for t in range(QT)]
            at = {item: i for i, item in enumerate(items)}
            N, ND = len(items), len(items) - QT
            splits = [item for item in items if item[0] in "QKM"]
            split_at = {item: i for i, item in enumerate(splits)}
            NS = len(splits)
            LOADS = 4 if own_k else 2
            PARTS = 4 if own_k else 2
            PAIRS = QT * UH // 2
            uses = [len(range(s, UNITS, STACKS)) for s in range(STACKS)]

            with ExitStack() as c:
                if own_k:
                    vv = sb(tag + "vv", [P, QT, HEADS, HD, 2], F32, c)
                else:
                    k_all = Ks[0][:, 0, :]
                    k_first = sb(tag + "k_first", [3 * HD, 1, SEQ], F32R, c)
                    vv = sb(tag + "vv", [P, QT, HD, 2], F32, c)
                parts = sb(tag + "parts", [P, PARTS, SEQ], F32R, c)
                spread = nc.dram_tensor(tag + "spread", (CHUNKS, PARTS, P, SEQ), F32, kind="Internal").ap()
                probs = [sb(f"{tag}probs{i}", [P, UH, SEQ - i * P], F32, c) for i in range(2)]
                o_raw = sb(tag + "o_raw", [P, 2, SEQ], F32, c)
                oT = sb(tag + "oT", [P, CHUNKS, SEQ], F32, c)
                den = sb(tag + "den", [P, SEQ], F32, c)
                neg_max = sb(tag + "neg_max", [P, QT, UH], F32, c)
                nm_hi = sb(tag + "nm_hi", [UH, SEQ], F32R, c)
                nm_lo = sb(tag + "nm_lo", [UH, SEQ], F32R, c)
                bank = [ps(f"{tag}bank{i}", [P, 512], F32, c) for i in range(3)]
                pS = [ps(f"{tag}pS{i}", [P, 2, 512], F32, c) for i in range(2)]
                pO = ps(tag + "pO", [P, 512], F32, c)

                ready, xt_done, bank_read, hi_done = (sem(tag + n) for n in ("ready", "xt_done", "bank_read", "hi_done"))
                s_ready, exp_done, pv_done, o_done, ones_in = (
                    sem(tag + n) for n in ("s_ready", "exp_done", "pv_done", "o_done", "ones_in"))
                spread_out = sem(tag + "spread_out")
                loaded = [sem(f"{tag}loaded{i}") for i in range(STACKS)]
                max_in = sem(tag + "max_in")
                packed = [sem(f"{tag}packed{i}") for i in range(2)]
                slopes_in, norm_done, s_den, s_res = (sem(tag + n) for n in ("slopes_in", "norm_done", "s_den", "s_res"))
                xhat_ready, s_ln, key_parts_in = sem(tag + "xhat"), sem(tag + "s_ln"), sem(tag + "key_parts_in")

                def psum_of(item):
                    return bank[at[item] % 3]

                def item_ready(eng, b, item):
                    eng.wait_ge(ready, b * N + at[item] + 1)

                def item_read(eng, b, item):
                    if item[0] == "T":
                        eng.wait_ge(xt_done, b * QT + item[1] + 1)
                    else:
                        eng.wait_ge(bank_read, ONE + b * ND + at[item] - QT + 1)

                def bank_free(pe, b, item):
                    if at[item] >= 3:
                        item_read(pe, b, items[at[item] - 3])
                    elif at[item] == 0:
                        pe.wait_ge(bank_read, ONE + b * ND)

                def stack_free(eng, b, n):
                    eng.wait_ge(s_ready, ONE + b * UNITS * PAIRS + max(n - STACKS + 1, 0) * PAIRS)

                def stack_loaded(eng, b, n):
                    eng.wait_ge(loaded[n % STACKS], (b * uses[n % STACKS] + n // STACKS + 1) * LOADS * 16)

                def keys(n, j, rows, cols):
                    return Ks[n % STACKS][0:rows, j, cols] if own_k else k_all[0:rows, cols]

                def part(kind, i):
                    return parts[:, i + (2 if kind == "K" else 0), :]

                with nc.Block() as block:
                    @block.tensor
                    def _(pe):
                        pe.wait_ge(got_weights, n_weights * 16)
                        for s in (s_ready, pv_done,):
                            pe.sem_inc(s, ONE)
                        with pe.Fori(0, BATCH) as b:
                            def project(kind, c, weights, cols):
                                item = (kind, c)
                                bank_free(pe, b, item)
                                m = weights[:, 0, cols].shape[-1]
                                for k in range(KC):
                                    last = pe.matmul(psum_of(item)[0:m, :], weights[:, k, cols], xT[:, k, :],
                                                     start=(k == 0), stop=(k == KC - 1))
                                last.then_inc(ready, 1)

                            def project_chunk(c):
                                project("Q", c, w_q, slice(c * P, (c + 1) * P))
                                if own_k:
                                    project("K", c, w_k, slice(c * P, (c + 1) * P))

                            def max_scores(n, lo, hi):
                                for g in range(lo, hi):
                                    if g == 0:
                                        if not own_k and n == 0:
                                            pe.wait_ge(key_parts_in, (b + 1) * 16)
                                        stack_loaded(pe, b, n)
                                        pe.wait_ge(slopes_in, b * UNITS + n + 1)
                                    bank_free(pe, b, ("A", n, g))
                                    out_bank = psum_of(("A", n, g))
                                    qt, heads = GROUPS[g]
                                    width = (qt + 1) * P
                                    for i, j in enumerate(heads):
                                        pe.matmul(out_bank[:, i * width:(i + 1) * width],
                                                  Qs[n % STACKS][0:MAX0, j, qt * P:(qt + 1) * P],
                                                  keys(n, j, MAX0, slice(0, width)), start=True, stop=False)
                                        last = pe.matmul(out_bank[:, (i + 1) * width - P:(i + 1) * width],
                                                         identb[:], causal[:], start=False, stop=True)
                                    last.then_inc(ready, 1)

                            def max_rows(n):
                                item_read(pe, b, ("A", n, len(GROUPS) - 1))
                                bank_free(pe, b, ("M", n))
                                for qt in range(QT):
                                    last = pe.transpose(psum_of(("M", n))[0:UH, qt * P:(qt + 1) * P],
                                                        neg_max[:, qt, :], ident[:])
                                last.then_inc(ready, 1)

                            def scores(n, kt):
                                if kt == 0:
                                    pe.wait_ge(max_in, DMA_ONE + (b * UNITS + n + 1) * 32)
                                for p in range(2):
                                    i = n * PAIRS + kt * 2 + p
                                    pe.wait_ge(exp_done, ONE + b * UNITS * PAIRS + max(i - 1, 0))
                                    for j in range(2):
                                        pe.matmul(pS[p][:, j, 0:SEQ - kt * P],
                                                  keys(n, 2 * p + j, P, slice(kt * P, (kt + 1) * P)),
                                                  Qs[n % STACKS][:, 2 * p + j, kt * P:SEQ], start=True, stop=False)
                                        last = pe.matmul(pS[p][:, j, 0:P], identb[:], causal_t[:], start=False, stop=True)
                                    last.then_inc(s_ready, 1)

                            def values(n, kt):
                                pe.wait_ge(exp_done, ONE + b * UNITS * PAIRS + n * PAIRS + kt * 2 + 2)
                                if kt == 0:
                                    pe.wait_ge(o_done, ONE + b * UNITS + n)
                                for j in range(UH):
                                    v_tile = (vv[:, kt, n * UH + j] if own_k else vv[:, kt]).rearrange("p d s -> p (d s)")
                                    last = pe.matmul(pO[32 * j:32 * (j + 1), kt * P:SEQ], v_tile,
                                                     probs[kt % 2][:, j, 0:SEQ - kt * P],
                                                     start=(kt == 0), stop=(kt == QT - 1))
                                last.then_inc(pv_done, 1)

                            pe.wait_ge(xhat_ready, ONE + b * QT)
                            for t in range(QT):
                                bank_free(pe, b, ("T", t))
                                for k in range(KC):
                                    last = pe.transpose(psum_of(("T", t))[:, k * P:(k + 1) * P],
                                                        xhat[:, t, k * P:(k + 1) * P], ident[:])
                                last.then_inc(ready, 1)
                            item_read(pe, b, ("T", QT - 1))
                            if not own_k:
                                project("K", 0, w_k, slice(0, 3 * HD))
                            project_chunk(0)
                            if own_k:
                                for t in range(QT):
                                    bank_free(pe, b, ("V", t))
                                    for k in range(KC):
                                        last = pe.matmul(psum_of(("V", t))[:], xT[:, k, t * P:(t + 1) * P], w_v[:, k, :],
                                                         start=(k == 0), stop=(k == KC - 1))
                                    last.then_inc(ready, 1)
                            else:
                                bank_free(pe, b, ("V", 0))
                                for t in range(QT):
                                    for k in range(KC):
                                        last = pe.matmul(psum_of(("V", 0))[:, t * HD:(t + 1) * HD],
                                                         xT[:, k, t * P:(t + 1) * P], w_v[:, k, :],
                                                         start=(k == 0), stop=(k == KC - 1))
                                last.then_inc(ready, 1)
                            project_chunk(1)
                            max_scores(0, 0, len(GROUPS))
                            max_rows(0)
                            max_scores(1, 0, HALF)
                            for n in range(UNITS):
                                scores(n, 0)
                                if n % 2 == 0 and n // 2 + 2 < CHUNKS:
                                    project_chunk(n // 2 + 2)
                                if n + 1 < UNITS:
                                    max_scores(n + 1, HALF, HALF + 3)
                                scores(n, 1)
                                if n + 1 < UNITS:
                                    max_scores(n + 1, HALF + 3, len(GROUPS))
                                values(n, 0)
                                scores(n, 2)
                                if n + 1 < UNITS:
                                    max_rows(n + 1)
                                values(n, 1)
                                scores(n, 3)
                                if n + 2 < UNITS:
                                    max_scores(n + 2, 0, 3)
                                values(n, 2)
                                if n + 2 < UNITS:
                                    max_scores(n + 2, 3, HALF)
                                values(n, 3)
                            pe.wait_ge(norm_done, ONE + (b + 1) * CHUNKS)
                            for t in range(QT):
                                bank_free(pe, b, ("W", t))
                                for k in range(CHUNKS):
                                    last = pe.matmul(psum_of(("W", t))[:], oT[:, k, t * P:(t + 1) * P], w_o[:, k, :],
                                                     start=(k == 0), stop=(k == CHUNKS - 1))
                                last.then_inc(ready, 1)

                    @block.scalar
                    def _(act):
                        for s in (exp_done, o_done,):
                            act.sem_inc(s, ONE)
                        with act.Fori(0, BATCH) as b:
                            def high(kind, c):
                                item_ready(act, b, (kind, c))
                                if not own_k and kind == "K":
                                    act.copy(k_first[:, 0, :], psum_of((kind, c))[0:3 * HD, :]).then_inc(hi_done, 1)
                                    return
                                dst = part(kind, 0)
                                act.wait_ge(spread_out, DMA_ONE + (b * CHUNKS + c) * 16)
                                if b_qk is None:
                                    act.copy(dst, psum_of((kind, c))[:]).then_inc(hi_done, 1)
                                else:
                                    col = c + (CHUNKS if kind == "K" else 0)
                                    act.activation(dst, psum_of((kind, c))[:], ACT.Identity,
                                                   bias=b_qk[:, col:col + 1]).then_inc(hi_done, 1)

                            def high_chunk(c):
                                high("Q", c)
                                if own_k:
                                    high("K", c)

                            def high_max(n):
                                act.wait_ge(max_in, DMA_ONE + (b * UNITS + n) * 32)
                                item_ready(act, b, ("M", n))
                                act.copy(nm_hi[:], psum_of(("M", n))[0:UH, :]).then_inc(hi_done, 1)

                            def exps(n, kt):
                                for p in range(2):
                                    act.wait_ge(pv_done, ONE + b * UNITS * QT + max(n * QT + kt - 1, 0))
                                    act.wait_ge(s_ready, ONE + b * UNITS * PAIRS + n * PAIRS + kt * 2 + p + 1)
                                    act.activation(probs[kt % 2][:, 2 * p:2 * p + 2, 0:SEQ - kt * P],
                                                   pS[p][:, :, 0:SEQ - kt * P], ACT.Exp, scale=SCORE_SCALE).then_inc(exp_done, 1)

                            for t in range(QT):
                                item_ready(act, b, ("T", t))
                                act.copy(xT[:, :, t * P:(t + 1) * P],
                                         psum_of(("T", t))[:].rearrange("p (k q) -> p k q", k=KC)).then_inc(xt_done, 1)
                            if not own_k:
                                high("K", 0)
                            high_chunk(0)
                            high_chunk(1)
                            high_max(0)
                            for n in range(UNITS):
                                exps(n, 0)
                                if n % 2 == 0 and n // 2 + 2 < CHUNKS:
                                    high_chunk(n // 2 + 2)
                                exps(n, 1)
                                exps(n, 2)
                                if n + 1 < UNITS:
                                    high_max(n + 1)
                                exps(n, 3)
                                act.wait_ge(packed[n % 2], DMA_ONE + (b * CHUNKS + n // 2) * 32)
                                act.wait_ge(pv_done, ONE + b * UNITS * QT + (n + 1) * QT)
                                act.copy(o_raw[:, n % 2, :], pO[:]).then_inc(o_done, 1)

                    @block.gpsimd
                    def _(pool):
                        for t in range(QT):
                            pool.memset(vv[:, t, :, :, 1] if own_k else vv[:, t, :, 1], 1.0).then_inc(ones_in, 1)
                        pool.wait_ge(ones_in, QT)
                        with pool.Fori(0, BATCH) as b:
                            for n in range(UNITS):
                                stack_free(pool, b, n)
                                pool.sem_inc(passed, 1)
                                pool.tensor_copy(Qs[n % STACKS][0:2, :, :],
                                                 slopes[:, n * UH:(n + 1) * UH].unsqueeze(2).broadcast_to([2, UH, SEQ])
                                                 ).then_inc(slopes_in, 1)

                    @block.vector
                    def _(dve):
                        dve.wait_ge(ones_in, QT)
                        for s in (xhat_ready, bank_read, norm_done,):
                            dve.sem_inc(s, ONE)
                        with dve.Fori(0, BATCH) as b:
                            def low(kind, c):
                                dve.wait_ge(hi_done, b * NS + split_at[(kind, c)] + 1)
                                src = psum_of((kind, c))
                                if not own_k and kind == "K":
                                    rows = k_first[2 * HD:3 * HD, 0, :]
                                    dve.tensor_tensor(rows, src[2 * HD:3 * HD, :], rows.bitcast(F32), ALU.subtract).then_inc(bank_read, 1)
                                    return
                                hi, lo = part(kind, 0), part(kind, 1)
                                if b_qk is None:
                                    dve.tensor_tensor(lo, src[:], hi.bitcast(F32),
                                                      ALU.subtract).then_inc(bank_read, 1)
                                else:
                                    col = c + (CHUNKS if kind == "K" else 0)
                                    dve.scalar_tensor_tensor(lo, src[:], b_qk[:, col:col + 1],
                                                             hi.bitcast(F32), ALU.add, ALU.subtract).then_inc(bank_read, 1)

                            def low_chunk(c):
                                low("Q", c)
                                if own_k:
                                    low("K", c)

                            def maxima(n, lo, hi):
                                for g in range(lo, hi):
                                    item_ready(dve, b, ("A", n, g))
                                    qt, heads = GROUPS[g]
                                    width, m = (qt + 1) * P, len(heads)
                                    dve.tensor_reduce(neg_max[:, qt, heads[0]:heads[0] + m],
                                                      psum_of(("A", n, g))[:, 0:m * width].rearrange("p (h k) -> p h k", h=m),
                                                      AX.X, ALU.max, negate=True).then_inc(bank_read, 1)

                            def low_max(n):
                                dve.wait_ge(hi_done, b * NS + split_at[("M", n)] + 1)
                                dve.tensor_tensor(nm_lo[:], psum_of(("M", n))[0:UH, :],
                                                  nm_hi[:].bitcast(F32), ALU.subtract).then_inc(bank_read, 1)

                            def normalise(c):
                                for s in range(2):
                                    dve.wait_ge(packed[s], DMA_ONE + (b * CHUNKS + c + 1) * 32)
                                dve.reciprocal(den[:], den[:]).then_inc(s_den, 1)
                                dve.wait_ge(s_den, b * CHUNKS + c + 1)
                                dve.tensor_tensor(oT[:, c, :], oT[:, c, :], den[:], ALU.mult).then_inc(norm_done, 1)

                            if not own_k:
                                low("K", 0)
                            low_chunk(0)
                            if own_k:
                                for t in range(QT):
                                    item_ready(dve, b, ("V", t))
                                    dve.tensor_tensor(vv[:, t, :, :, 0], psum_of(("V", t))[:].rearrange("p (h d) -> p h d", h=HEADS),
                                                      b_v[:].rearrange("p (h d) -> p h d", h=HEADS), ALU.add).then_inc(bank_read, 1)
                            else:
                                item_ready(dve, b, ("V", 0))
                                dve.tensor_copy(vv[:, :, :, 0], psum_of(("V", 0))[:, 0:QT * HD].rearrange("p (t d) -> p t d", t=QT)
                                                ).then_inc(bank_read, 1)
                            low_chunk(1)

                            def xhat_free():
                                item_ready(dve, b, ("T", QT - 1))

                            dve.wait_ge(bank_read, ONE + b * ND)
                            layer_norm(dve, x, xhat, ln_small, (b + 1) % BATCH, s_ln, b * LN_STEPS, xhat_free, xhat_ready)
                            maxima(0, 0, len(GROUPS))
                            low_max(0)
                            maxima(1, 0, HALF)
                            for n in range(UNITS):
                                if n % 2 == 0 and n // 2 + 2 < CHUNKS:
                                    low_chunk(n // 2 + 2)
                                if n + 1 < UNITS:
                                    maxima(n + 1, HALF, len(GROUPS))
                                    low_max(n + 1)
                                if n + 2 < UNITS:
                                    maxima(n + 2, 0, HALF)
                                if n % 2 == 0 and n >= 2:
                                    normalise(n // 2 - 1)
                            normalise(CHUNKS - 1)
                            for t in range(QT):
                                item_ready(dve, b, ("W", t))
                                xt = x[:, b * QT + t, :]
                                if b_o is None:
                                    dve.tensor_tensor(xt, psum_of(("W", t))[:], xt, ALU.add).then_inc(bank_read, 1)
                                else:
                                    dve.tensor_tensor(xt, psum_of(("W", t))[:], xt, ALU.add).then_inc(s_res, 1)
                                    dve.wait_ge(s_res, b * QT + t + 1)
                                    dve.tensor_tensor(xt, xt, b_o[:], ALU.add).then_inc(bank_read, 1)

                    @block.sync
                    def _(sp):
                        for s in (spread_out, max_in, packed[0], packed[1],):
                            sp.sem_inc(s, DMA_ONE)
                        with sp.Fori(0, BATCH) as b:
                            def store_parts(c):
                                item_read(sp, b, ("K", c) if own_k else ("Q", c))
                                sp.dma_start(spread[c].rearrange("i p t -> p i t"),
                                             parts[:].bitcast(F32)).then_inc(spread_out, 16)

                            def load_stack(n):
                                c, first = n // 2, (n % 2) * UH
                                sp.wait_ge(spread_out, DMA_ONE + (b * CHUNKS + c + 1) * 16)
                                sp.sem_inc(passed, 1)
                                stack_free(sp, b, n)
                                rows = spread[c].rearrange("i (d h) t -> (i d) h t", d=HD)[:, first:first + UH, :]

                                def load(stack, at, lo, hi):
                                    sp.dma_start(stack[n % STACKS][PART0 + at * HD:PART0 + (at + hi - lo) * HD, :, :].bitcast(F32),
                                                 rows[lo * HD:hi * HD]).then_inc(loaded[n % STACKS], 16)

                                load(Qs, 0, 0, 2)
                                load(Qs, 2, 0, 1)
                                if own_k:
                                    load(Ks, 0, 2, 3)
                                    load(Ks, 1, 2, 4)

                            def load_max(n):
                                item_read(sp, b, ("M", n))
                                for i, part in enumerate((nm_hi, nm_lo)):
                                    sp.dma_start(Qs[n % STACKS][MAX0 + i:MAX0 + i + 1, :, :].bitcast(F32),
                                                 part[:].bitcast(F32)).then_inc(max_in, 16)

                            def pack(n):
                                c, r = n // 2, (n % 2) * UH * HD
                                sp.wait_ge(o_done, ONE + b * UNITS + n + 1)
                                sp.sem_inc(passed, 1)
                                sp.wait_ge(norm_done, ONE + b * CHUNKS + c)
                                for i, dst in enumerate((oT[r:r + UH * HD, c, :], den[r:r + UH * HD, :])):
                                    sp.dma_start(dst, o_raw[i:P:2, n % 2, :]).then_inc(packed[n % 2], 16)

                            if not own_k:
                                item_read(sp, b, ("K", 0))
                                sp.dma_start(k_all[PART0:PART0 + 3 * HD, :].bitcast(F32),
                                             k_first[:, 0, :].bitcast(F32)).then_inc(key_parts_in, 16)
                            store_parts(0)
                            load_stack(0)
                            load_stack(1)
                            load_max(0)
                            store_parts(1)
                            load_stack(2)
                            for n in range(UNITS):
                                if n % 2 == 0 and n // 2 + 2 < CHUNKS:
                                    store_parts(n // 2 + 2)
                                if n + 1 < UNITS:
                                    load_max(n + 1)
                                if n + STACKS < UNITS:
                                    load_stack(n + STACKS)
                                pack(n)

        if stages >= 1:
            ffn0("a_", True)
        if stages >= 2:
            attention("m_", w_q0, w_k0, w_v0, w_o0, False, got_att0, 4, None, None, None)
        layer0a.close()
        if stages >= 3:
            ffn0("b_", False)
        layer0.close()
        if stages < 4:
            with nc.Block() as block:
                @block.sync
                def _(sp):
                    sp.wait_ge(got_base1, 16)
                    sp.wait_ge(got_att0, 64)
                    sp.dma_start(out.rearrange("b (t p) d -> p (b t) d", p=P), x[:]).then_inc(stored, 16)
                    sp.wait_ge(stored, 16)
        else:
            layer1 = ExitStack()
            w_qk1 = sb("w_qk1", [P, KC, 2 * D], F32, layer1)
            w_v1 = sb("w_v1", [P, KC, D], F32, layer1)
            w_o1 = sb("w_o1", [P, KC, D], F32, layer1)
            b_v1 = sb("b_v1", [P, D], F32, layer1)
            b_o1 = sb("b_o1", [P, D], F32, layer1)
            b_qk1 = sb("b_qk1", [P, 2 * CHUNKS], F32, layer1)

            def load_layer1(sp):
                for dst, src in ((w_qk1, "wqk1"), (w_v1, "wv1"), (w_o1, "wo1")):
                    sp.dma_start(dst[:], w[src].rearrange("(c p) m -> p c m", p=P)).then_inc(got_att1, 16)
                sp.dma_start(b_v1[:], w["bv1"].partition_broadcast(P)).then_inc(got_att1, 16)
                sp.dma_start(b_o1[:], w["bo1"].partition_broadcast(P)).then_inc(got_att1, 16)
                sp.dma_start(b_qk1[:], w["bqk1"]).then_inc(got_att1, 16)

            ffn1("c_", True, stages == 4, load_layer1 if stages > 4 else None)
            if stages > 4:
                attention("h_", w_qk1[:, :, 0:D], w_qk1[:, :, D:2 * D], w_v1, w_o1, True, got_att1, 6, b_qk1, b_v1, b_o1)
                layer1.close()
                ffn1("d_", False, True, None)


def kernel(stages=6, **inputs):
    import numpy as _np
    import concourse.bacc as _bacc
    from concourse import mybir as _mybir
    from concourse.bass_utils import run_bass_kernel_spmd as _run

    g = {k: _np.asarray(v) for k, v in inputs.items()}

    def by_dim(m):
        return m.reshape(*m.shape[:-1], CHUNKS, P // HD, HD).swapaxes(-1, -2).reshape(m.shape)

    kv = g["L0_attn_Wkv"]
    wqkv = g["L1_attn_w_qkv"].T
    slopes = (4.0 * 2.0 ** (-0.25 * _np.arange(1, HEADS + 1))).astype(_np.float32)
    hi = (slopes.view(_np.uint32) & _np.uint32(0xFFFFF000)).view(_np.float32)
    pos = _np.arange(SEQ, dtype=_np.float32)
    laid = {
        "x": g["L0_attn_hidden_states"],
        "ar0": _np.concatenate([g["L0_ffn_A"].reshape(E0 * R0, D).T, g["L0_ffn_route_w"].T], axis=1),
        "b0": g["L0_ffn_Bw"].transpose(0, 2, 1).reshape(E0 * R0, D),
        "wq0": by_dim(g["L0_attn_Wq"]),
        "wk0": _np.concatenate([kv[:, :HD]] * 3, axis=1),
        "wv0": kv[:, HD:],
        "wo0": g["L0_attn_Wo"],
        "wqk1": _np.concatenate([by_dim(wqkv[:, :D]), by_dim(wqkv[:, D:2 * D])], axis=1),
        "wv1": wqkv[:, 2 * D:],
        "wo1": g["L1_attn_w_out"].T,
        "bqk1": _np.concatenate([by_dim(g["L1_attn_b_qkv"][:D]), by_dim(g["L1_attn_b_qkv"][D:2 * D])]).reshape(2 * CHUNKS, P).T,
        "bv1": g["L1_attn_b_qkv"][2 * D:],
        "bo1": g["L1_attn_b_out"],
        "base": g["L1_ffn_W_base"].T,
        "b_base": g["L1_ffn_b_base"],
        "lora_a": g["L1_ffn_lora_A"].reshape(E1 * R1, D),
        "lora_b": g["L1_ffn_lora_B"].transpose(0, 2, 1).reshape(E1 * R1, D),
        "router_w": g["L1_ffn_router_W"],
        "router_b": g["L1_ffn_router_b"],
        "prior": g["L1_ffn_domain_prior"],
        "active": g["L1_ffn_active"],
        "slopes": _np.stack([hi, slopes - hi]),
        "key_rows": _np.stack([pos, pos, pos * 0 + 1, pos * 0 + 1]),
    }
    nc = _bacc.Bacc("TRN2", target_bir_lowering=False, num_devices=1)
    arrays, aps = {}, {}
    for name, a in laid.items():
        a = _np.ascontiguousarray(a)
        arrays[f"in_{name}"] = a
        aps[name] = nc.dram_tensor(f"in_{name}", a.shape, _mybir.dt.from_np(a.dtype), kind="ExternalInput").ap()
    out = nc.dram_tensor("out_x", (BATCH, SEQ, D), F32, kind="ExternalOutput").ap()
    macaron(nc, aps.pop("x"), aps, out, stages)
    r = _run(nc, [arrays], core_ids=[0])
    return r.results[0]["out_x"]
```

```python
from contextlib import ExitStack

import numpy as np

import concourse.bass as bass
from concourse import mybir

F32 = mybir.dt.float32
F32R = mybir.dt.float32r
BF16 = mybir.dt.bfloat16
I32 = mybir.dt.int32
U32 = mybir.dt.uint32
ALU = mybir.AluOpType
ACT = mybir.ActivationFunctionType
AX = mybir.AxisListType

P = 128
BATCH, SEQ, D = 4, 512, 512
TOKENS = BATCH * SEQ
KC = D // P
QT = SEQ // P
HEADS, HD = 32, 16
E0, R0 = 8, 16
E1, A1, R1 = 16, 4, 8
Z1 = A1 * R1
EPS = 1e-5
MASKED = -1e30
SCORE_SCALE = HD ** -0.5
RSQRT_MAGIC = 1597463007.0

UH = 4
UNITS = HEADS // UH
CHUNKS = HEADS * HD // P
STACKS = 3
PART0 = 2
MAX0 = P - 2


ONE, DMA_ONE = 1, 16


def twice(b, t):
    return b * QT + max(t - 1, 0)


class LayerNorm:

    STEPS = QT + 7 + 1 + 9

    def __init__(self, dve, x, xhat, small, nb, sem, base):
        self.dve, self.x, self.xhat, self.nb, self.sem, self.base = dve, x, xhat, nb, sem, base
        self.stats, self.mean, self.var, self.y, self.a = small

    def statistics(self, t):
        self.dve.bn_stats(self.stats[:, t, :], self.x[:, self.nb * QT + t, :]).then_inc(self.sem, 1)

    def scales(self):
        dve, sem, base, stats = self.dve, self.sem, self.base, self.stats
        mean, var, y, a = self.mean, self.var, self.y, self.a
        n = QT
        dve.wait_ge(sem, base + n)
        dve.tensor_tensor(mean[:], stats[:, :, 1], stats[:, :, 4], ALU.add).then_inc(sem, 1)
        dve.tensor_tensor(a[:], stats[:, :, 1], stats[:, :, 4], ALU.subtract).then_inc(sem, 1)
        dve.tensor_tensor(var[:], stats[:, :, 2], stats[:, :, 5], ALU.add).then_inc(sem, 1)
        dve.wait_ge(sem, base + n + 3)
        dve.tensor_scalar(mean[:], mean[:], 0.5, None, ALU.mult).then_inc(sem, 1)
        dve.tensor_tensor(a[:], a[:], a[:], ALU.mult).then_inc(sem, 1)
        dve.tensor_scalar(var[:], var[:], 1.0 / D, EPS, ALU.mult, ALU.add).then_inc(sem, 1)
        dve.wait_ge(sem, base + n + 6)
        dve.scalar_tensor_tensor(var[:], a[:], 0.25, var[:], ALU.mult, ALU.add).then_inc(sem, 1)
        n += 7
        dve.wait_ge(sem, base + n)
        dve.tensor_scalar(y[:].bitcast(I32), var[:].bitcast(I32), -0.5, RSQRT_MAGIC, ALU.mult, ALU.add).then_inc(sem, 1)
        n += 1
        for _ in range(3):
            dve.wait_ge(sem, base + n)
            dve.tensor_tensor(a[:], y[:], y[:], ALU.mult).then_inc(sem, 1)
            dve.wait_ge(sem, base + n + 1)
            dve.scalar_tensor_tensor(a[:], a[:], -0.5, var[:], ALU.mult, ALU.mult).then_inc(sem, 1)
            dve.wait_ge(sem, base + n + 2)
            dve.scalar_tensor_tensor(y[:], a[:], 1.5, y[:], ALU.add, ALU.mult).then_inc(sem, 1)
            n += 3
        assert n == self.STEPS
        dve.wait_ge(sem, base + n)

    def rows(self, t, ready):
        self.dve.tensor_scalar(self.xhat[:, t, :], self.x[:, self.nb * QT + t, :], self.mean[:, t:t + 1],
                               self.y[:, t:t + 1], ALU.subtract, ALU.mult).then_inc(ready, 1)

    def whole(self, xhat_free, ready):
        for t in range(QT):
            self.statistics(t)
        self.scales()
        xhat_free()
        for t in range(QT):
            self.rows(t, ready)


def macaron(nc, x_in, w, out, stages=6):
    ctx = ExitStack()
    nsem = [0]

    def sb(name, shape, dt=F32, c=ctx):
        return c.enter_context(nc.sbuf_tensor(name, shape, dt))

    def ps(name, shape, dt=F32, c=ctx):
        return c.enter_context(nc.psum_tensor(name, shape, dt))

    def sem(name):
        nsem[0] += 1
        return ctx.enter_context(nc.semaphore(name))

    with ctx:
        x = sb("x", [P, TOKENS // P, D])
        xhat = sb("xhat", [P, QT, D])
        xT = sb("xT", [P, KC, SEQ])
        ident = sb("ident", [P, P])
        identb = sb("identb", [P, P], BF16)
        causal = sb("causal", [P, P], BF16)
        ln_small = (sb("ln_stats", [P, QT, 6]), sb("ln_mean", [P, QT]), sb("ln_ve", [P, QT]),
                    sb("ln_y", [P, QT]), sb("ln_a", [P, QT]))
        w_base = sb("w_base", [P, KC, D])
        w_z1 = sb("w_z1", [P, KC, Z1 + A1])
        w_b1 = sb("w_b1", [Z1, D])
        half_b = sb("half_b", [P, D])
        gate_b = sb("gate_b", [P, A1])
        causal_t = sb("causal_t", [P, P], BF16)
        Qs = [sb(f"Qs{i}", [P, UH, SEQ], F32R) for i in range(STACKS)]
        Ks = [sb(f"Ks{i}", [P, UH, SEQ], F32R) for i in range(STACKS)]
        spread_q = nc.dram_tensor("spread_q", (CHUNKS, 2 + 2 * HD, P // HD, SEQ), F32, kind="Internal").ap()
        got_consts, zeroed, rounded, keys_in, passed = (
            sem(n) for n in ("got_consts", "zeroed_stacks", "rounded", "keys_in", "passed"))

        got_x0, got_x, got_ffn0, got_att0, got_raw1, got_base1, got_att1 = (
            sem(n) for n in ("got_x0", "got_x", "got_ffn0", "got_att0", "got_raw1", "got_base1", "got_att1"))
        stored = sem("stored")
        x_rows = x_in.rearrange("b (t p) d -> p (b t) d", p=P)

        layer0 = ExitStack()
        w_ar0 = sb("w_ar0", [P, KC, E0 * R0 + E0], F32, layer0)
        w_b0 = sb("w_b0", [P, D], F32, layer0)
        number8 = sb("number8", [P, E0], F32, layer0)
        layer0a = ExitStack()
        w_q0 = sb("w_q0", [P, KC, D], F32, layer0a)
        w_k0 = sb("w_k0", [P, KC, 3 * HD], F32, layer0a)
        w_v0 = sb("w_v0", [P, KC, HD], F32, layer0a)
        w_o0 = sb("w_o0", [P, KC, D], F32, layer0a)

        with ExitStack() as c:
            act_i = sb("act_i", [P, A1], I32, c)
            act_f = sb("act_f", [P, A1], F32, c)
            act_n = sb("act_n", [P, A1], F32, c)
            row_i = sb("row_i", [P, R1 + 2], I32, c)
            row_f = sb("row_f", [P, R1 + 2], F32, c)
            row_e = sb("row_e", [P, 1], I32, c)
            row_r = sb("row_r", [P, 1], I32, c)
            rank_i = sb("rank_i", [P, R1], I32, c)
            rank_f = sb("rank_f", [P, R1], F32, c)
            iota_i = sb("iota_i", [P, E0], I32, c)
            part_i = sb("part_i", [P, 1], I32, c)
            part_f = sb("part_f", [P, 1], F32, c)
            sel_e = sb("sel_e", [P, A1], F32, c)
            sel_r = sb("sel_r", [P, R1], F32, c)
            sel_er = sb("sel_er", [P, A1, R1], F32, c)
            sel_e16 = sb("sel_e16", [E1, A1], F32, c)
            lora_a = sb("lora_a", [P, D], F32, c)
            lora_b = sb("lora_b", [P, D], F32, c)
            rout = sb("rout", [E1, D], F32, c)
            rb = sb("rb", [E1, 1], F32, c)
            prior = sb("prior", [E1, 1], F32, c)
            lprior = sb("lprior", [E1, 1], F32, c)
            bias_bc = sb("bias_bc", [E1, P], F32, c)
            ones16 = sb("ones16", [E1, P], F32, c)
            pg = ps("pg", [P, KC, 512], F32, c)
            pb = ps("pb", [P, 512], F32, c)
            pl = ps("pl", [P, 512], F32, c)
            consts, iotas, zeroed_masks = sem("consts"), sem("iotas"), sem("zeroed_masks")
            s_dve, s_ln, s_act = sem("s_dve"), sem("s_ln"), sem("s_act")
            picked, xhat_ready = sem("picked"), sem("xhat_ready0")

            with nc.Block() as block:
                @block.sync
                def _(sp):
                    for t in range(QT):
                        sp.dma_start(x[:, t, :], x_rows[:, t, :]).then_inc(got_x0, 16)
                    sp.dma_start(w_ar0[:], w["ar0"].rearrange("(c p) m -> p c m", p=P)).then_inc(got_ffn0, 16)
                    sp.dma_start(w_b0[:], w["b0"]).then_inc(got_ffn0, 16)
                    sp.dma_start(act_i[:], w["active"].partition_broadcast(P)).then_inc(got_raw1, 16)
                    sp.dma_start(lora_a[:], w["lora_a"]).then_inc(got_raw1, 16)
                    sp.dma_start(lora_b[:], w["lora_b"]).then_inc(got_raw1, 16)
                    sp.dma_start(rout[:], w["router_w"]).then_inc(got_raw1, 16)
                    sp.dma_start(rb[:], w["router_b"].rearrange("(e a) -> e a", a=1)).then_inc(got_raw1, 16)
                    sp.dma_start(prior[:], w["prior"].rearrange("(e a) -> e a", a=1)).then_inc(got_raw1, 16)
                    sp.dma_start(half_b[:], w["b_base"].partition_broadcast(P)).then_inc(got_raw1, 16)
                    for b in range(1, BATCH):
                        sp.dma_start(x[:, b * QT:(b + 1) * QT, :], x_rows[:, b * QT:(b + 1) * QT, :]).then_inc(got_x, 16)
                    for dst, src in ((w_q0, "wq0"), (w_k0, "wk0"), (w_v0, "wv0"), (w_o0, "wo0")):
                        sp.dma_start(dst[:], w[src].rearrange("(c p) m -> p c m", p=P)).then_inc(got_att0, 16)
                    sp.dma_start(w_base[:], w["base"].rearrange("(c p) m -> p c m", p=P)).then_inc(got_base1, 16)

                @block.gpsimd
                def _(pool):
                    pool.memset(ident[:], 0.0).then_inc(zeroed_masks, 1)
                    pool.memset(identb[:], 0.0).then_inc(zeroed_masks, 1)
                    pool.memset(causal[:], 0.0).then_inc(zeroed_masks, 1)
                    pool.memset(causal_t[:], 0.0).then_inc(zeroed_masks, 1)
                    pool.iota(part_i[:], [[0, 1]], base=0, channel_multiplier=1).then_inc(iotas, 1)
                    pool.iota(rank_i[:], [[1, R1]], base=0, channel_multiplier=0).then_inc(iotas, 1)
                    pool.iota(iota_i[:], [[1, E0]], base=0, channel_multiplier=0).then_inc(iotas, 1)
                    pool.wait_ge(zeroed_masks, 4)
                    for m in (ident, identb):
                        pool.affine_select(out=m[:], in_=m[:], compare_op=ALU.not_equal, fill=1.0, base=0,
                                           pattern=[[-1, P]], channel_multiplier=1).then_inc(consts, 1)
                    pool.affine_select(out=causal[:], in_=causal[:], compare_op=ALU.is_ge, fill=MASKED, base=0,
                                       pattern=[[-1, P]], channel_multiplier=1).then_inc(consts, 1)
                    pool.affine_select(out=causal_t[:], in_=causal_t[:], compare_op=ALU.is_ge, fill=MASKED, base=0,
                                       pattern=[[1, P]], channel_multiplier=-1).then_inc(consts, 1)
                    pool.memset(ones16[:], 1.0).then_inc(consts, 1)

                @block.scalar
                def _(act):
                    act.wait_ge(s_dve, 1)
                    act.activation(lprior[:], prior[:], ACT.Ln).then_inc(s_act, 1)
                    act.wait_ge(picked, 1)
                    act.copy(w_z1[:], pg[:, :, 0:Z1 + A1]).then_inc(s_act, 1)
                    act.wait_ge(picked, 2)
                    act.copy(w_b1[:], pb[0:Z1, :]).then_inc(s_act, 1)
                    act.wait_ge(picked, 3)
                    act.copy(gate_b[:], pl[:, 0:A1]).then_inc(s_act, 1)

                @block.vector
                def _(dve):
                    k = 0

                    def step(ins):
                        nonlocal k
                        ins.then_inc(s_dve, 1)
                        k += 1
                        dve.wait_ge(s_dve, k)

                    dve.wait_ge(got_raw1, 7 * 16)
                    step(dve.tensor_scalar(prior[:], prior[:], 1e-12, None, ALU.add))
                    step(dve.tensor_copy(act_f[:], act_i[:]))
                    step(dve.tensor_scalar(act_n[:], act_f[:], 0.0, float(E1), ALU.is_lt, ALU.mult))
                    step(dve.tensor_tensor(act_f[:], act_f[:], act_n[:], ALU.add))
                    dve.wait_ge(iotas, 3)
                    step(dve.tensor_scalar(row_e[:], part_i[:], 3, None, ALU.logical_shift_right))
                    step(dve.tensor_scalar(row_r[:], part_i[:], R1 - 1, None, ALU.bitwise_and))
                    step(dve.tensor_copy(row_f[:, 0:1], row_e[:]))
                    step(dve.tensor_copy(row_f[:, 1:2], row_r[:]))
                    step(dve.tensor_copy(part_f[:], part_i[:]))
                    step(dve.tensor_copy(rank_f[:], rank_i[:]))
                    step(dve.tensor_scalar(number8[:], iota_i[:], float(-E0), None, ALU.add))
                    step(dve.tensor_scalar(sel_e[:], act_f[:], row_f[:, 0:1], None, ALU.is_equal))
                    step(dve.tensor_scalar(sel_r[:], rank_f[:], row_f[:, 1:2], None, ALU.is_equal))
                    step(dve.tensor_tensor(sel_er[:], sel_e[:].unsqueeze(2).broadcast_to([P, A1, R1]),
                                           sel_r[:].unsqueeze(1).broadcast_to([P, A1, R1]), ALU.mult))
                    step(dve.tensor_scalar(sel_e16[:], act_f[0:E1, :], part_f[0:E1, :], None, ALU.is_equal))
                    dve.wait_ge(s_act, 1)
                    step(dve.tensor_tensor(rb[:], rb[:], lprior[:], ALU.add))
                    dve.wait_ge(consts, 5)
                    step(dve.tensor_scalar(bias_bc[:], ones16[:], rb[:, 0:1], None, ALU.mult))
                    step(dve.tensor_scalar(half_b[:], half_b[:], 0.5, None, ALU.mult))
                    dve.wait_ge(got_x0, QT * 16)
                    LayerNorm(dve, x, xhat, ln_small, 0, s_ln, 0).whole(lambda: None, xhat_ready)

                @block.tensor
                def _(pe):
                    pe.wait_ge(s_dve, 17)
                    for k in range(KC):
                        last = pe.matmul(pg[:, k, 0:Z1], lora_a[:, k * P:(k + 1) * P], sel_er[:].rearrange("p a r -> p (a r)"),
                                         start=True, stop=True)
                        last = pe.matmul(pg[:, k, Z1:Z1 + A1], rout[:, k * P:(k + 1) * P], sel_e16[:],
                                         start=True, stop=True)
                    last.then_inc(picked, 1)
                    pe.matmul(pb[0:Z1, :], sel_er[:].rearrange("p a r -> p (a r)"), lora_b[:],
                              start=True, stop=True).then_inc(picked, 1)
                    pe.matmul(pl[:, 0:A1], bias_bc[:], sel_e16[:], start=True, stop=True).then_inc(picked, 1)

        def transposes(pe, b, pT, ready, done):
            for t in range(QT):
                if t == 0:
                    pe.wait_ge(done, ONE + b * QT)
                elif t > 1:
                    pe.wait_ge(done, ONE + b * QT + t - 1)
                for k in range(KC):
                    last = pe.transpose(pT[t % 2][:, k * P:(k + 1) * P], xhat[:, t, k * P:(k + 1) * P], ident[:])
                last.then_inc(ready, 1)

        def ffn0(tag, first):
            with ExitStack() as c:
                mx = sb(tag + "mx", [P, 2], F32, c)
                hit = sb(tag + "hit", [P, 2, E0], F32, c)
                pick = sb(tag + "pick", [P, 2], F32, c)
                gate = sb(tag + "gate", [P, 2, E0], F32, c)
                if first:
                    key_rows = sb("key_rows", [4, SEQ], F32, c)
                    key_rows_r = sb("key_rows_r", [4, SEQ], F32R, c)
                wh = sb(tag + "wh", [P, 2, E0 * R0], F32, c)
                whT = sb(tag + "whT", [P, 2, P], F32, c)
                pT = [ps(f"{tag}pT{i}", [P, 512], F32, c) for i in range(2)]
                pH = [ps(f"{tag}pH{i}", [P, 512], F32, c) for i in range(2)]
                pW = [ps(f"{tag}pW{i}", [P, 512], F32, c) for i in range(2)]
                pY = [ps(f"{tag}pY{i}", [P, 512], F32, c) for i in range(2)]
                xt_ready, xt_done, h_ready, wh_done, wt_ready, wt_done, y_ready, x_done = (
                    sem(tag + n) for n in ("xt_ready", "xt_done", "h_ready", "wh_done", "wt_ready", "wt_done",
                                           "y_ready", "x_done"))
                xhat_ready, s_ln, s_gate = sem(tag + "xhat"), sem(tag + "s_ln"), sem(tag + "s_gate")

                with nc.Block() as block:
                    if first:
                        @block.gpsimd
                        def _(pool):
                            for m in Ks + Qs:
                                pool.memset(m[:].bitcast(F32), 0.0).then_inc(zeroed, 1)
                            pool.wait_ge(got_consts, 32)
                            pool.wait_ge(zeroed, 2 * STACKS)
                            pool.tensor_copy(key_rows_r[:], key_rows[:]).then_inc(rounded, 1)

                        @block.sync
                        def _(sp):
                            sp.dma_start(key_rows[:], w["key_rows"]).then_inc(got_consts, 16)
                            sp.dma_start(spread_q[:, 0:2, :, :], w["slopes"]).then_inc(got_consts, 16)
                            sp.wait_ge(zeroed, 2 * STACKS)
                            sp.wait_ge(rounded, 1)
                            for m in Ks:
                                for row, at in ((0, 0), (2, MAX0)):
                                    for j in range(UH):
                                        sp.dma_start(m[at:at + 2, j, :].bitcast(F32),
                                                     key_rows_r[row:row + 2, :].bitcast(F32)).then_inc(keys_in, 16)
                            sp.wait_ge(keys_in, 2 * UH * STACKS * 16)

                    @block.tensor
                    def _(pe):
                        if first:
                            pe.wait_ge(got_ffn0, 2 * 16)
                        for s in (h_ready, wt_ready, y_ready,):
                            pe.sem_inc(s, ONE)
                        with pe.Fori(0, BATCH) as b:
                            pe.wait_ge(xhat_ready, ONE + b * QT)
                            transposes(pe, b, pT, xt_ready, xt_done)

                            def up(t):
                                pe.wait_ge(xt_done, ONE + b * QT + t + 1)
                                pe.wait_ge(wh_done, ONE + twice(b, t))
                                for k in range(KC):
                                    last = pe.matmul(pH[t % 2][:, 0:E0 * R0 + E0], xT[:, k, t * P:(t + 1) * P],
                                                     w_ar0[:, k, :], start=(k == 0), stop=(k == KC - 1))
                                last.then_inc(h_ready, 1)

                            def down(t):
                                pe.wait_ge(wh_done, ONE + b * QT + t + 1)
                                pe.wait_ge(wt_done, ONE + twice(b, t))
                                pe.transpose(pW[t % 2][:, 0:P], wh[:, t % 2, :], ident[:]).then_inc(wt_ready, 1)
                                pe.wait_ge(wt_done, ONE + b * QT + t + 1)
                                pe.wait_ge(x_done, ONE + twice(b, t))
                                pe.matmul(pY[t % 2][:], whT[:, t % 2, :], w_b0[:], start=True, stop=True).then_inc(y_ready, 1)

                            up(0)
                            for t in range(1, QT):
                                up(t)
                                down(t - 1)
                            down(QT - 1)

                    @block.scalar
                    def _(act):
                        for s in (xt_done, wt_done,):
                            act.sem_inc(s, ONE)
                        with act.Fori(0, BATCH) as b:
                            for t in range(QT):
                                act.wait_ge(xt_ready, b * QT + t + 1)
                                if t == 0:
                                    act.wait_ge(h_ready, ONE + b * QT)
                                act.copy(xT[:, :, t * P:(t + 1) * P],
                                         pT[t % 2][:].rearrange("p (k q) -> p k q", k=KC)).then_inc(xt_done, 1)
                            for t in range(QT):
                                act.wait_ge(wt_ready, ONE + b * QT + t + 1)
                                act.wait_ge(y_ready, ONE + twice(b, t))
                                act.copy(whT[:, t % 2, :], pW[t % 2][:, 0:P]).then_inc(wt_done, 1)

                    @block.vector
                    def _(dve):
                        if first:
                            dve.wait_ge(got_x, (BATCH - 1) * 16)
                        for s in (xhat_ready, wh_done, x_done,):
                            dve.sem_inc(s, ONE)
                        with dve.Fori(0, BATCH) as b:
                            def xhat_free():
                                dve.wait_ge(xt_ready, (b + 1) * QT)

                            dve.wait_ge(x_done, ONE + b * QT)
                            LayerNorm(dve, x, xhat, ln_small, (b + 1) % BATCH, s_ln, b * LayerNorm.STEPS).whole(xhat_free, xhat_ready)

                            def route(t):
                                i, n = t % 2, b * QT * 4 + t * 4
                                dve.wait_ge(h_ready, ONE + b * QT + t + 1)
                                logits = pH[i][:, E0 * R0:E0 * R0 + E0]
                                dve.tensor_reduce(mx[:, i:i + 1], logits, AX.X, ALU.max).then_inc(s_gate, 1)
                                dve.wait_ge(s_gate, n + 1)
                                dve.scalar_tensor_tensor(hit[:, i, :], logits, mx[:, i:i + 1], number8[:],
                                                         ALU.is_ge, ALU.mult).then_inc(s_gate, 1)
                                dve.wait_ge(s_gate, n + 2)
                                dve.tensor_reduce(pick[:, i:i + 1], hit[:, i, :], AX.X, ALU.min).then_inc(s_gate, 1)
                                dve.wait_ge(s_gate, n + 3)
                                dve.tensor_scalar(gate[:, i, :], number8[:], pick[:, i:i + 1], mx[:, i:i + 1],
                                                  ALU.is_equal, ALU.mult).then_inc(s_gate, 1)
                                dve.wait_ge(s_gate, n + 4)
                                dve.wait_ge(wt_ready, ONE + twice(b, t))
                                dve.tensor_tensor(wh[:, i, :].rearrange("p (e r) -> p e r", e=E0),
                                                  pH[i][:, 0:E0 * R0].rearrange("p (e r) -> p e r", e=E0),
                                                  gate[:, i, :].unsqueeze(2).broadcast_to([P, E0, R0]),
                                                  ALU.mult).then_inc(wh_done, 1)

                            def residual(t):
                                dve.wait_ge(y_ready, ONE + b * QT + t + 1)
                                xt = x[:, b * QT + t, :]
                                dve.scalar_tensor_tensor(xt, pY[t % 2][:], 0.5, xt, ALU.mult, ALU.add).then_inc(x_done, 1)

                            route(0)
                            for t in range(1, QT):
                                route(t)
                                residual(t - 1)
                            residual(QT - 1)

        def ffn1(tag, first, last_stage, prefetch):
            with ExitStack() as c:
                lg = sb(tag + "lg", [P, 2, A1], F32, c)
                nm = sb(tag + "nm", [P, 2], F32, c)
                ex = sb(tag + "ex", [P, 2, A1], F32, c)
                sm = sb(tag + "sm", [P, 2], F32, c)
                rs = sb(tag + "rs", [P, 2], F32, c)
                al = sb(tag + "al", [P, 2, A1], F32, c)
                wz = sb(tag + "wz", [P, 2, Z1], F32, c)
                wzT = sb(tag + "wzT", [Z1, 2, P], F32, c)
                pT = [ps(f"{tag}pT{i}", [P, 512], F32, c) for i in range(2)]
                pZ = [ps(f"{tag}pZ{i}", [P, 512], F32, c) for i in range(2)]
                pW = [ps(f"{tag}pW{i}", [P, 512], F32, c) for i in range(2)]
                pY = [ps(f"{tag}pY{i}", [P, 512], F32, c) for i in range(2)]
                xt_ready, xt_done, z_ready, lg_done, ex_done, wz_done, wt_ready, wt_done, y_ready, x_done = (
                    sem(tag + n) for n in ("xt_ready", "xt_done", "z_ready", "lg_done", "ex_done", "wz_done",
                                           "wt_ready", "wt_done", "y_ready", "x_done"))
                xhat_ready, s_ln, s_gate, s_res = sem(tag + "xhat"), sem(tag + "s_ln"), sem(tag + "s_gate"), sem(tag + "s_res")

                with nc.Block() as block:
                    @block.tensor
                    def _(pe):
                        if first:
                            pe.wait_ge(got_base1, 16)
                        for s in (wt_ready, y_ready,):
                            pe.sem_inc(s, ONE)
                        with pe.Fori(0, BATCH) as b:
                            pe.wait_ge(xhat_ready, ONE + b * QT)
                            transposes(pe, b, pT, xt_ready, xt_done)

                            def low_rank(t):
                                pe.wait_ge(xt_done, ONE + b * QT + t + 1)
                                pe.wait_ge(wz_done, ONE + twice(b, t))
                                for k in range(KC):
                                    last = pe.matmul(pZ[t % 2][:, 0:Z1 + A1], xT[:, k, t * P:(t + 1) * P],
                                                     w_z1[:, k, :], start=(k == 0), stop=(k == KC - 1))
                                last.then_inc(z_ready, 1)

                            def base(t):
                                pe.wait_ge(x_done, ONE + twice(b, t))
                                for k in range(KC):
                                    pe.matmul(pY[t % 2][:], xT[:, k, t * P:(t + 1) * P], w_base[:, k, :],
                                              start=(k == 0), stop=False)

                            def experts(t):
                                pe.wait_ge(wz_done, ONE + b * QT + t + 1)
                                pe.wait_ge(wt_done, ONE + twice(b, t))
                                pe.transpose(pW[t % 2][0:Z1, 0:P], wz[:, t % 2, :], ident[:]).then_inc(wt_ready, 1)
                                pe.wait_ge(wt_done, ONE + b * QT + t + 1)
                                pe.matmul(pY[t % 2][:], wzT[:, t % 2, :], w_b1[:], start=False, stop=True).then_inc(y_ready, 1)

                            low_rank(0)
                            for t in range(QT):
                                base(t)
                                if t + 1 < QT:
                                    low_rank(t + 1)
                                experts(t)

                    @block.scalar
                    def _(act):
                        for s in (xt_done, wt_done,):
                            act.sem_inc(s, ONE)
                        with act.Fori(0, BATCH) as b:
                            for t in range(QT):
                                act.wait_ge(xt_ready, b * QT + t + 1)
                                if t == 0:
                                    act.wait_ge(y_ready, ONE + b * QT)
                                act.copy(xT[:, :, t * P:(t + 1) * P],
                                         pT[t % 2][:].rearrange("p (k q) -> p k q", k=KC)).then_inc(xt_done, 1)
                            for t in range(QT):
                                i = t % 2
                                act.wait_ge(lg_done, b * QT + t + 1)
                                act.activation(ex[:, i, :], lg[:, i, :], ACT.Exp, bias=nm[:, i:i + 1],
                                               accum_out=sm[:, i:i + 1]).then_inc(ex_done, 1)
                                act.wait_ge(wt_ready, ONE + b * QT + t + 1)
                                act.wait_ge(y_ready, ONE + twice(b, t))
                                act.copy(wzT[:, i, :], pW[i][0:Z1, 0:P]).then_inc(wt_done, 1)

                    @block.vector
                    def _(dve):
                        for s in (xhat_ready, wz_done, x_done,):
                            dve.sem_inc(s, ONE)
                        with dve.Fori(0, BATCH) as b:
                            def xhat_free():
                                dve.wait_ge(xt_ready, (b + 1) * QT)

                            dve.wait_ge(x_done, ONE + b * QT)
                            LayerNorm(dve, x, xhat, ln_small, (b + 1) % BATCH, s_ln, b * LayerNorm.STEPS).whole(xhat_free, xhat_ready)

                            def gate(t):
                                i, n = t % 2, b * QT * 3 + t * 3
                                dve.wait_ge(z_ready, b * QT + t + 1)
                                dve.tensor_tensor(lg[:, i, :], pZ[i][:, Z1:Z1 + A1], gate_b[:], ALU.add).then_inc(s_gate, 1)
                                dve.wait_ge(s_gate, n + 1)
                                dve.tensor_reduce(nm[:, i:i + 1], lg[:, i, :], AX.X, ALU.max, negate=True).then_inc(lg_done, 1)
                                dve.wait_ge(ex_done, b * QT + t + 1)
                                dve.reciprocal(rs[:, i:i + 1], sm[:, i:i + 1]).then_inc(s_gate, 1)
                                dve.wait_ge(s_gate, n + 2)
                                dve.tensor_scalar(al[:, i, :], ex[:, i, :], rs[:, i:i + 1], 2.0, ALU.mult, ALU.mult).then_inc(s_gate, 1)
                                dve.wait_ge(s_gate, n + 3)
                                dve.wait_ge(wt_ready, ONE + twice(b, t))
                                dve.tensor_tensor(wz[:, i, :].rearrange("p (a r) -> p a r", a=A1),
                                                  pZ[i][:, 0:Z1].rearrange("p (a r) -> p a r", a=A1),
                                                  al[:, i, :].unsqueeze(2).broadcast_to([P, A1, R1]),
                                                  ALU.mult).then_inc(wz_done, 1)

                            def residual(t):
                                dve.wait_ge(y_ready, ONE + b * QT + t + 1)
                                xt = x[:, b * QT + t, :]
                                dve.scalar_tensor_tensor(xt, pY[t % 2][:], 0.5, xt, ALU.mult, ALU.add).then_inc(s_res, 1)
                                dve.wait_ge(s_res, b * QT + t + 1)
                                dve.tensor_tensor(xt, xt, half_b[:], ALU.add).then_inc(x_done, 1)

                            gate(0)
                            for t in range(1, QT):
                                gate(t)
                                residual(t - 1)
                            residual(QT - 1)

                    @block.sync
                    def _(sp):
                        if prefetch is not None:
                            prefetch(sp)
                        if last_stage:
                            out_rows = out.rearrange("b (t p) d -> p (b t) d", p=P)
                            with sp.Fori(0, TOKENS // P) as i:
                                sp.wait_ge(x_done, ONE + i + 1)
                                sp.dma_start(out_rows[:, bass.ds(i, 1), :], x[:, bass.ds(i, 1), :]).then_inc(stored, 16)
                            sp.wait_ge(stored, TOKENS // P * 16)

        def attention(tag, w_q, w_k, w_v, w_o, own_k, got_weights, n_weights, b_qk, b_v, b_o):
            GROUPS = [(0, (0, 1, 2, 3)), (1, (0, 1)), (1, (2, 3))] + [(qt, (j,)) for qt in (2, 3) for j in range(UH)]
            HALF = 5

            def groups(n, lo, hi):
                return [("A", n, g) for g in range(lo, hi)] if n < UNITS else []

            def projected(c):
                return [("Q", c)] + ([("K", c)] if own_k else [])

            items = [("T", t) for t in range(QT)]
            if not own_k:
                items += [("K", 0)]
            items += projected(0) + [("V", t) for t in (range(QT) if own_k else (0,))] + projected(1)
            items += groups(0, 0, len(GROUPS)) + [("M", 0)] + groups(1, 0, HALF)
            for n in range(UNITS):
                if n % 2 == 0 and n // 2 + 2 < CHUNKS:
                    items += projected(n // 2 + 2)
                if n + 1 < UNITS:
                    items += groups(n + 1, HALF, len(GROUPS)) + [("M", n + 1)] + groups(n + 2, 0, HALF)
            at = {item: i for i, item in enumerate(items)}
            by_dve = [item for item in items if item[0] not in "TM"]
            dve_at = {item: i for i, item in enumerate(by_dve)}
            N, ND = len(items), len(by_dve)
            splits = [item for item in items if item[0] in "QK"]
            split_at = {item: i for i, item in enumerate(splits)}
            NS = len(splits)
            LOADS = 4 if own_k else 2
            PARTS = 4 if own_k else 2
            SPREADS = PARTS // 2
            PAIRS = QT * UH // 2
            uses = [len(range(s, UNITS, STACKS)) for s in range(STACKS)]

            with ExitStack() as c:
                if own_k:
                    vv = sb(tag + "vv", [P, QT, HEADS, HD, 2], F32, c)
                else:
                    k_all = Ks[0][:, 0, :]
                    k_first = sb(tag + "k_first", [3 * HD, 1, SEQ], F32R, c)
                    vv = sb(tag + "vv", [P, QT, HD, 2], F32, c)
                parts = sb(tag + "parts", [P, PARTS, SEQ], F32R, c)
                if own_k:
                    spread_k = nc.dram_tensor(tag + "spread_k", (CHUNKS, 2 * HD, P // HD, SEQ), F32, kind="Internal").ap()
                probs = [sb(f"{tag}probs{i}", [P, UH, SEQ - i * P], F32, c) for i in range(2)]
                o_raw = sb(tag + "o_raw", [P, 2, SEQ], F32, c)
                oT = sb(tag + "oT", [P, CHUNKS, SEQ], F32, c)
                den = sb(tag + "den", [P, SEQ], F32, c)
                sums = sb(tag + "sums", [P, 2, SEQ // HD], F32, c)
                inv_dram = nc.dram_tensor(tag + "inv", (CHUNKS, P // HD, SEQ), F32, kind="Internal").ap()
                neg_max = sb(tag + "neg_max", [P, QT, UH], F32, c)
                nm_parts = sb(tag + "nm_parts", [P, QT, 2, UH], F32R, c)
                nm_rows = sb(tag + "nm_rows", [2 * UH, SEQ], F32R, c)
                bank = [ps(f"{tag}bank{i}", [P, 512], F32, c) for i in range(3)]
                pS = [ps(f"{tag}pS{i}", [P, 2, 512], F32, c) for i in range(2)]
                pO = ps(tag + "pO", [P, 512], F32, c)

                ready, xt_done, bank_read, hi_done = (sem(tag + n) for n in ("ready", "xt_done", "bank_read", "hi_done"))
                s_ready, exp_done, pv_done, o_done, ones_in, max_split, s_split, max_rows_out, w_ready, x_done = (
                    sem(tag + n) for n in ("s_ready", "exp_done", "pv_done", "o_done", "ones_in", "max_split", "s_split",
                                           "max_rows_out", "w_ready", "x_done"))
                spread_out = sem(tag + "spread_out")
                loaded = [sem(f"{tag}loaded{i}") for i in range(STACKS)]
                max_in = sem(tag + "max_in")
                packed = [sem(f"{tag}packed{i}") for i in range(2)]
                inverted, inv_out, inv_in, norm_done, s_res = (
                    sem(tag + n) for n in ("inverted", "inv_out", "inv_in", "norm_done", "s_res"))
                xhat_ready, s_ln, key_parts_in = sem(tag + "xhat"), sem(tag + "s_ln"), sem(tag + "key_parts_in")

                def psum_of(item):
                    return bank[at[item] % 3]

                def item_ready(eng, b, item):
                    eng.wait_ge(ready, b * N + at[item] + 1)

                def item_read(eng, b, item):
                    if item[0] == "T":
                        eng.wait_ge(xt_done, b * QT + item[1] + 1)
                    elif item[0] == "M":
                        eng.wait_ge(max_rows_out, b * UNITS + item[1] + 1)
                    else:
                        eng.wait_ge(bank_read, ONE + b * ND + dve_at[item] + 1)

                def bank_free(pe, b, item):
                    if at[item] >= 3:
                        item_read(pe, b, items[at[item] - 3])
                    elif at[item] == 0:
                        pe.wait_ge(bank_read, ONE + b * ND)

                def stack_free(eng, b, n):
                    eng.wait_ge(s_ready, ONE + b * UNITS * PAIRS + max(n - STACKS + 1, 0) * PAIRS)

                def stack_loaded(eng, b, n):
                    eng.wait_ge(loaded[n % STACKS], (b * uses[n % STACKS] + n // STACKS + 1) * LOADS * 16)

                def keys(n, j, rows, cols):
                    return Ks[n % STACKS][0:rows, j, cols] if own_k else k_all[0:rows, cols]

                def part(kind, i):
                    return parts[:, i + (2 if kind == "K" else 0), :]

                with nc.Block() as block:
                    @block.tensor
                    def _(pe):
                        pe.wait_ge(got_weights, n_weights * 16)
                        for s in (s_ready, pv_done,):
                            pe.sem_inc(s, ONE)
                        with pe.Fori(0, BATCH) as b:
                            def project(kind, c, weights, cols):
                                item = (kind, c)
                                bank_free(pe, b, item)
                                m = weights[:, 0, cols].shape[-1]
                                for k in range(KC):
                                    last = pe.matmul(psum_of(item)[0:m, :], weights[:, k, cols], xT[:, k, :],
                                                     start=(k == 0), stop=(k == KC - 1))
                                last.then_inc(ready, 1)

                            def project_chunk(c):
                                project("Q", c, w_q, slice(c * P, (c + 1) * P))
                                if own_k:
                                    project("K", c, w_k, slice(c * P, (c + 1) * P))

                            def max_scores(n, lo, hi):
                                for g in range(lo, hi):
                                    if g == 0:
                                        if not own_k and n == 0:
                                            pe.wait_ge(key_parts_in, (b + 1) * 16)
                                        stack_loaded(pe, b, n)
                                    bank_free(pe, b, ("A", n, g))
                                    out_bank = psum_of(("A", n, g))
                                    qt, heads = GROUPS[g]
                                    width = (qt + 1) * P
                                    for i, j in enumerate(heads):
                                        pe.matmul(out_bank[:, i * width:(i + 1) * width],
                                                  Qs[n % STACKS][0:MAX0, j, qt * P:(qt + 1) * P],
                                                  keys(n, j, MAX0, slice(0, width)), start=True, stop=False)
                                        last = pe.matmul(out_bank[:, (i + 1) * width - P:(i + 1) * width],
                                                         identb[:], causal[:], start=False, stop=True)
                                    last.then_inc(ready, 1)

                            def max_rows(n):
                                pe.wait_ge(max_split, ONE + b * UNITS + n + 1)
                                bank_free(pe, b, ("M", n))
                                for qt in range(QT):
                                    last = pe.transpose(psum_of(("M", n))[0:2 * UH, qt * P:(qt + 1) * P],
                                                        nm_parts[:, qt].rearrange("p i h -> p (i h)").bitcast(F32), ident[:])
                                last.then_inc(ready, 1)

                            def scores(n, kt):
                                if kt == 0:
                                    pe.wait_ge(max_in, DMA_ONE + (b * UNITS + n + 1) * 16)
                                    if n == 0:
                                        pe.wait_ge(x_done, ONE + b * QT)
                                for p in range(2):
                                    i = n * PAIRS + kt * 2 + p
                                    pe.wait_ge(exp_done, ONE + b * UNITS * PAIRS + max(i - 1, 0))
                                    for j in range(2):
                                        pe.matmul(pS[p][:, j, 0:SEQ - kt * P],
                                                  keys(n, 2 * p + j, P, slice(kt * P, (kt + 1) * P)),
                                                  Qs[n % STACKS][:, 2 * p + j, kt * P:SEQ], start=True, stop=False)
                                        last = pe.matmul(pS[p][:, j, 0:P], identb[:], causal_t[:], start=False, stop=True)
                                    last.then_inc(s_ready, 1)

                            def values(n, kt):
                                pe.wait_ge(exp_done, ONE + b * UNITS * PAIRS + n * PAIRS + kt * 2 + 2)
                                if kt == 0:
                                    pe.wait_ge(o_done, ONE + b * UNITS + n)
                                for j in range(UH):
                                    v_tile = (vv[:, kt, n * UH + j] if own_k else vv[:, kt]).rearrange("p d s -> p (d s)")
                                    last = pe.matmul(pO[32 * j:32 * (j + 1), kt * P:SEQ], v_tile,
                                                     probs[kt % 2][:, j, 0:SEQ - kt * P],
                                                     start=(kt == 0), stop=(kt == QT - 1))
                                last.then_inc(pv_done, 1)

                            pe.wait_ge(xhat_ready, ONE + b * QT)
                            for t in range(QT):
                                bank_free(pe, b, ("T", t))
                                for k in range(KC):
                                    last = pe.transpose(psum_of(("T", t))[:, k * P:(k + 1) * P],
                                                        xhat[:, t, k * P:(k + 1) * P], ident[:])
                                last.then_inc(ready, 1)
                            item_read(pe, b, ("T", QT - 1))
                            if not own_k:
                                project("K", 0, w_k, slice(0, 3 * HD))
                            project_chunk(0)
                            if own_k:
                                for t in range(QT):
                                    bank_free(pe, b, ("V", t))
                                    for k in range(KC):
                                        last = pe.matmul(psum_of(("V", t))[:], xT[:, k, t * P:(t + 1) * P], w_v[:, k, :],
                                                         start=(k == 0), stop=(k == KC - 1))
                                    last.then_inc(ready, 1)
                            else:
                                bank_free(pe, b, ("V", 0))
                                for t in range(QT):
                                    for k in range(KC):
                                        last = pe.matmul(psum_of(("V", 0))[:, t * HD:(t + 1) * HD],
                                                         xT[:, k, t * P:(t + 1) * P], w_v[:, k, :],
                                                         start=(k == 0), stop=(k == KC - 1))
                                last.then_inc(ready, 1)
                            project_chunk(1)
                            max_scores(0, 0, len(GROUPS))
                            max_rows(0)
                            max_scores(1, 0, HALF)
                            for n in range(UNITS):
                                scores(n, 0)
                                if n % 2 == 0 and n // 2 + 2 < CHUNKS:
                                    project_chunk(n // 2 + 2)
                                if n + 1 < UNITS:
                                    max_scores(n + 1, HALF, HALF + 3)
                                scores(n, 1)
                                if n + 1 < UNITS:
                                    max_scores(n + 1, HALF + 3, len(GROUPS))
                                values(n, 0)
                                scores(n, 2)
                                if n + 1 < UNITS:
                                    max_rows(n + 1)
                                values(n, 1)
                                scores(n, 3)
                                if n + 2 < UNITS:
                                    max_scores(n + 2, 0, 3)
                                values(n, 2)
                                if n + 2 < UNITS:
                                    max_scores(n + 2, 3, HALF)
                                values(n, 3)
                            pe.wait_ge(exp_done, ONE + (b + 1) * UNITS * PAIRS)
                            pe.wait_ge(norm_done, ONE + b * CHUNKS + CHUNKS - 1)
                            for t in range(QT):
                                for k in range(CHUNKS - 1):
                                    pe.matmul(pS[t // 2][:, t % 2, :], oT[:, k, t * P:(t + 1) * P], w_o[:, k, :],
                                              start=(k == 0), stop=False)
                            pe.wait_ge(norm_done, ONE + (b + 1) * CHUNKS)
                            for t in range(QT):
                                pe.matmul(pS[t // 2][:, t % 2, :], oT[:, CHUNKS - 1, t * P:(t + 1) * P],
                                          w_o[:, CHUNKS - 1, :], start=False, stop=True).then_inc(w_ready, 1)

                    @block.scalar
                    def _(act):
                        for s in (exp_done, o_done,):
                            act.sem_inc(s, ONE)
                        with act.Fori(0, BATCH) as b:
                            def high(kind, c):
                                item_ready(act, b, (kind, c))
                                if not own_k and kind == "K":
                                    act.copy(k_first[:, 0, :], psum_of((kind, c))[0:3 * HD, :]).then_inc(hi_done, 1)
                                    return
                                dst = part(kind, 0)
                                act.wait_ge(spread_out, DMA_ONE + (b * CHUNKS + c) * SPREADS * 16)
                                if b_qk is None:
                                    act.copy(dst, psum_of((kind, c))[:]).then_inc(hi_done, 1)
                                else:
                                    col = c + (CHUNKS if kind == "K" else 0)
                                    act.activation(dst, psum_of((kind, c))[:], ACT.Identity,
                                                   bias=b_qk[:, col:col + 1]).then_inc(hi_done, 1)

                            def high_chunk(c):
                                high("Q", c)
                                if own_k:
                                    high("K", c)

                            def copy_max(n):
                                act.wait_ge(max_in, DMA_ONE + (b * UNITS + n) * 16)
                                item_ready(act, b, ("M", n))
                                act.copy(nm_rows[:], psum_of(("M", n))[0:2 * UH, :]).then_inc(max_rows_out, 1)

                            def exps(n, kt):
                                for p in range(2):
                                    act.wait_ge(pv_done, ONE + b * UNITS * QT + max(n * QT + kt - 1, 0))
                                    act.wait_ge(s_ready, ONE + b * UNITS * PAIRS + n * PAIRS + kt * 2 + p + 1)
                                    act.activation(probs[kt % 2][:, 2 * p:2 * p + 2, 0:SEQ - kt * P],
                                                   pS[p][:, :, 0:SEQ - kt * P], ACT.Exp, scale=SCORE_SCALE).then_inc(exp_done, 1)

                            for t in range(QT):
                                item_ready(act, b, ("T", t))
                                act.copy(xT[:, :, t * P:(t + 1) * P],
                                         psum_of(("T", t))[:].rearrange("p (k q) -> p k q", k=KC)).then_inc(xt_done, 1)
                            if not own_k:
                                high("K", 0)
                            high_chunk(0)
                            high_chunk(1)
                            copy_max(0)
                            for n in range(UNITS):
                                exps(n, 0)
                                if n % 2 == 0 and n // 2 + 2 < CHUNKS:
                                    high_chunk(n // 2 + 2)
                                exps(n, 1)
                                exps(n, 2)
                                if n + 1 < UNITS:
                                    copy_max(n + 1)
                                exps(n, 3)
                                act.wait_ge(packed[n % 2], DMA_ONE + (b * CHUNKS + n // 2) * 32)
                                act.wait_ge(pv_done, ONE + b * UNITS * QT + (n + 1) * QT)
                                act.copy(o_raw[:, n % 2, :], pO[:]).then_inc(o_done, 1)

                    @block.gpsimd
                    def _(pool):
                        for t in range(QT):
                            pool.memset(vv[:, t, :, :, 1] if own_k else vv[:, t, :, 1], 1.0).then_inc(ones_in, 1)

                    @block.vector
                    def _(dve):
                        dve.wait_ge(ones_in, QT)
                        for s in (xhat_ready, bank_read, norm_done, max_split, x_done, inverted,):
                            dve.sem_inc(s, ONE)
                        with dve.Fori(0, BATCH) as b:
                            def low(kind, c):
                                dve.wait_ge(hi_done, b * NS + split_at[(kind, c)] + 1)
                                src = psum_of((kind, c))
                                if not own_k and kind == "K":
                                    rows = k_first[2 * HD:3 * HD, 0, :]
                                    dve.tensor_tensor(rows, src[2 * HD:3 * HD, :], rows.bitcast(F32), ALU.subtract).then_inc(bank_read, 1)
                                    return
                                hi, lo = part(kind, 0), part(kind, 1)
                                if b_qk is None:
                                    dve.tensor_tensor(lo, src[:], hi.bitcast(F32),
                                                      ALU.subtract).then_inc(bank_read, 1)
                                else:
                                    col = c + (CHUNKS if kind == "K" else 0)
                                    dve.scalar_tensor_tensor(lo, src[:], b_qk[:, col:col + 1],
                                                             hi.bitcast(F32), ALU.add, ALU.subtract).then_inc(bank_read, 1)

                            def low_chunk(c):
                                low("Q", c)
                                if own_k:
                                    low("K", c)

                            def maxima(n, lo, hi):
                                for g in range(lo, hi):
                                    item_ready(dve, b, ("A", n, g))
                                    qt, heads = GROUPS[g]
                                    width, m = (qt + 1) * P, len(heads)
                                    dve.tensor_reduce(neg_max[:, qt, heads[0]:heads[0] + m],
                                                      psum_of(("A", n, g))[:, 0:m * width].rearrange("p (h k) -> p h k", h=m),
                                                      AX.X, ALU.max, negate=True).then_inc(bank_read, 1)

                            def split_max(n):
                                item_read(dve, b, ("A", n, len(GROUPS) - 1))
                                hi, lo = nm_parts[:, :, 0, :], nm_parts[:, :, 1, :]
                                dve.tensor_copy(hi, neg_max[:]).then_inc(s_split, 1)
                                dve.wait_ge(s_split, b * UNITS + n + 1)
                                dve.tensor_tensor(lo, neg_max[:], hi.bitcast(F32), ALU.subtract).then_inc(max_split, 1)

                            def invert_sums(c):
                                for s in range(2):
                                    dve.wait_ge(packed[s], DMA_ONE + (b * CHUNKS + c + 1) * 32)
                                dve.reciprocal(sums[:, c % 2, :], sums[:, c % 2, :]).then_inc(inverted, 1)

                            def normalise(c):
                                dve.wait_ge(inv_in, (b * CHUNKS + c + 1) * 16)
                                dve.tensor_tensor(oT[:, c, :], oT[:, c, :], den[:], ALU.mult).then_inc(norm_done, 1)

                            if not own_k:
                                low("K", 0)
                            low_chunk(0)
                            if own_k:
                                for t in range(QT):
                                    item_ready(dve, b, ("V", t))
                                    dve.tensor_tensor(vv[:, t, :, :, 0], psum_of(("V", t))[:].rearrange("p (h d) -> p h d", h=HEADS),
                                                      b_v[:].rearrange("p (h d) -> p h d", h=HEADS), ALU.add).then_inc(bank_read, 1)
                            else:
                                item_ready(dve, b, ("V", 0))
                                dve.tensor_copy(vv[:, :, :, 0], psum_of(("V", 0))[:, 0:QT * HD].rearrange("p (t d) -> p t d", t=QT)
                                                ).then_inc(bank_read, 1)
                            low_chunk(1)

                            dve.wait_ge(x_done, ONE + b * QT)
                            norm = LayerNorm(dve, x, xhat, ln_small, (b + 1) % BATCH, s_ln, b * LayerNorm.STEPS)
                            maxima(0, 0, len(GROUPS))
                            split_max(0)
                            maxima(1, 0, HALF)
                            for n in range(UNITS):
                                if n % 2 == 0 and n // 2 + 2 < CHUNKS:
                                    low_chunk(n // 2 + 2)
                                if n + 1 < UNITS:
                                    maxima(n + 1, HALF, len(GROUPS))
                                    split_max(n + 1)
                                if n % 2 == 0 and n >= 2:
                                    invert_sums(n // 2 - 1)
                                if n + 2 < UNITS:
                                    maxima(n + 2, 0, HALF)
                                if n < QT:
                                    norm.statistics(n)
                                elif n == QT:
                                    norm.scales()
                                elif n == QT + 1:
                                    item_ready(dve, b, ("T", QT - 1))
                                    for t in range(QT):
                                        norm.rows(t, xhat_ready)
                                if n % 2 == 1 and n >= 3:
                                    normalise((n - 3) // 2)
                            invert_sums(CHUNKS - 1)
                            normalise(CHUNKS - 1)
                            for t in range(QT):
                                dve.wait_ge(w_ready, b * QT + t + 1)
                                xt, y = x[:, b * QT + t, :], pS[t // 2][:, t % 2, :]
                                if b_o is None:
                                    dve.tensor_tensor(xt, y, xt, ALU.add).then_inc(x_done, 1)
                                else:
                                    dve.tensor_tensor(xt, y, xt, ALU.add).then_inc(s_res, 1)
                                    dve.wait_ge(s_res, b * QT + t + 1)
                                    dve.tensor_tensor(xt, xt, b_o[:], ALU.add).then_inc(x_done, 1)

                    @block.sync
                    def _(sp):
                        for s in (spread_out, max_in, packed[0], packed[1], inv_out,):
                            sp.sem_inc(s, DMA_ONE)
                        with sp.Fori(0, BATCH) as b:
                            def store_parts(c):
                                item_read(sp, b, ("K", c) if own_k else ("Q", c))
                                for i, dram in enumerate((spread_q[c, 2:, :, :], spread_k[c]) if own_k else (spread_q[c, 2:, :, :],)):
                                    sp.dma_start(dram.rearrange("(i d) h t -> (d h) i t", i=2),
                                                 parts[:, 2 * i:2 * i + 2, :].bitcast(F32)).then_inc(spread_out, 16)

                            def load_stack(n):
                                c, first = n // 2, (n % 2) * UH
                                sp.wait_ge(spread_out, DMA_ONE + (b * CHUNKS + c + 1) * SPREADS * 16)
                                sp.sem_inc(passed, 1)
                                stack_free(sp, b, n)

                                def load(stack, dram, at, lo, hi):
                                    sp.dma_start(stack[n % STACKS][at:at + hi - lo, :, :].bitcast(F32),
                                                 dram[c, lo:hi, first:first + UH, :]).then_inc(loaded[n % STACKS], 16)

                                load(Qs, spread_q, 0, 0, 2 + 2 * HD)
                                load(Qs, spread_q, 2 + 2 * HD, 2, 2 + HD)
                                if own_k:
                                    load(Ks, spread_k, PART0, 0, HD)
                                    load(Ks, spread_k, PART0 + HD, 0, 2 * HD)

                            def load_max(n):
                                item_read(sp, b, ("M", n))
                                sp.dma_start(Qs[n % STACKS][MAX0:MAX0 + 2, :, :].bitcast(F32),
                                             nm_rows[:].bitcast(F32)).then_inc(max_in, 16)

                            def pack(n):
                                c, r = n // 2, (n % 2) * UH * HD
                                sp.wait_ge(o_done, ONE + b * UNITS + n + 1)
                                sp.dma_start(oT[r:r + UH * HD, c, :], o_raw[0:P:2, n % 2, :]).then_inc(packed[n % 2], 16)
                                if n % 2 == 0:
                                    sp.wait_ge(inv_out, DMA_ONE + (b * CHUNKS + max(c - 1, 0)) * 16)
                                sp.dma_start(sums[r:r + UH * HD, c % 2, :], o_raw[1:P:2 * HD, n % 2, :]).then_inc(packed[n % 2], 16)

                            def spread_sums(c):
                                sp.wait_ge(inverted, ONE + b * CHUNKS + c + 1)
                                sp.dma_start(inv_dram[c].rearrange("h (d q) -> (h d) q", d=HD), sums[:, c % 2, :]).then_inc(inv_out, 16)
                                sp.wait_ge(inv_out, DMA_ONE + (b * CHUNKS + c + 1) * 16)
                                sp.sem_inc(passed, 1)
                                sp.wait_ge(norm_done, ONE + b * CHUNKS + c)
                                sp.dma_start(den[:], inv_dram[c].unsqueeze(1).broadcast_to([P // HD, HD, SEQ])).then_inc(inv_in, 16)

                            if not own_k:
                                item_read(sp, b, ("K", 0))
                                sp.dma_start(k_all[PART0:PART0 + 3 * HD, :].bitcast(F32),
                                             k_first[:, 0, :].bitcast(F32)).then_inc(key_parts_in, 16)
                            store_parts(0)
                            load_stack(0)
                            load_stack(1)
                            load_max(0)
                            store_parts(1)
                            load_stack(2)
                            for n in range(UNITS):
                                if n % 2 == 0 and n // 2 + 2 < CHUNKS:
                                    store_parts(n // 2 + 2)
                                if n + 1 < UNITS:
                                    load_max(n + 1)
                                if n % 2 == 1 and n >= 3:
                                    spread_sums((n - 3) // 2)
                                if n + STACKS < UNITS:
                                    load_stack(n + STACKS)
                                pack(n)
                            spread_sums(CHUNKS - 1)

        if stages >= 1:
            ffn0("a_", True)
        if stages >= 2:
            attention("m_", w_q0, w_k0, w_v0, w_o0, False, got_att0, 4, None, None, None)
        layer0a.close()
        if stages >= 3:
            ffn0("b_", False)
        layer0.close()
        if stages < 4:
            with nc.Block() as block:
                @block.sync
                def _(sp):
                    sp.wait_ge(got_base1, 16)
                    sp.wait_ge(got_att0, 64)
                    sp.dma_start(out.rearrange("b (t p) d -> p (b t) d", p=P), x[:]).then_inc(stored, 16)
                    sp.wait_ge(stored, 16)
        else:
            layer1 = ExitStack()
            w_qk1 = sb("w_qk1", [P, KC, 2 * D], F32, layer1)
            w_v1 = sb("w_v1", [P, KC, D], F32, layer1)
            w_o1 = sb("w_o1", [P, KC, D], F32, layer1)
            b_v1 = sb("b_v1", [P, D], F32, layer1)
            b_o1 = sb("b_o1", [P, D], F32, layer1)
            b_qk1 = sb("b_qk1", [P, 2 * CHUNKS], F32, layer1)

            def load_layer1(sp):
                for dst, src in ((w_qk1, "wqk1"), (w_v1, "wv1"), (w_o1, "wo1")):
                    sp.dma_start(dst[:], w[src].rearrange("(c p) m -> p c m", p=P)).then_inc(got_att1, 16)
                sp.dma_start(b_v1[:], w["bv1"].partition_broadcast(P)).then_inc(got_att1, 16)
                sp.dma_start(b_o1[:], w["bo1"].partition_broadcast(P)).then_inc(got_att1, 16)
                sp.dma_start(b_qk1[:], w["bqk1"]).then_inc(got_att1, 16)

            ffn1("c_", True, stages == 4, load_layer1 if stages > 4 else None)
            if stages > 4:
                attention("h_", w_qk1[:, :, 0:D], w_qk1[:, :, D:2 * D], w_v1, w_o1, True, got_att1, 6, b_qk1, b_v1, b_o1)
                layer1.close()
                ffn1("d_", False, True, None)


def kernel(stages=6, **inputs):
    import numpy as _np
    import concourse.bacc as _bacc
    from concourse import mybir as _mybir
    from concourse.bass_utils import run_bass_kernel_spmd as _run

    g = {k: _np.asarray(v) for k, v in inputs.items()}

    def by_dim(m):
        return m.reshape(*m.shape[:-1], CHUNKS, P // HD, HD).swapaxes(-1, -2).reshape(m.shape)

    kv = g["L0_attn_Wkv"]
    wqkv = g["L1_attn_w_qkv"].T
    slopes = (4.0 * 2.0 ** (-0.25 * _np.arange(1, HEADS + 1))).astype(_np.float32)
    hi = (slopes.view(_np.uint32) & _np.uint32(0xFFFFF000)).view(_np.float32)
    pos = _np.arange(SEQ, dtype=_np.float32)
    laid = {
        "x": g["L0_attn_hidden_states"],
        "ar0": _np.concatenate([g["L0_ffn_A"].reshape(E0 * R0, D).T, g["L0_ffn_route_w"].T], axis=1),
        "b0": g["L0_ffn_Bw"].transpose(0, 2, 1).reshape(E0 * R0, D),
        "wq0": by_dim(g["L0_attn_Wq"]),
        "wk0": _np.concatenate([kv[:, :HD]] * 3, axis=1),
        "wv0": kv[:, HD:],
        "wo0": g["L0_attn_Wo"],
        "wqk1": _np.concatenate([by_dim(wqkv[:, :D]), by_dim(wqkv[:, D:2 * D])], axis=1),
        "wv1": wqkv[:, 2 * D:],
        "wo1": g["L1_attn_w_out"].T,
        "bqk1": _np.concatenate([by_dim(g["L1_attn_b_qkv"][:D]), by_dim(g["L1_attn_b_qkv"][D:2 * D])]).reshape(2 * CHUNKS, P).T,
        "bv1": g["L1_attn_b_qkv"][2 * D:],
        "bo1": g["L1_attn_b_out"],
        "base": g["L1_ffn_W_base"].T,
        "b_base": g["L1_ffn_b_base"],
        "lora_a": g["L1_ffn_lora_A"].reshape(E1 * R1, D),
        "lora_b": g["L1_ffn_lora_B"].transpose(0, 2, 1).reshape(E1 * R1, D),
        "router_w": g["L1_ffn_router_W"],
        "router_b": g["L1_ffn_router_b"],
        "prior": g["L1_ffn_domain_prior"],
        "active": g["L1_ffn_active"],
        "slopes": _np.ascontiguousarray(_np.broadcast_to(_np.stack([hi, slopes - hi]).reshape(2, CHUNKS, P // HD, 1).swapaxes(0, 1), (CHUNKS, 2, P // HD, SEQ))),
        "key_rows": _np.stack([pos, pos, pos * 0 + 1, pos * 0 + 1]),
    }
    nc = _bacc.Bacc("TRN2", target_bir_lowering=False, num_devices=1)
    arrays, aps = {}, {}
    for name, a in laid.items():
        a = _np.ascontiguousarray(a)
        arrays[f"in_{name}"] = a
        aps[name] = nc.dram_tensor(f"in_{name}", a.shape, _mybir.dt.from_np(a.dtype), kind="ExternalInput").ap()
    out = nc.dram_tensor("out_x", (BATCH, SEQ, D), F32, kind="ExternalOutput").ap()
    macaron(nc, aps.pop("x"), aps, out, stages)
    r = _run(nc, [arrays], core_ids=[0])
    return r.results[0]["out_x"]
```

```python
from contextlib import ExitStack

import numpy as np

import concourse.bass as bass
from concourse import mybir

F32 = mybir.dt.float32
F32R = mybir.dt.float32r
BF16 = mybir.dt.bfloat16
I32 = mybir.dt.int32
U32 = mybir.dt.uint32
ALU = mybir.AluOpType
ACT = mybir.ActivationFunctionType
AX = mybir.AxisListType

P = 128
BATCH, SEQ, D = 4, 512, 512
TOKENS = BATCH * SEQ
KC = D // P
QT = SEQ // P
HEADS, HD = 32, 16
E0, R0 = 8, 16
E1, A1, R1 = 16, 4, 8
Z1 = A1 * R1
EPS = 1e-5
MASKED = -1e30
SCORE_SCALE = HD ** -0.5
RSQRT_MAGIC = 1597463007.0

UH = 4
UNITS = HEADS // UH
CHUNKS = HEADS * HD // P
STACKS = 3
PART0 = 2
V0 = 64
KV_COLS = V0 + HD
MAX0 = P - 2


ONE, DMA_ONE = 1, 16


def twice(b, t):
    return b * QT + max(t - 1, 0)


class LayerNorm:

    STEPS = 14
    COUNTS = QT + 7 + 1 + 9

    def __init__(self, dve, x, small, nb, sem, base):
        self.dve, self.x, self.nb, self.sem, self.base = dve, x, nb, sem, base
        self.stats, self.mean, self.var, self.y, self.a, self.shift = small

    def statistics(self, t):
        self.dve.bn_stats(self.stats[:, t, :], self.x[:, self.nb * QT + t, :]).then_inc(self.sem, 1)

    def scale_step(self, i, rows_made, scaled):
        dve, sem, base, stats = self.dve, self.sem, self.base, self.stats
        mean, var, y, a = self.mean, self.var, self.y, self.a
        if i == 0:
            dve.wait_ge(sem, base + QT)
            dve.tensor_tensor(mean[:], stats[:, :, 1], stats[:, :, 4], ALU.add).then_inc(sem, 1)
            dve.tensor_tensor(a[:], stats[:, :, 1], stats[:, :, 4], ALU.subtract).then_inc(sem, 1)
            dve.tensor_tensor(var[:], stats[:, :, 2], stats[:, :, 5], ALU.add).then_inc(sem, 1)
        elif i == 1:
            dve.wait_ge(sem, base + QT + 3)
            dve.tensor_scalar(mean[:], mean[:], 0.5, None, ALU.mult).then_inc(sem, 1)
            dve.tensor_tensor(a[:], a[:], a[:], ALU.mult).then_inc(sem, 1)
            dve.tensor_scalar(var[:], var[:], 1.0 / D, EPS, ALU.mult, ALU.add).then_inc(sem, 1)
        elif i == 2:
            dve.wait_ge(sem, base + QT + 6)
            dve.scalar_tensor_tensor(var[:], a[:], 0.25, var[:], ALU.mult, ALU.add).then_inc(sem, 1)
        elif i == 3:
            rows_made()
            dve.wait_ge(sem, base + QT + 7)
            dve.tensor_scalar(y[:].bitcast(I32), var[:].bitcast(I32), -0.5, RSQRT_MAGIC, ALU.mult, ALU.add).then_inc(sem, 1)
        elif i < self.STEPS - 1:
            dve.wait_ge(sem, base + QT + 8 + i - 4)
            if i % 3 == 1:
                dve.tensor_tensor(a[:], y[:], y[:], ALU.mult).then_inc(sem, 1)
            elif i % 3 == 2:
                dve.scalar_tensor_tensor(a[:], a[:], -0.5, var[:], ALU.mult, ALU.mult).then_inc(sem, 1)
            else:
                dve.scalar_tensor_tensor(y[:], a[:], 1.5, y[:], ALU.add, ALU.mult).then_inc(sem, 1)
        elif i == self.STEPS - 1:
            dve.wait_ge(sem, base + self.COUNTS)
            dve.scalar_tensor_tensor(self.shift[:], mean[:], -1.0, y[:], ALU.mult, ALU.mult).then_inc(scaled, 1)


def normed_row(act, x, xhat, small, nb, t, ready):
    y, shift = small[3], small[5]
    act.activation(xhat[:, t, :], x[:, nb * QT + t, :], ACT.Identity, bias=shift[:, t:t + 1],
                   scale=y[:, t:t + 1]).then_inc(ready, 1)


class Steps:

    def __init__(self, transposes=None, first=None, head=None, units=None, output=None,
                 copy_xt=None, invert_sums=None, normalise=None, residual=None, spread_sums=None):
        self.transposes = transposes
        self.first = first
        self.head = head
        self.units = units
        self.output = output
        self.copy_xt = copy_xt
        self.invert_sums = invert_sums
        self.normalise = normalise
        self.residual = residual
        self.spread_sums = spread_sums


def macaron(nc, x_in, w, out):
    ctx = ExitStack()
    nsem = [0]

    def sb(name, shape, dt=F32, c=ctx):
        return c.enter_context(nc.sbuf_tensor(name, shape, dt))

    def ps(name, shape, dt=F32, c=ctx):
        return c.enter_context(nc.psum_tensor(name, shape, dt))

    def sem(name):
        nsem[0] += 1
        return ctx.enter_context(nc.semaphore(name))

    with ctx:
        x = sb("x", [P, TOKENS // P, D])
        xhat = sb("xhat", [P, QT, D])
        ident = sb("ident", [P, P])
        identb = sb("identb", [P, P], BF16)
        causal = sb("causal", [P, P], BF16)
        ln_small = (sb("ln_stats", [P, QT, 6]), sb("ln_mean", [P, QT]), sb("ln_ve", [P, QT]),
                    sb("ln_y", [P, QT]), sb("ln_a", [P, QT]), sb("ln_shift", [P, QT]))
        w_z1 = sb("w_z1", [P, KC, Z1 + A1])
        w_b1 = sb("w_b1", [Z1, D])
        half_b = sb("half_b", [P, D])
        gate_b = sb("gate_b", [P, A1])
        causal_t = sb("causal_t", [P, P], BF16)
        Qs = [sb(f"Qs{i}", [P, UH, SEQ], F32R) for i in range(STACKS)]
        Ks = [sb(f"Ks{i}", [P, UH, SEQ], F32R) for i in range(STACKS)]
        spread_q = nc.dram_tensor("spread_q", (CHUNKS, 2 + 2 * HD, P // HD, SEQ), F32, kind="Internal").ap()
        weights_split = sem("weights_split")
        got_consts, zeroed, rounded, keys_in, passed = (
            sem(n) for n in ("got_consts", "zeroed_stacks", "rounded", "keys_in", "passed"))

        got_x0 = [sem(f"got_x0_{t}") for t in range(QT)]
        got_x, got_ffn0, got_att0, got_raw1, got_base1, got_att1 = (
            sem(n) for n in ("got_x", "got_ffn0", "got_att0", "got_raw1", "got_base1", "got_att1"))
        stored = sem("stored")
        x_rows = x_in.rearrange("b (t p) d -> p (b t) d", p=P)

        w_ar0 = sb("w_ar0", [P, KC, E0 * R0 + E0])
        w_b0 = sb("w_b0", [P, D])
        number8 = sb("number8", [P, E0])
        layer0a = ExitStack()
        split0 = [(sb(name + "_high", shape, F32R, layer0a), sb(name + "_low", shape, F32R, layer0a))
                  for name, shape in (("w_q0", [P, KC, D]), ("w_kv0", [P, KC, KV_COLS]), ("w_o0", [P, KC, D]))]
        loaded0 = ExitStack()
        whole0 = [sb(name, shape, F32, loaded0)
                  for name, shape in (("w_q0", [P, KC, D]), ("w_kv0", [P, KC, KV_COLS]), ("w_o0", [P, KC, D]))]

        with ExitStack() as c:
            act_i = sb("act_i", [P, A1], I32, c)
            act_f = sb("act_f", [P, A1], F32, c)
            act_n = sb("act_n", [P, A1], F32, c)
            row_i = sb("row_i", [P, R1 + 2], I32, c)
            row_f = sb("row_f", [P, R1 + 2], F32, c)
            row_e = sb("row_e", [P, 1], I32, c)
            row_r = sb("row_r", [P, 1], I32, c)
            rank_i = sb("rank_i", [P, R1], I32, c)
            rank_f = sb("rank_f", [P, R1], F32, c)
            iota_i = sb("iota_i", [P, E0], I32, c)
            part_i = sb("part_i", [P, 1], I32, c)
            part_f = sb("part_f", [P, 1], F32, c)
            sel_e = sb("sel_e", [P, A1], F32, c)
            sel_r = sb("sel_r", [P, R1], F32, c)
            sel_er = sb("sel_er", [P, A1, R1], F32, c)
            sel_e16 = sb("sel_e16", [E1, A1], F32, c)
            lora_a = sb("lora_a", [P, D], F32, c)
            lora_b = sb("lora_b", [P, D], F32, c)
            rout = sb("rout", [E1, D], F32, c)
            rb = sb("rb", [E1, 1], F32, c)
            prior = sb("prior", [E1, 1], F32, c)
            lprior = sb("lprior", [E1, 1], F32, c)
            bias_bc = sb("bias_bc", [E1, P], F32, c)
            ones16 = sb("ones16", [E1, P], F32, c)
            pg = ps("pg", [P, KC, 512], F32, c)
            pb = ps("pb", [P, 512], F32, c)
            pl = ps("pl", [P, 512], F32, c)
            consts, iotas, zeroed_masks = sem("consts"), sem("iotas"), sem("zeroed_masks")
            s_dve, s_ln, s_act = sem("s_dve"), sem("s_ln"), sem("s_act")
            picked, scaled, rows_made = sem("picked"), sem("scaled0"), sem("rows_made0")

            with nc.Block() as block:
                @block.sync
                def _(sp):
                    for t in range(QT):
                        sp.dma_start(x[:, t, :], x_rows[:, t, :]).then_inc(got_x0[t], 16)
                    sp.dma_start(w_ar0[:], w["ar0"].rearrange("(c p) m -> p c m", p=P)).then_inc(got_ffn0, 16)
                    sp.dma_start(w_b0[:], w["b0"]).then_inc(got_ffn0, 16)
                    sp.dma_start(act_i[:], w["active"].partition_broadcast(P)).then_inc(got_raw1, 16)
                    sp.dma_start(lora_a[:], w["lora_a"]).then_inc(got_raw1, 16)
                    sp.dma_start(lora_b[:], w["lora_b"]).then_inc(got_raw1, 16)
                    sp.dma_start(rout[:], w["router_w"]).then_inc(got_raw1, 16)
                    sp.dma_start(rb[:], w["router_b"].rearrange("(e a) -> e a", a=1)).then_inc(got_raw1, 16)
                    sp.dma_start(prior[:], w["prior"].rearrange("(e a) -> e a", a=1)).then_inc(got_raw1, 16)
                    sp.dma_start(half_b[:], w["b_base"].partition_broadcast(P)).then_inc(got_raw1, 16)
                    for b in range(1, BATCH):
                        sp.dma_start(x[:, b * QT:(b + 1) * QT, :], x_rows[:, b * QT:(b + 1) * QT, :]).then_inc(got_x, 16)
                    for dst, src in zip(whole0, ("wq0", "wkv0", "wo0")):
                        sp.dma_start(dst[:], w[src].rearrange("(c p) m -> p c m", p=P)).then_inc(got_att0, 16)

                @block.gpsimd
                def _(pool):
                    pool.memset(ident[:], 0.0).then_inc(zeroed_masks, 1)
                    pool.memset(identb[:], 0.0).then_inc(zeroed_masks, 1)
                    pool.memset(causal[:], 0.0).then_inc(zeroed_masks, 1)
                    pool.memset(causal_t[:], 0.0).then_inc(zeroed_masks, 1)
                    pool.iota(part_i[:], [[0, 1]], base=0, channel_multiplier=1).then_inc(iotas, 1)
                    pool.iota(rank_i[:], [[1, R1]], base=0, channel_multiplier=0).then_inc(iotas, 1)
                    pool.iota(iota_i[:], [[1, E0]], base=0, channel_multiplier=0).then_inc(iotas, 1)
                    pool.wait_ge(zeroed_masks, 4)
                    for m in (ident, identb):
                        pool.affine_select(out=m[:], in_=m[:], compare_op=ALU.not_equal, fill=1.0, base=0,
                                           pattern=[[-1, P]], channel_multiplier=1).then_inc(consts, 1)
                    pool.affine_select(out=causal[:], in_=causal[:], compare_op=ALU.is_ge, fill=MASKED, base=0,
                                       pattern=[[-1, P]], channel_multiplier=1).then_inc(consts, 1)
                    pool.affine_select(out=causal_t[:], in_=causal_t[:], compare_op=ALU.is_ge, fill=MASKED, base=0,
                                       pattern=[[1, P]], channel_multiplier=-1).then_inc(consts, 1)
                    pool.memset(ones16[:], 1.0).then_inc(consts, 1)

                @block.scalar
                def _(act):
                    act.wait_ge(scaled, 1)
                    for t in range(QT):
                        normed_row(act, x, xhat, ln_small, 0, t, rows_made)
                    act.wait_ge(s_dve, 1)
                    act.activation(lprior[:], prior[:], ACT.Ln).then_inc(s_act, 1)
                    act.wait_ge(picked, 1)
                    act.copy(w_z1[:], pg[:, :, 0:Z1 + A1]).then_inc(s_act, 1)
                    act.wait_ge(picked, 2)
                    act.copy(w_b1[:], pb[0:Z1, :]).then_inc(s_act, 1)
                    act.wait_ge(picked, 3)
                    act.copy(gate_b[:], pl[:, 0:A1]).then_inc(s_act, 1)

                @block.vector
                def _(dve):
                    k = 0

                    def step(ins):
                        nonlocal k
                        ins.then_inc(s_dve, 1)
                        k += 1
                        dve.wait_ge(s_dve, k)

                    norm = LayerNorm(dve, x, ln_small, 0, s_ln, 0)
                    for t in range(QT):
                        dve.wait_ge(got_x0[t], 16)
                        norm.statistics(t)
                    for i in range(LayerNorm.STEPS):
                        norm.scale_step(i, lambda: None, scaled)
                    dve.wait_ge(got_raw1, 7 * 16)
                    step(dve.tensor_scalar(prior[:], prior[:], 1e-12, None, ALU.add))
                    step(dve.tensor_copy(act_f[:], act_i[:]))
                    step(dve.tensor_scalar(act_n[:], act_f[:], 0.0, float(E1), ALU.is_lt, ALU.mult))
                    step(dve.tensor_tensor(act_f[:], act_f[:], act_n[:], ALU.add))
                    dve.wait_ge(iotas, 3)
                    step(dve.tensor_scalar(row_e[:], part_i[:], 3, None, ALU.logical_shift_right))
                    step(dve.tensor_scalar(row_r[:], part_i[:], R1 - 1, None, ALU.bitwise_and))
                    step(dve.tensor_copy(row_f[:, 0:1], row_e[:]))
                    step(dve.tensor_copy(row_f[:, 1:2], row_r[:]))
                    step(dve.tensor_copy(part_f[:], part_i[:]))
                    step(dve.tensor_copy(rank_f[:], rank_i[:]))
                    step(dve.tensor_scalar(number8[:], iota_i[:], float(-E0), None, ALU.add))
                    step(dve.tensor_scalar(sel_e[:], act_f[:], row_f[:, 0:1], None, ALU.is_equal))
                    step(dve.tensor_scalar(sel_r[:], rank_f[:], row_f[:, 1:2], None, ALU.is_equal))
                    step(dve.tensor_tensor(sel_er[:], sel_e[:].unsqueeze(2).broadcast_to([P, A1, R1]),
                                           sel_r[:].unsqueeze(1).broadcast_to([P, A1, R1]), ALU.mult))
                    step(dve.tensor_scalar(sel_e16[:], act_f[0:E1, :], part_f[0:E1, :], None, ALU.is_equal))
                    dve.wait_ge(s_act, 1)
                    step(dve.tensor_tensor(rb[:], rb[:], lprior[:], ALU.add))
                    dve.wait_ge(consts, 5)
                    step(dve.tensor_scalar(bias_bc[:], ones16[:], rb[:, 0:1], None, ALU.mult))
                    step(dve.tensor_scalar(half_b[:], half_b[:], 0.5, None, ALU.mult))

                @block.tensor
                def _(pe):
                    pe.wait_ge(s_dve, 17)
                    for k in range(KC):
                        last = pe.matmul(pg[:, k, 0:Z1], lora_a[:, k * P:(k + 1) * P], sel_er[:].rearrange("p a r -> p (a r)"),
                                         start=True, stop=True)
                        last = pe.matmul(pg[:, k, Z1:Z1 + A1], rout[:, k * P:(k + 1) * P], sel_e16[:],
                                         start=True, stop=True)
                    last.then_inc(picked, 1)
                    pe.matmul(pb[0:Z1, :], sel_er[:].rearrange("p a r -> p (a r)"), lora_b[:],
                              start=True, stop=True).then_inc(picked, 1)
                    pe.matmul(pl[:, 0:A1], bias_bc[:], sel_e16[:], start=True, stop=True).then_inc(picked, 1)

        def transpose_tile(pe, b, t, pT, ready, done, wt_done):
            if t == 0:
                pe.wait_ge(wt_done, ONE + b * QT)
            elif t > 1:
                pe.wait_ge(done, ONE + b * QT + t - 1)
            for k in range(KC):
                last = pe.transpose(pT[t % 2][:, k * P:(k + 1) * P], xhat[:, t, k * P:(k + 1) * P], ident[:])
            last.then_inc(ready, 1)

        def next_rows(act, b, t, scaled, xt_ready, xhat_ready):
            if t == 0:
                act.wait_ge(scaled, b + 1)
                act.wait_ge(xt_ready, (b + 1) * QT)
            for i in (t, t + 1):
                normed_row(act, x, xhat, ln_small, (b + 1) % BATCH, i, xhat_ready)

        def ffn0(tag, first, prefetch=None):
            with ExitStack() as c:
                mx = sb(tag + "mx", [P, 2], F32, c)
                hit = sb(tag + "hit", [P, 2, E0], F32, c)
                pick = sb(tag + "pick", [P, 2], F32, c)
                gate = sb(tag + "gate", [P, 2, E0], F32, c)
                if first:
                    key_rows = sb("key_rows", [4, SEQ], F32, c)
                    key_rows_r = sb("key_rows_r", [4, SEQ], F32R, c)
                xT = sb(tag + "xT", [P, KC, SEQ], F32, c)
                wh = sb(tag + "wh", [P, 2, E0 * R0], F32, c)
                whT = sb(tag + "whT", [P, 2, P], F32, c)
                pT = [ps(f"{tag}pT{i}", [P, 512], F32, c) for i in range(2)]
                pH = [ps(f"{tag}pH{i}", [P, 512], F32, c) for i in range(2)]
                pY = [ps(f"{tag}pY{i}", [P, 512], F32, c) for i in range(QT)]
                xt_ready, xt_done, h_ready, wh_done, wt_ready, wt_done, y_ready, x_done = (
                    sem(tag + n) for n in ("xt_ready", "xt_done", "h_ready", "wh_done", "wt_ready", "wt_done",
                                           "y_ready", "x_done"))
                xhat_ready, s_ln, scaled, s_gate = sem(tag + "xhat"), sem(tag + "s_ln"), sem(tag + "scaled"), sem(tag + "s_gate")

                with nc.Block() as block:
                    if first:
                        @block.gpsimd
                        def _(pool):
                            for m in Ks + Qs:
                                pool.memset(m[:].bitcast(F32), 0.0).then_inc(zeroed, 1)
                            pool.wait_ge(got_consts, 32)
                            pool.wait_ge(zeroed, 2 * STACKS)
                            pool.tensor_copy(key_rows_r[:], key_rows[:]).then_inc(rounded, 1)
                            pool.wait_ge(got_att0, 3 * 16)
                            for m, (high, low) in zip(whole0, split0):
                                pool.tensor_copy(high[:], m[:]).then_inc(weights_split, 1)
                            for i, (m, (high, low)) in enumerate(zip(whole0, split0)):
                                pool.wait_ge(weights_split, i + 1)
                                pool.tensor_tensor(low[:], m[:], high[:].bitcast(F32), ALU.subtract).then_inc(weights_split, 1)

                        @block.sync
                        def _(sp):
                            sp.dma_start(key_rows[:], w["key_rows"]).then_inc(got_consts, 16)
                            sp.dma_start(spread_q[:, 0:2, :, :], w["slopes"]).then_inc(got_consts, 16)
                            sp.wait_ge(zeroed, 2 * STACKS)
                            sp.wait_ge(rounded, 1)
                            for m in Ks:
                                for row, at in ((0, 0), (2, MAX0)):
                                    for j in range(UH):
                                        sp.dma_start(m[at:at + 2, j, :].bitcast(F32),
                                                     key_rows_r[row:row + 2, :].bitcast(F32)).then_inc(keys_in, 16)
                            sp.wait_ge(keys_in, 2 * UH * STACKS * 16)
                    else:
                        @block.sync
                        def _(sp):
                            prefetch(sp)

                    @block.tensor
                    def _(pe):
                        if first:
                            pe.wait_ge(got_ffn0, 2 * 16)
                        for s in (h_ready, wt_ready, y_ready,):
                            pe.sem_inc(s, ONE)
                        with pe.Fori(0, BATCH) as b:
                            pe.wait_ge(xhat_ready, ONE + b * QT)
                            transpose_tile(pe, b, 0, pT, xt_ready, xt_done, wt_done)

                            def up(t):
                                pe.wait_ge(xt_done, ONE + b * QT + t + 1)
                                pe.wait_ge(wh_done, ONE + twice(b, t))
                                for k in range(KC):
                                    last = pe.matmul(pH[t % 2][:, 0:E0 * R0 + E0], xT[:, k, t * P:(t + 1) * P],
                                                     w_ar0[:, k, :], start=(k == 0), stop=(k == KC - 1))
                                last.then_inc(h_ready, 1)

                            def turn(t):
                                pe.wait_ge(wh_done, ONE + b * QT + t + 1)
                                if t < 2:
                                    pe.wait_ge(xt_done, ONE + b * QT + t + 3)
                                else:
                                    pe.wait_ge(wt_done, ONE + b * QT + t - 1)
                                pe.transpose(pT[t % 2][:, 0:P], wh[:, t % 2, :], ident[:]).then_inc(wt_ready, 1)

                            def down(t):
                                pe.wait_ge(wt_done, ONE + b * QT + t + 1)
                                if t == 0:
                                    pe.wait_ge(x_done, ONE + b * QT)
                                pe.matmul(pY[t][:], whT[:, t % 2, :], w_b0[:], start=True, stop=True).then_inc(y_ready, 1)

                            transpose_tile(pe, b, 1, pT, xt_ready, xt_done, wt_done)
                            for t in range(QT):
                                up(t)
                                if t + 2 < QT:
                                    transpose_tile(pe, b, t + 2, pT, xt_ready, xt_done, wt_done)
                                if t >= 2:
                                    down(t - 2)
                                if t >= 1:
                                    turn(t - 1)
                            down(QT - 2)
                            turn(QT - 1)
                            down(QT - 1)

                    @block.scalar
                    def _(act):
                        for s in (xt_done, wt_done, xhat_ready):
                            act.sem_inc(s, ONE)
                        with act.Fori(0, BATCH) as b:
                            for t in range(QT):
                                act.wait_ge(xt_ready, b * QT + t + 1)
                                if t == 0:
                                    act.wait_ge(h_ready, ONE + b * QT)
                                act.copy(xT[:, :, t * P:(t + 1) * P],
                                         pT[t % 2][:].rearrange("p (k q) -> p k q", k=KC)).then_inc(xt_done, 1)
                            for t in range(QT):
                                if t == QT - 1:
                                    next_rows(act, b, 0, scaled, xt_ready, xhat_ready)
                                act.wait_ge(wt_ready, ONE + b * QT + t + 1)
                                act.wait_ge(y_ready, ONE + twice(b, t))
                                act.copy(whT[:, t % 2, :], pT[t % 2][:, 0:P]).then_inc(wt_done, 1)
                                if t == QT - 1:
                                    next_rows(act, b, 2, scaled, xt_ready, xhat_ready)

                    @block.vector
                    def _(dve):
                        if first:
                            dve.wait_ge(got_x, (BATCH - 1) * 16)
                        for s in (wh_done, x_done,):
                            dve.sem_inc(s, ONE)
                        with dve.Fori(0, BATCH) as b:
                            norm = LayerNorm(dve, x, ln_small, (b + 1) % BATCH, s_ln, b * LayerNorm.COUNTS)

                            def norm_step(t, i):
                                norm.scale_step(t * 5 + i, lambda: dve.wait_ge(xhat_ready, ONE + b * QT), scaled)

                            dve.wait_ge(x_done, ONE + b * QT)
                            for t in range(QT):
                                norm.statistics(t)

                            def route(t):
                                i, n = t % 2, b * QT * 4 + t * 4
                                dve.wait_ge(h_ready, ONE + b * QT + t + 1)
                                logits = pH[i][:, E0 * R0:E0 * R0 + E0]
                                dve.tensor_reduce(mx[:, i:i + 1], logits, AX.X, ALU.max).then_inc(s_gate, 1)
                                norm_step(t, 0)
                                dve.wait_ge(s_gate, n + 1)
                                dve.scalar_tensor_tensor(hit[:, i, :], logits, mx[:, i:i + 1], number8[:],
                                                         ALU.is_ge, ALU.mult).then_inc(s_gate, 1)
                                norm_step(t, 1)
                                dve.wait_ge(s_gate, n + 2)
                                dve.tensor_reduce(pick[:, i:i + 1], hit[:, i, :], AX.X, ALU.min).then_inc(s_gate, 1)
                                norm_step(t, 2)
                                dve.wait_ge(s_gate, n + 3)
                                dve.tensor_scalar(gate[:, i, :], number8[:], pick[:, i:i + 1], mx[:, i:i + 1],
                                                  ALU.is_equal, ALU.mult).then_inc(s_gate, 1)
                                norm_step(t, 3)
                                dve.wait_ge(s_gate, n + 4)
                                dve.wait_ge(wt_ready, ONE + twice(b, t))
                                dve.tensor_tensor(wh[:, i, :].rearrange("p (e r) -> p e r", e=E0),
                                                  pH[i][:, 0:E0 * R0].rearrange("p (e r) -> p e r", e=E0),
                                                  gate[:, i, :].unsqueeze(2).broadcast_to([P, E0, R0]),
                                                  ALU.mult).then_inc(wh_done, 1)
                                norm_step(t, 4)

                            def residual(t):
                                dve.wait_ge(y_ready, ONE + b * QT + t + 1)
                                xt = x[:, b * QT + t, :]
                                dve.scalar_tensor_tensor(xt, pY[t][:], 0.5, xt, ALU.mult, ALU.add).then_inc(x_done, 1)

                            route(0)
                            for t in range(1, QT):
                                route(t)
                                residual(t - 1)
                            residual(QT - 1)

        def ffn1(tag, first, last_stage, prefetch):
            with ExitStack() as c:
                xT = sb(tag + "xT", [P, KC, SEQ], F32, c)
                lg = sb(tag + "lg", [P, 2, A1], F32, c)
                nm = sb(tag + "nm", [P, 2], F32, c)
                ex = sb(tag + "ex", [P, 2, A1], F32, c)
                sm = sb(tag + "sm", [P, 2], F32, c)
                rs = sb(tag + "rs", [P, 2], F32, c)
                al = sb(tag + "al", [P, 2, A1], F32, c)
                wz = sb(tag + "wz", [P, 2, Z1], F32, c)
                wzT = sb(tag + "wzT", [Z1, 2, P], F32, c)
                pT = [ps(f"{tag}pT{i}", [P, 512], F32, c) for i in range(2)]
                pZ = [ps(f"{tag}pZ{i}", [P, 512], F32, c) for i in range(2)]
                pY = [ps(f"{tag}pY{i}", [P, 512], F32, c) for i in range(QT)]
                xt_ready, xt_done, z_ready, lg_done, ex_done, wz_done, wt_ready, wt_done, y_ready, x_done = (
                    sem(tag + n) for n in ("xt_ready", "xt_done", "z_ready", "lg_done", "ex_done", "wz_done",
                                           "wt_ready", "wt_done", "y_ready", "x_done"))
                xhat_ready, s_ln, scaled, s_gate, s_res = (
                    sem(tag + n) for n in ("xhat", "s_ln", "scaled", "s_gate", "s_res"))

                with nc.Block() as block:
                    @block.tensor
                    def _(pe):
                        if first:
                            pe.wait_ge(got_base1, 16)
                        for s in (wt_ready, y_ready,):
                            pe.sem_inc(s, ONE)
                        with pe.Fori(0, BATCH) as b:
                            pe.wait_ge(xhat_ready, ONE + b * QT)
                            transpose_tile(pe, b, 0, pT, xt_ready, xt_done, wt_done)

                            def low_rank(t, k):
                                if k == 0:
                                    pe.wait_ge(xt_done, ONE + b * QT + t + 1)
                                    pe.wait_ge(wz_done, ONE + twice(b, t))
                                mm = pe.matmul(pZ[t % 2][:, 0:Z1 + A1], xT[:, k, t * P:(t + 1) * P],
                                               w_z1[:, k, :], start=(k == 0), stop=(k == KC - 1))
                                if k == KC - 1:
                                    mm.then_inc(z_ready, 1)

                            def base(t, k):
                                if k == 0 and t == 0:
                                    pe.wait_ge(x_done, ONE + b * QT)
                                pe.matmul(pY[t][:], xT[:, k, t * P:(t + 1) * P], w_base[:, k, :],
                                          start=(k == 0), stop=False)

                            def turn(t):
                                pe.wait_ge(wz_done, ONE + b * QT + t + 1)
                                if t < 2:
                                    pe.wait_ge(xt_done, ONE + b * QT + t + 3)
                                else:
                                    pe.wait_ge(wt_done, ONE + b * QT + t - 1)
                                pe.transpose(pT[t % 2][0:Z1, 0:P], wz[:, t % 2, :], ident[:]).then_inc(wt_ready, 1)

                            def experts(t):
                                pe.wait_ge(wt_done, ONE + b * QT + t + 1)
                                pe.matmul(pY[t][:], wzT[:, t % 2, :], w_b1[:], start=False, stop=True).then_inc(y_ready, 1)

                            transpose_tile(pe, b, 1, pT, xt_ready, xt_done, wt_done)
                            for k in range(KC):
                                low_rank(0, k)
                            for t in range(QT):
                                for k in range(KC):
                                    base(t, k)
                                    if t + 1 < QT:
                                        low_rank(t + 1, k)
                                    if t == 0 and k < 2:
                                        transpose_tile(pe, b, 2 + k, pT, xt_ready, xt_done, wt_done)
                                    if t > 0 and k == 0:
                                        turn(t - 1)
                                    if t > 0 and k == 1:
                                        experts(t - 1)
                                    if t == QT - 1 and k == 2:
                                        turn(t)
                            experts(QT - 1)

                    @block.scalar
                    def _(act):
                        for s in (xt_done, wt_done, xhat_ready):
                            act.sem_inc(s, ONE)
                        with act.Fori(0, BATCH) as b:
                            for t in range(QT):
                                act.wait_ge(xt_ready, b * QT + t + 1)
                                if t == 0:
                                    act.wait_ge(y_ready, ONE + b * QT)
                                act.copy(xT[:, :, t * P:(t + 1) * P],
                                         pT[t % 2][:].rearrange("p (k q) -> p k q", k=KC)).then_inc(xt_done, 1)
                            for t in range(QT):
                                i = t % 2
                                act.wait_ge(lg_done, b * QT + t + 1)
                                act.activation(ex[:, i, :], lg[:, i, :], ACT.Exp, bias=nm[:, i:i + 1],
                                               accum_out=sm[:, i:i + 1]).then_inc(ex_done, 1)
                                if t == QT - 1:
                                    next_rows(act, b, 0, scaled, xt_ready, xhat_ready)
                                act.wait_ge(wt_ready, ONE + b * QT + t + 1)
                                act.wait_ge(y_ready, ONE + twice(b, t))
                                act.copy(wzT[:, i, :], pT[i][0:Z1, 0:P]).then_inc(wt_done, 1)
                                if t == QT - 1:
                                    next_rows(act, b, 2, scaled, xt_ready, xhat_ready)

                    @block.vector
                    def _(dve):
                        for s in (wz_done, x_done,):
                            dve.sem_inc(s, ONE)
                        with dve.Fori(0, BATCH) as b:
                            norm = LayerNorm(dve, x, ln_small, (b + 1) % BATCH, s_ln, b * LayerNorm.COUNTS)

                            def norm_step(t, i):
                                norm.scale_step(t * 5 + i, lambda: dve.wait_ge(xhat_ready, ONE + b * QT), scaled)

                            dve.wait_ge(x_done, ONE + b * QT)
                            for t in range(QT):
                                norm.statistics(t)

                            def gate(t):
                                i, n = t % 2, b * QT * 3 + t * 3
                                dve.wait_ge(z_ready, b * QT + t + 1)
                                dve.tensor_tensor(lg[:, i, :], pZ[i][:, Z1:Z1 + A1], gate_b[:], ALU.add).then_inc(s_gate, 1)
                                norm_step(t, 0)
                                dve.wait_ge(s_gate, n + 1)
                                dve.tensor_reduce(nm[:, i:i + 1], lg[:, i, :], AX.X, ALU.max, negate=True).then_inc(lg_done, 1)
                                norm_step(t, 1)
                                norm_step(t, 2)
                                dve.wait_ge(ex_done, b * QT + t + 1)
                                dve.reciprocal(rs[:, i:i + 1], sm[:, i:i + 1]).then_inc(s_gate, 1)
                                norm_step(t, 3)
                                dve.wait_ge(s_gate, n + 2)
                                dve.tensor_scalar(al[:, i, :], ex[:, i, :], rs[:, i:i + 1], 2.0, ALU.mult, ALU.mult).then_inc(s_gate, 1)
                                norm_step(t, 4)
                                dve.wait_ge(s_gate, n + 3)
                                dve.wait_ge(wt_ready, ONE + twice(b, t))
                                dve.tensor_tensor(wz[:, i, :].rearrange("p (a r) -> p a r", a=A1),
                                                  pZ[i][:, 0:Z1].rearrange("p (a r) -> p a r", a=A1),
                                                  al[:, i, :].unsqueeze(2).broadcast_to([P, A1, R1]),
                                                  ALU.mult).then_inc(wz_done, 1)

                            def residual(t):
                                dve.wait_ge(y_ready, ONE + b * QT + t + 1)
                                xt = x[:, b * QT + t, :]
                                dve.scalar_tensor_tensor(xt, pY[t][:], 0.5, xt, ALU.mult, ALU.add).then_inc(s_res, 1)
                                dve.wait_ge(s_res, b * QT + t + 1)
                                dve.tensor_tensor(xt, xt, half_b[:], ALU.add).then_inc(x_done, 1)

                            gate(0)
                            for t in range(1, QT):
                                gate(t)
                                residual(t - 1)
                            residual(QT - 1)

                    @block.sync
                    def _(sp):
                        if prefetch is not None:
                            prefetch(sp)
                        if last_stage:
                            out_rows = out.rearrange("b (t p) d -> p (b t) d", p=P)
                            with sp.Fori(0, TOKENS // P) as i:
                                sp.wait_ge(x_done, ONE + i + 1)
                                sp.dma_start(out_rows[:, bass.ds(i, 1), :], x[:, bass.ds(i, 1), :]).then_inc(stored, 16)
                            sp.wait_ge(stored, TOKENS // P * 16)

        def attention(tag, w_q, w_k, w_v, w_o, own_k, got_weights, n_weights, b_qk, b_v, b_o):
            GROUPS = [(0, (0, 1, 2, 3)), (1, (0, 1)), (1, (2, 3))] + [(qt, (j,)) for qt in (2, 3) for j in range(UH)]
            HALF = 5

            def groups(n, lo, hi):
                return [("A", n, g) for g in range(lo, hi)] if n < UNITS else []

            def projected(c):
                return [("Q", c)] + ([("K", c)] if own_k else [])

            if own_k:
                FIRST = [("Q", 0), ("K", 0)]
                HEAD = [("V", 0), ("V", 1), ("V", 2), ("V", 3), ("A", 0, 0, 3), ("P", 0), ("A", 0, 3, 6), ("P", 1),
                        ("A", 0, 6, 9), ("P", 2), ("N",), ("A", 0, 9, 11), ("O", 0), ("Q", 1), ("M", 0), ("O", 1),
                        ("O", 2), ("P", 3), ("O", 3), ("A", 1, 0, 3), ("K", 1), ("A", 1, 3, HALF)]
            else:
                FIRST = [("K", 0), ("Q", 0)]
                HEAD = [("Q", 1), ("V", 0), ("Q", 2), ("A", 0, 0, 3), ("P", 0), ("A", 0, 3, 5), ("P", 1), ("A", 0, 5, 7),
                        ("P", 2), ("A", 0, 7, 9), ("N",), ("P", 3), ("A", 0, 9, 11), ("O", 0), ("O", 1), ("M", 0),
                        ("O", 2), ("O", 3), ("A", 1, 0, HALF)]
            EARLY = 2 if own_k else 3
            items = [("T", t) for t in range(QT)] + FIRST
            for step in HEAD:
                items += groups(*step[1:]) if step[0] == "A" else [] if step[0] in "NOP" else [step]
            for n in range(UNITS):
                items += groups(n + 1, HALF, HALF + 2)
                if n % 2 == 0 and n // 2 + EARLY < CHUNKS:
                    items += projected(n // 2 + EARLY)
                if n + 1 < UNITS:
                    items += groups(n + 1, HALF + 2, len(GROUPS)) + [("M", n + 1)] + groups(n + 2, 0, HALF)
            at = {item: i for i, item in enumerate(items)}
            by_dve = [item for item in items if item[0] not in "TM"]
            dve_at = {item: i for i, item in enumerate(by_dve)}
            N, ND = len(items), len(by_dve)
            splits = [item for item in items if item[0] in "QK"]
            split_at = {item: i for i, item in enumerate(splits)}
            NS = len(splits)
            LOADS = 4 if own_k else 2
            PARTS = 4
            SPREADS = 2 if own_k else 1
            PIECES = [(0, (0, 1)), (0, (2, 3)), (1, (0, 1)), (1, (2, 3)), (2, (0, 1, 2, 3)), (3, (0, 1, 2, 3))]
            NP = len(PIECES)
            done_with = [2, 4, 5, 6]
            uses = [len(range(s, UNITS, STACKS)) for s in range(STACKS)]

            with ExitStack() as c:
                if own_k:
                    vv = sb(tag + "vv", [P, QT, HEADS, HD, 2], F32, c)
                    xT = sb(tag + "xT", [P, KC, SEQ], F32, c)
                else:
                    k_all = Ks[0][:, 0, :]
                    kv_first = sb(tag + "kv_first", [KV_COLS, 1, SEQ], F32R, c)
                    k_first, vT = kv_first[0:3 * HD], kv_first[:, 0, :].bitcast(F32)
                    xT_high = sb(tag + "xT_high", [P, KC, SEQ], F32R, c)
                    xT_low = sb(tag + "xT_low", [P, KC, SEQ], F32R, c)
                    oT_high = sb(tag + "oT_high", [P, CHUNKS, SEQ], F32R, c)
                    oT_low = sb(tag + "oT_low", [P, CHUNKS, SEQ], F32R, c)
                    vv = sb(tag + "vv", [P, QT, HD, 2], F32, c)
                parts = sb(tag + "parts", [P, PARTS, SEQ], F32R, c)
                if own_k:
                    spread_k = nc.dram_tensor(tag + "spread_k", (CHUNKS, 2 * HD, P // HD, SEQ), F32, kind="Internal").ap()
                probs = [sb(f"{tag}probs{i}", [P, UH, SEQ - i * P], F32, c) for i in range(2)]
                o_raw = sb(tag + "o_raw", [P, 2, SEQ], F32, c)
                OT = CHUNKS if own_k else 2
                oT = sb(tag + "oT", [P, OT, SEQ], F32, c)
                den = sb(tag + "den", [P, SEQ], F32, c)
                sums = sb(tag + "sums", [P, 2, SEQ // HD], F32, c)
                inv_dram = nc.dram_tensor(tag + "inv", (CHUNKS, P // HD, SEQ), F32, kind="Internal").ap()
                neg_max = sb(tag + "neg_max", [P, QT, UH], F32, c)
                nm_parts = sb(tag + "nm_parts", [P, QT, 2, UH], F32R, c)
                nm_rows = sb(tag + "nm_rows", [2 * UH, SEQ], F32R, c)
                bank = [ps(f"{tag}bank{i}", [P, 512], F32, c) for i in range(3)]
                pS = [ps(f"{tag}pS{i}", [P, 2, 512], F32, c) for i in range(2)]
                pO = ps(tag + "pO", [P, 512], F32, c)

                ready, xt_done, bank_read, hi_done = (sem(tag + n) for n in ("ready", "xt_done", "bank_read", "hi_done"))
                s_ready, exp_done, pv_done, o_done, ones_in, max_split, s_split, max_rows_out, w_ready, x_done = (
                    sem(tag + n) for n in ("s_ready", "exp_done", "pv_done", "o_done", "ones_in", "max_split", "s_split",
                                           "max_rows_out", "w_ready", "x_done"))
                spread_out = [sem(f"{tag}spread_out{i}") for i in range(2)]
                loaded = [sem(f"{tag}loaded{i}") for i in range(STACKS)]
                max_in = sem(tag + "max_in")
                packed = [sem(f"{tag}packed{i}") for i in range(2)]
                inverted, inv_out, inv_in, norm_done, s_res = (
                    sem(tag + n) for n in ("inverted", "inv_out", "inv_in", "norm_done", "s_res"))
                xhat_ready, s_ln, scaled, key_parts_in, xt_high, s_norm, v_in = (
                    sem(tag + n) for n in ("xhat", "s_ln", "scaled", "key_parts_in", "xt_high", "s_norm", "v_in"))

                def psum_of(item):
                    return bank[at[item] % 3]

                def item_ready(eng, b, item):
                    eng.wait_ge(ready, b * N + at[item] + 1)

                def item_read(eng, b, item):
                    if item[0] == "T":
                        eng.wait_ge(xt_done, b * QT + item[1] + 1)
                    elif item[0] == "M":
                        eng.wait_ge(max_rows_out, b * UNITS + item[1] + 1)
                    else:
                        eng.wait_ge(bank_read, ONE + b * ND + dve_at[item] + 1)

                def bank_free(pe, b, item):
                    if at[item] >= 3:
                        item_read(pe, b, items[at[item] - 3])
                    elif at[item] == 0:
                        pe.wait_ge(bank_read, ONE + b * ND)

                def stack_free(eng, b, n):
                    eng.wait_ge(s_ready, ONE + b * UNITS * NP + max(n - STACKS + 1, 0) * NP)

                def stack_loaded(eng, b, n):
                    eng.wait_ge(loaded[n % STACKS], (b * uses[n % STACKS] + n // STACKS + 1) * LOADS * 16)

                def piece_of(i):
                    kt, heads = PIECES[i]
                    buf = pS[i % 2]
                    if kt < 2:
                        return buf[:, :, 0:SEQ - kt * P]
                    if kt == 2:
                        return buf[:].rearrange("p i (j w) -> p (i j) w", w=2 * P)
                    return buf[:, 0, :].rearrange("p (j w) -> p j w", w=P)

                def keys(n, j, rows, cols):
                    return Ks[n % STACKS][0:rows, j, cols] if own_k else k_all[0:rows, cols]

                def parts_stored(eng, b, c):
                    eng.wait_ge(spread_out[c % 2], DMA_ONE + (b * (CHUNKS // 2) + c // 2 + 1) * SPREADS * 16)

                def first_part(kind, c):
                    return 2 * (kind == "K") if own_k else 2 * (c % 2)

                def part(kind, c, i):
                    return parts[:, first_part(kind, c) + i, :]

                with nc.Block() as block:
                    @block.tensor
                    def _(pe):
                        if own_k:
                            pe.wait_ge(got_weights, n_weights * 16)
                        else:
                            pe.wait_ge(weights_split, 2 * 3)
                        for s in (s_ready, pv_done,):
                            pe.sem_inc(s, ONE)

                        def batch(b):
                            def project(kind, c, weights, cols):
                                item = (kind, c)
                                bank_free(pe, b, item)
                                m = cols.stop - cols.start
                                for k in range(KC):
                                    if own_k:
                                        factors = ((weights, xT),)
                                    else:
                                        high, low = weights
                                        factors = ((high, xT_high), (high, xT_low), (low, xT_high))
                                    for i, (a, b_) in enumerate(factors):
                                        last = pe.matmul(psum_of(item)[0:m, :], a[:, k, cols], b_[:, k, :], start=(k + i == 0),
                                                         stop=(k == KC - 1 and i == len(factors) - 1))
                                last.then_inc(ready, 1)

                            def project_chunk(c):
                                for item in projected(c):
                                    project_item(*item)

                            def max_scores(n, lo, hi):
                                for g in range(lo, hi):
                                    if g == 0:
                                        if not own_k and n == 0:
                                            pe.wait_ge(key_parts_in, (b + 1) * 16)
                                        stack_loaded(pe, b, n)
                                    bank_free(pe, b, ("A", n, g))
                                    out_bank = psum_of(("A", n, g))
                                    qt, heads = GROUPS[g]
                                    width = (qt + 1) * P
                                    view = out_bank[:, 0:len(heads) * width].rearrange("p (h k) -> p h k", k=width)
                                    for i, j in enumerate(heads):
                                        pe.matmul(view[:, i, :], Qs[n % STACKS][0:MAX0, j, qt * P:(qt + 1) * P],
                                                  keys(n, j, MAX0, slice(0, width)), start=(i == 0), stop=False)
                                    pe.matmul(view[:, :, width - P:width], identb[:],
                                              causal[:].unsqueeze(1).broadcast_to([P, len(heads), P]),
                                              start=False, stop=True).then_inc(ready, 1)

                            def max_rows(n):
                                pe.wait_ge(max_split, ONE + b * UNITS + n + 1)
                                bank_free(pe, b, ("M", n))
                                for qt in range(QT):
                                    last = pe.transpose(psum_of(("M", n))[0:2 * UH, qt * P:(qt + 1) * P],
                                                        nm_parts[:, qt].rearrange("p i h -> p (i h)").bitcast(F32), ident[:])
                                last.then_inc(ready, 1)

                            def scores(n, i):
                                kt, heads = PIECES[i]
                                if i == 0:
                                    pe.wait_ge(max_in, DMA_ONE + (b * UNITS + n + 1) * 16)
                                    if n == 0:
                                        pe.wait_ge(x_done, ONE + b * QT)
                                pe.wait_ge(exp_done, ONE + b * UNITS * NP + max(n * NP + i - 1, 0))
                                piece = piece_of(i)
                                each = (1, 1, 2, 4)[kt]
                                step = 1 if own_k else each
                                for at in range(0, len(heads), step):
                                    j = heads[at]
                                    pe.matmul(piece[:, at:at + step, :], keys(n, j, P, slice(kt * P, (kt + 1) * P)),
                                              Qs[n % STACKS][:, j:j + step, kt * P:SEQ], start=(at % each == 0), stop=False)
                                for at in range(0, len(heads), each):
                                    last = pe.matmul(piece[:, at:at + each, 0:P], identb[:],
                                                     causal_t[:].unsqueeze(1).broadcast_to([P, each, P]),
                                                     start=False, stop=True)
                                last.then_inc(s_ready, 1)

                            def values(n, kt):
                                pe.wait_ge(exp_done, ONE + b * UNITS * NP + n * NP + done_with[kt])
                                if kt == 0:
                                    pe.wait_ge(o_done, ONE + b * UNITS + n)
                                for j in range(UH):
                                    v_tile = (vv[:, kt, n * UH + j] if own_k else vv[:, kt]).rearrange("p d s -> p (d s)")
                                    last = pe.matmul(pO[32 * j:32 * (j + 1), kt * P:SEQ], v_tile,
                                                     probs[kt % 2][:, j, 0:SEQ - kt * P],
                                                     start=(kt == 0), stop=(kt == QT - 1))
                                last.then_inc(pv_done, 1)

                            def transposes():
                                pe.wait_ge(xhat_ready, ONE + b * QT)
                                for t in range(QT):
                                    bank_free(pe, b, ("T", t))
                                    for k in range(KC):
                                        last = pe.transpose(psum_of(("T", t))[:, k * P:(k + 1) * P],
                                                            xhat[:, t, k * P:(k + 1) * P], ident[:])
                                    last.then_inc(ready, 1)

                            def project_item(kind, c):
                                if kind == "V" and not own_k:
                                    pe.wait_ge(v_in, b + 1)
                                    pe.sem_inc(passed, 1)
                                    bank_free(pe, b, ("V", 0))
                                    pe.sem_inc(passed, 1)
                                    for t in range(QT):
                                        last = pe.transpose(psum_of(("V", 0))[:, t * HD:(t + 1) * HD],
                                                            vT[V0:KV_COLS, t * P:(t + 1) * P], ident[V0:KV_COLS, V0:KV_COLS])
                                    last.then_inc(ready, 1)
                                elif kind == "V":
                                    bank_free(pe, b, ("V", c))
                                    for k in range(KC):
                                        last = pe.matmul(psum_of(("V", c))[:], xT[:, k, c * P:(c + 1) * P], w_v[:, k, :],
                                                         start=(k == 0), stop=(k == KC - 1))
                                    last.then_inc(ready, 1)
                                elif kind == "Q":
                                    project("Q", c, w_q, slice(c * P, (c + 1) * P))
                                elif own_k:
                                    project("K", c, w_k, slice(c * P, (c + 1) * P))
                                else:
                                    project("K", 0, w_k, slice(0, KV_COLS))

                            def first(i):
                                if i == 0:
                                    item_read(pe, b, ("T", QT - 1))
                                project_item(*FIRST[i])

                            def head(before):
                                for step in HEAD:
                                    if step[0] == "A":
                                        max_scores(*step[1:])
                                    elif step[0] == "M":
                                        max_rows(0)
                                    elif step[0] in "QKV":
                                        project_item(*step)
                                    elif before is not None and step[0] == "P":
                                        before.output(step[1], range(CHUNKS - 1))
                                    elif before is not None and step[0] == "O":
                                        before.output(step[1], range(CHUNKS - 1, CHUNKS))

                            def units(following):
                                for n in range(UNITS):
                                    ahead, after = n + 1 < UNITS, n + 2 < UNITS
                                    early = following is not None and not ahead
                                    scores(n, 0)
                                    scores(n, 1)
                                    if ahead:
                                        max_scores(n + 1, HALF, HALF + 2)
                                    if early:
                                        following.transposes()
                                    if n % 2 == 0 and n // 2 + EARLY < CHUNKS:
                                        project_chunk(n // 2 + EARLY)
                                    scores(n, 2)
                                    if ahead:
                                        max_scores(n + 1, HALF + 2, HALF + 4)
                                    scores(n, 3)
                                    if early:
                                        following.first(0)
                                    values(n, 0)
                                    if ahead:
                                        max_scores(n + 1, HALF + 4, len(GROUPS))
                                    scores(n, 4)
                                    values(n, 1)
                                    if ahead:
                                        max_rows(n + 1)
                                    if early:
                                        following.first(1)
                                    scores(n, 5)
                                    if after:
                                        max_scores(n + 2, 0, 2)
                                    values(n, 2)
                                    if after:
                                        max_scores(n + 2, 2, 4)
                                    values(n, 3)
                                    if after:
                                        max_scores(n + 2, 4, HALF)

                            def output(t, chunks):
                                if t == 0:
                                    pe.wait_ge(exp_done, ONE + (b + 1) * UNITS * NP)
                                    pe.wait_ge(norm_done, ONE + b * CHUNKS + chunks[-1] + 1)
                                for k in chunks:
                                    if own_k:
                                        factors = ((oT, w_o),)
                                    else:
                                        high, low = w_o
                                        factors = ((oT_high, high), (oT_high, low), (oT_low, high))
                                    for i, (a, b_) in enumerate(factors):
                                        last = pe.matmul(pS[t // 2][:, t % 2, :], a[:, k, t * P:(t + 1) * P], b_[:, k, :],
                                                         start=(k + i == 0), stop=(k == CHUNKS - 1 and i == len(factors) - 1))
                                if chunks[-1] == CHUNKS - 1:
                                    last.then_inc(w_ready, 1)

                            return Steps(transposes=transposes, first=first, head=head, units=units, output=output)

                        start = batch(0)
                        start.transposes()
                        start.first(0)
                        start.first(1)
                        start.head(None)
                        with pe.Fori(0, BATCH - 1) as b:
                            this, following = batch(b), batch(b + 1)
                            this.units(following)
                            following.head(this)
                        end = batch(BATCH - 1)
                        end.units(None)
                        for chunks in (range(CHUNKS - 1), range(CHUNKS - 1, CHUNKS)):
                            for t in range(QT):
                                end.output(t, chunks)

                    @block.scalar
                    def _(act):
                        for s in (exp_done, o_done, xhat_ready):
                            act.sem_inc(s, ONE)

                        def batch(b):
                            def high(kind, c):
                                item_ready(act, b, (kind, c))
                                if not own_k and kind == "K":
                                    act.copy(vT[V0:KV_COLS, :], psum_of((kind, c))[V0:KV_COLS, :]).then_inc(v_in, 1)
                                    act.copy(k_first[:, 0, :], psum_of((kind, c))[0:3 * HD, :]).then_inc(hi_done, 1)
                                    return
                                dst = part(kind, c, 0)
                                parts_stored(act, b, c - (1 if own_k else 2))
                                if b_qk is None:
                                    act.copy(dst, psum_of((kind, c))[:]).then_inc(hi_done, 1)
                                else:
                                    col = c + (CHUNKS if kind == "K" else 0)
                                    act.activation(dst, psum_of((kind, c))[:], ACT.Identity,
                                                   bias=b_qk[:, col:col + 1]).then_inc(hi_done, 1)

                            def high_chunk(c):
                                high("Q", c)
                                if own_k:
                                    high("K", c)

                            def copy_max(n):
                                act.wait_ge(max_in, DMA_ONE + (b * UNITS + n) * 16)
                                item_ready(act, b, ("M", n))
                                act.copy(nm_rows[:], psum_of(("M", n))[0:2 * UH, :]).then_inc(max_rows_out, 1)

                            def exps(n, i):
                                kt, heads = PIECES[i]
                                act.wait_ge(pv_done, ONE + b * UNITS * QT + max(n * QT + kt - 1, 0))
                                act.wait_ge(s_ready, ONE + b * UNITS * NP + n * NP + i + 1)
                                act.activation(probs[kt % 2][:, heads[0]:heads[-1] + 1, 0:SEQ - kt * P], piece_of(i),
                                               ACT.Exp, scale=SCORE_SCALE).then_inc(exp_done, 1)

                            def copy_xt():
                                for t in range(QT):
                                    item_ready(act, b, ("T", t))
                                    act.copy((xT if own_k else xT_high)[:, :, t * P:(t + 1) * P],
                                             psum_of(("T", t))[:].rearrange("p (k q) -> p k q", k=KC)
                                             ).then_inc(xt_done if own_k else xt_high, 1)

                            def first(i):
                                high(*FIRST[i])

                            def head():
                                for step in HEAD:
                                    if step[0] in "QK":
                                        high(*step)
                                    elif step[0] == "M":
                                        copy_max(0)

                            def units(following):
                                for n in range(UNITS):
                                    early = following is not None and n + 1 == UNITS
                                    exps(n, 0)
                                    exps(n, 1)
                                    if early:
                                        following.copy_xt()
                                    if n % 2 == 0 and n // 2 + EARLY < CHUNKS:
                                        high_chunk(n // 2 + EARLY)
                                    exps(n, 2)
                                    exps(n, 3)
                                    if early:
                                        following.first(0)
                                    exps(n, 4)
                                    if n + 1 < UNITS:
                                        copy_max(n + 1)
                                    if early:
                                        following.first(1)
                                    exps(n, 5)
                                    if n >= UNITS - 3 and n < UNITS - 1:
                                        if n == UNITS - 3:
                                            act.wait_ge(scaled, b + 1)
                                            item_ready(act, b, ("T", QT - 1))
                                        for t in range(2 * (n - UNITS + 3), 2 * (n - UNITS + 4)):
                                            normed_row(act, x, xhat, ln_small, (b + 1) % BATCH, t, xhat_ready)
                                    act.wait_ge(packed[n % 2], DMA_ONE + (b * CHUNKS + n // 2) * 32)
                                    act.wait_ge(pv_done, ONE + b * UNITS * QT + (n + 1) * QT)
                                    act.copy(o_raw[:, n % 2, :], pO[:]).then_inc(o_done, 1)

                            return Steps(copy_xt=copy_xt, first=first, head=head, units=units)

                        start = batch(0)
                        start.copy_xt()
                        start.first(0)
                        start.first(1)
                        start.head()
                        with act.Fori(0, BATCH - 1) as b:
                            this, following = batch(b), batch(b + 1)
                            this.units(following)
                            following.head()
                        batch(BATCH - 1).units(None)

                    @block.gpsimd
                    def _(pool):
                        for t in range(QT):
                            pool.memset(vv[:, t, :, :, 1] if own_k else vv[:, t, :, 1], 1.0).then_inc(ones_in, 1)

                    @block.vector
                    def _(dve):
                        dve.wait_ge(ones_in, QT)
                        for s in (bank_read, norm_done, max_split, x_done, inverted,):
                            dve.sem_inc(s, ONE)

                        def batch(b):
                            def low(kind, c):
                                dve.wait_ge(hi_done, b * NS + split_at[(kind, c)] + 1)
                                src = psum_of((kind, c))
                                if not own_k and kind == "K":
                                    rows = k_first[2 * HD:3 * HD, 0, :]
                                    dve.tensor_tensor(rows, src[2 * HD:3 * HD, :], rows.bitcast(F32), ALU.subtract).then_inc(bank_read, 1)
                                    return
                                hi, lo = part(kind, c, 0), part(kind, c, 1)
                                if b_qk is None:
                                    dve.tensor_tensor(lo, src[:], hi.bitcast(F32),
                                                      ALU.subtract).then_inc(bank_read, 1)
                                else:
                                    col = c + (CHUNKS if kind == "K" else 0)
                                    dve.scalar_tensor_tensor(lo, src[:], b_qk[:, col:col + 1],
                                                             hi.bitcast(F32), ALU.add, ALU.subtract).then_inc(bank_read, 1)

                            def low_chunk(c):
                                low("Q", c)
                                if own_k:
                                    low("K", c)

                            def maxima(n, lo, hi):
                                for g in range(lo, hi):
                                    item_ready(dve, b, ("A", n, g))
                                    qt, heads = GROUPS[g]
                                    width, m = (qt + 1) * P, len(heads)
                                    dve.tensor_reduce(neg_max[:, qt, heads[0]:heads[0] + m],
                                                      psum_of(("A", n, g))[:, 0:m * width].rearrange("p (h k) -> p h k", h=m),
                                                      AX.X, ALU.max, negate=True).then_inc(bank_read, 1)

                            def split_max(n):
                                item_read(dve, b, ("A", n, len(GROUPS) - 1))
                                hi, lo = nm_parts[:, :, 0, :], nm_parts[:, :, 1, :]
                                dve.tensor_copy(hi, neg_max[:]).then_inc(s_split, 1)
                                dve.wait_ge(s_split, b * UNITS + n + 1)
                                dve.tensor_tensor(lo, neg_max[:], hi.bitcast(F32), ALU.subtract).then_inc(max_split, 1)

                            def invert_sums(c):
                                for s in range(2):
                                    dve.wait_ge(packed[s], DMA_ONE + (b * CHUNKS + c + 1) * 32)
                                dve.reciprocal(sums[:, c % 2, :], sums[:, c % 2, :]).then_inc(inverted, 1)

                            def normalise(c):
                                dve.wait_ge(inv_in, (b * CHUNKS + c + 1) * 16)
                                product = dve.tensor_tensor(oT[:, c % OT, :], oT[:, c % OT, :], den[:], ALU.mult)
                                if own_k:
                                    product.then_inc(norm_done, 1)
                                else:
                                    product.then_inc(s_norm, 1)
                                    dve.wait_ge(s_norm, (b * CHUNKS + c) * 2 + 1)
                                    dve.tensor_copy(oT_high[:, c, :], oT[:, c % OT, :]).then_inc(s_norm, 1)
                                    dve.wait_ge(s_norm, (b * CHUNKS + c) * 2 + 2)
                                    dve.tensor_tensor(oT_low[:, c, :], oT[:, c % OT, :], oT_high[:, c, :].bitcast(F32),
                                                      ALU.subtract).then_inc(norm_done, 1)

                            def low_xt():
                                for t in range(QT):
                                    dve.wait_ge(xt_high, b * QT + t + 1)
                                    tile = slice(t * P, (t + 1) * P)
                                    dve.tensor_tensor(xT_low[:, :, tile], psum_of(("T", t))[:].rearrange("p (k q) -> p k q", k=KC),
                                                      xT_high[:, :, tile].bitcast(F32), ALU.subtract).then_inc(xt_done, 1)

                            def take_item(kind, c):
                                if kind != "V":
                                    low(kind, c)
                                elif own_k:
                                    item_ready(dve, b, ("V", c))
                                    dve.tensor_tensor(vv[:, c, :, :, 0], psum_of(("V", c))[:].rearrange("p (h d) -> p h d", h=HEADS),
                                                      b_v[:].rearrange("p (h d) -> p h d", h=HEADS), ALU.add).then_inc(bank_read, 1)
                                else:
                                    item_ready(dve, b, ("V", 0))
                                    dve.tensor_copy(vv[:, :, :, 0], psum_of(("V", 0))[:, 0:QT * HD].rearrange("p (t d) -> p t d", t=QT)
                                                    ).then_inc(bank_read, 1)

                            def first(i):
                                if i == 0 and not own_k:
                                    low_xt()
                                low(*FIRST[i])

                            def head(before):
                                for step in HEAD:
                                    if step == HEAD[1] and before is not None:
                                        before.invert_sums(CHUNKS - 1)
                                    if step[0] == "N" and before is not None:
                                        before.normalise(CHUNKS - 1)
                                    if step[0] == "A":
                                        maxima(*step[1:])
                                    elif step[0] == "O":
                                        if before is not None:
                                            before.residual(step[1])
                                    elif step[0] in "QKV":
                                        take_item(*step)
                                    if step[0:2] == ("A", 0) and step[3] == len(GROUPS):
                                        split_max(0)

                            def units(following):
                                dve.wait_ge(x_done, ONE + b * QT)
                                norm = LayerNorm(dve, x, ln_small, (b + 1) % BATCH, s_ln, b * LayerNorm.COUNTS)
                                for n in range(UNITS):
                                    if n + 1 < UNITS:
                                        maxima(n + 1, HALF, HALF + 2)
                                    if n % 2 == 0 and n // 2 + EARLY < CHUNKS:
                                        low_chunk(n // 2 + EARLY)
                                    if n + 1 < UNITS:
                                        maxima(n + 1, HALF + 2, len(GROUPS))
                                        split_max(n + 1)
                                    if n % 2 == 0 and n >= 2:
                                        invert_sums(n // 2 - 1)
                                    if n + 1 == UNITS and following is not None:
                                        following.first(0)
                                    if n % 2 == 1 and n >= 3:
                                        normalise((n - 3) // 2)
                                    if n < QT // 2:
                                        norm.statistics(2 * n)
                                        norm.statistics(2 * n + 1)
                                    elif n < QT // 2 + 3:
                                        part = (LayerNorm.STEPS + 2) // 3
                                        for i in range((n - QT // 2) * part, min((n - QT // 2 + 1) * part, LayerNorm.STEPS)):
                                            norm.scale_step(i, lambda: dve.wait_ge(xhat_ready, ONE + b * QT), scaled)
                                    if b_o is not None and 2 <= n < 2 + QT:
                                        xt = x[:, b * QT + n - 2, :]
                                        dve.tensor_tensor(xt, xt, b_o[:], ALU.add).then_inc(s_res, 1)
                                    if n + 2 < UNITS:
                                        maxima(n + 2, 0, HALF)
                                if following is not None:
                                    following.first(1)
                                else:
                                    invert_sums(CHUNKS - 1)

                            def residual(t):
                                dve.wait_ge(w_ready, b * QT + t + 1)
                                if b_o is not None:
                                    dve.wait_ge(s_res, b * QT + t + 1)
                                xt = x[:, b * QT + t, :]
                                dve.tensor_tensor(xt, pS[t // 2][:, t % 2, :], xt, ALU.add).then_inc(x_done, 1)

                            return Steps(first=first, head=head, units=units, invert_sums=invert_sums, normalise=normalise, residual=residual)

                        start = batch(0)
                        start.first(0)
                        start.first(1)
                        start.head(None)
                        with dve.Fori(0, BATCH - 1) as b:
                            this, following = batch(b), batch(b + 1)
                            this.units(following)
                            following.head(this)
                        end = batch(BATCH - 1)
                        end.units(None)
                        end.normalise(CHUNKS - 1)
                        for t in range(QT):
                            end.residual(t)

                    @block.sync
                    def _(sp):
                        for s in (*spread_out, max_in, packed[0], packed[1], inv_out,):
                            sp.sem_inc(s, DMA_ONE)

                        def batch(b):
                            def store_parts(c):
                                item_read(sp, b, ("K", c) if own_k else ("Q", c))
                                for i, dram in enumerate((spread_q[c, 2:, :, :], spread_k[c]) if own_k else (spread_q[c, 2:, :, :],)):
                                    at = first_part("QK"[i], c)
                                    sp.dma_start(dram.rearrange("(i d) h t -> (d h) i t", i=2),
                                                 parts[:, at:at + 2, :].bitcast(F32)).then_inc(spread_out[c % 2], 16)

                            def load_stack(n):
                                c, first = n // 2, (n % 2) * UH
                                parts_stored(sp, b, c)
                                sp.sem_inc(passed, 1)
                                stack_free(sp, b, n)

                                def load(stack, dram, at, lo, hi):
                                    sp.dma_start(stack[n % STACKS][at:at + hi - lo, :, :].bitcast(F32),
                                                 dram[c, lo:hi, first:first + UH, :]).then_inc(loaded[n % STACKS], 16)

                                load(Qs, spread_q, 0, 0, 2 + 2 * HD)
                                load(Qs, spread_q, 2 + 2 * HD, 2, 2 + HD)
                                if own_k:
                                    load(Ks, spread_k, PART0, 0, HD)
                                    load(Ks, spread_k, PART0 + HD, 0, 2 * HD)

                            def load_max(n):
                                item_read(sp, b, ("M", n))
                                sp.dma_start(Qs[n % STACKS][MAX0:MAX0 + 2, :, :].bitcast(F32),
                                             nm_rows[:].bitcast(F32)).then_inc(max_in, 16)

                            def pack(n):
                                c, r = n // 2, (n % 2) * UH * HD
                                if not own_k and n % 2 == 0:
                                    sp.wait_ge(norm_done, ONE + b * CHUNKS + max(c - 1, 0))
                                    sp.sem_inc(passed, 1)
                                sp.wait_ge(o_done, ONE + b * UNITS + n + 1)
                                sp.dma_start(oT[r:r + UH * HD, c % OT, :], o_raw[0:P:2, n % 2, :]).then_inc(packed[n % 2], 16)
                                if n % 2 == 0:
                                    sp.wait_ge(inv_out, DMA_ONE + (b * CHUNKS + max(c - 1, 0)) * 16)
                                sp.dma_start(sums[r:r + UH * HD, c % 2, :], o_raw[1:P:2 * HD, n % 2, :]).then_inc(packed[n % 2], 16)

                            def spread_sums(c):
                                sp.wait_ge(inverted, ONE + b * CHUNKS + c + 1)
                                sp.dma_start(inv_dram[c].rearrange("h (d q) -> (h d) q", d=HD), sums[:, c % 2, :]).then_inc(inv_out, 16)
                                sp.wait_ge(inv_out, DMA_ONE + (b * CHUNKS + c + 1) * 16)
                                sp.sem_inc(passed, 1)
                                sp.wait_ge(norm_done, ONE + b * CHUNKS + c)
                                sp.dma_start(den[:], inv_dram[c].unsqueeze(1).broadcast_to([P // HD, HD, SEQ])).then_inc(inv_in, 16)

                            def first():
                                if not own_k:
                                    item_read(sp, b, ("K", 0))
                                    sp.wait_ge(s_ready, ONE + b * UNITS * NP)
                                    sp.dma_start(k_all[PART0:PART0 + 3 * HD, :].bitcast(F32),
                                                 k_first[:, 0, :].bitcast(F32)).then_inc(key_parts_in, 16)
                                store_parts(0)

                            def head(before):
                                load_stack(0)
                                if before is not None:
                                    before.spread_sums(CHUNKS - 1)
                                load_stack(1)
                                for step in HEAD:
                                    if step[0] == ("K" if own_k else "Q"):
                                        store_parts(step[1])
                                        if step[1] == 1:
                                            load_stack(2)
                                    elif step[0] == "M":
                                        load_max(0)

                            def units(following):
                                for n in range(UNITS):
                                    if n % 2 == 1 and n >= 3:
                                        spread_sums((n - 3) // 2)
                                    if n % 2 == 0 and n // 2 + EARLY < CHUNKS:
                                        store_parts(n // 2 + EARLY)
                                    if n + 1 < UNITS:
                                        load_max(n + 1)
                                    if n + STACKS < UNITS:
                                        load_stack(n + STACKS)
                                    if following is not None and n + 1 == UNITS:
                                        following.first()
                                    pack(n)

                            return Steps(first=first, head=head, units=units, spread_sums=spread_sums)

                        start = batch(0)
                        start.first()
                        start.head(None)
                        with sp.Fori(0, BATCH - 1) as b:
                            this, following = batch(b), batch(b + 1)
                            this.units(following)
                            following.head(this)
                        end = batch(BATCH - 1)
                        end.units(None)
                        end.spread_sums(CHUNKS - 1)

        ffn0("a_", True)
        loaded0.close()
        attention("m_", split0[0], split0[1], None, split0[2], False, None, 0, None, None, None)
        layer0a.close()

        w_base = sb("w_base", [P, KC, D])

        def load_base(sp):
            sp.dma_start(w_base[:], w["base"].rearrange("(c p) m -> p c m", p=P)).then_inc(got_base1, 16)

        ffn0("b_", False, load_base)

        layer1 = ExitStack()
        w_qk1 = sb("w_qk1", [P, KC, 2 * D], F32, layer1)
        w_v1 = sb("w_v1", [P, KC, D], F32, layer1)
        w_o1 = sb("w_o1", [P, KC, D], F32, layer1)
        b_v1 = sb("b_v1", [P, D], F32, layer1)
        b_o1 = sb("b_o1", [P, D], F32, layer1)
        b_qk1 = sb("b_qk1", [P, 2 * CHUNKS], F32, layer1)

        def load_layer1(sp):
            for dst, src in ((w_qk1, "wqk1"), (w_v1, "wv1"), (w_o1, "wo1")):
                sp.dma_start(dst[:], w[src].rearrange("(c p) m -> p c m", p=P)).then_inc(got_att1, 16)
            sp.dma_start(b_v1[:], w["bv1"].partition_broadcast(P)).then_inc(got_att1, 16)
            sp.dma_start(b_o1[:], w["bo1"].partition_broadcast(P)).then_inc(got_att1, 16)
            sp.dma_start(b_qk1[:], w["bqk1"]).then_inc(got_att1, 16)

        ffn1("c_", True, False, load_layer1)
        attention("h_", w_qk1[:, :, 0:D], w_qk1[:, :, D:2 * D], w_v1, w_o1, True, got_att1, 6, b_qk1, b_v1, b_o1)
        layer1.close()
        ffn1("d_", False, True, None)


def kernel(**inputs):
    import numpy as _np
    import concourse.bacc as _bacc
    from concourse import mybir as _mybir
    from concourse.bass_utils import run_bass_kernel_spmd as _run

    g = {k: _np.asarray(v) for k, v in inputs.items()}

    def by_dim(m):
        return m.reshape(*m.shape[:-1], CHUNKS, P // HD, HD).swapaxes(-1, -2).reshape(m.shape)

    kv = g["L0_attn_Wkv"]
    wqkv = g["L1_attn_w_qkv"].T
    slopes = (4.0 * 2.0 ** (-0.25 * _np.arange(1, HEADS + 1))).astype(_np.float32)
    hi = (slopes.view(_np.uint32) & _np.uint32(0xFFFFF000)).view(_np.float32)
    pos = _np.arange(SEQ, dtype=_np.float32)
    laid = {
        "x": g["L0_attn_hidden_states"],
        "ar0": _np.concatenate([g["L0_ffn_A"].reshape(E0 * R0, D).T, g["L0_ffn_route_w"].T], axis=1),
        "b0": g["L0_ffn_Bw"].transpose(0, 2, 1).reshape(E0 * R0, D),
        "wq0": by_dim(g["L0_attn_Wq"]),
        "wkv0": _np.concatenate([kv[:, :HD]] * 3 + [_np.zeros_like(kv[:, :HD]), kv[:, HD:]], axis=1),
        "wo0": g["L0_attn_Wo"],
        "wqk1": _np.concatenate([by_dim(wqkv[:, :D]), by_dim(wqkv[:, D:2 * D])], axis=1),
        "wv1": wqkv[:, 2 * D:],
        "wo1": g["L1_attn_w_out"].T,
        "bqk1": _np.concatenate([by_dim(g["L1_attn_b_qkv"][:D]), by_dim(g["L1_attn_b_qkv"][D:2 * D])]).reshape(2 * CHUNKS, P).T,
        "bv1": g["L1_attn_b_qkv"][2 * D:],
        "bo1": g["L1_attn_b_out"],
        "base": g["L1_ffn_W_base"].T,
        "b_base": g["L1_ffn_b_base"],
        "lora_a": g["L1_ffn_lora_A"].reshape(E1 * R1, D),
        "lora_b": g["L1_ffn_lora_B"].transpose(0, 2, 1).reshape(E1 * R1, D),
        "router_w": g["L1_ffn_router_W"],
        "router_b": g["L1_ffn_router_b"],
        "prior": g["L1_ffn_domain_prior"],
        "active": g["L1_ffn_active"],
        "slopes": _np.ascontiguousarray(_np.broadcast_to(_np.stack([hi, slopes - hi]).reshape(2, CHUNKS, P // HD, 1).swapaxes(0, 1), (CHUNKS, 2, P // HD, SEQ))),
        "key_rows": _np.stack([pos, pos, pos * 0 + 1, pos * 0 + 1]),
    }
    nc = _bacc.Bacc("TRN2", target_bir_lowering=False, num_devices=1)
    arrays, aps = {}, {}
    for name, a in laid.items():
        a = _np.ascontiguousarray(a)
        arrays[f"in_{name}"] = a
        aps[name] = nc.dram_tensor(f"in_{name}", a.shape, _mybir.dt.from_np(a.dtype), kind="ExternalInput").ap()
    out = nc.dram_tensor("out_x", (BATCH, SEQ, D), F32, kind="ExternalOutput").ap()
    macaron(nc, aps.pop("x"), aps, out)
    r = _run(nc, [arrays], core_ids=[0])
    return r.results[0]["out_x"]
```
